# Optimizing a Trainium2 kernel written in Bass

```python
import numpy as np
import jax
import jax.numpy as jnp

def _softmax(x, axis=-1):
    return jax.nn.softmax(x, axis=axis)

def _gelu(x):
    return jax.nn.gelu(x, approximate=True)

def _silu(x):
    return jax.nn.silu(x)

def _sigmoid(x):
    return jax.nn.sigmoid(x)

def _layernorm(x, axis=-1, eps=1e-05):
    m = jnp.mean(x, axis=axis, keepdims=True)
    v = jnp.var(x, axis=axis, keepdims=True)
    return (x - m) / jnp.sqrt(v + eps)

def _scatter_add(tgt, idx, src, axis=0):
    return tgt.at[idx].add(src)

def _segment_sum(src, seg, n):
    return jax.ops.segment_sum(src, seg, n)
kernel_name = 'mk_gps_d1_gnn_r8_e4079a'

def setup_inputs(seed: int=0):
    np.random.seed(seed)
    _w = jnp.asarray

    def _rec_inputs():
        import jax
        import jax.numpy as jnp
        _gk = jax.random.key(seed)
        x = -0.0003713 + 1 * jax.random.normal(jax.random.fold_in(_gk, 1), (6250, 256), jnp.float32)
        src = jax.random.randint(jax.random.fold_in(_gk, 2), (200000,), 0, 6250, jnp.int32)
        dst = jax.random.randint(jax.random.fold_in(_gk, 3), (200000,), 0, 6250, jnp.int32)
        _o = jnp.argsort(dst, stable=True)
        src = src[_o]
        dst = dst[_o]
        return (x, src, dst)
    x, src, dst = _rec_inputs()

    def _L0_gnn_setup():
        import jax, jax.numpy as jnp
        import numpy as np
        N_NODES = 6250
        EPS = 1e-12
        key = jax.random.key(seed)
        k1, k2, k3 = jax.random.split(key, 3)
        d_in, d_out, n_edges = (256, 256, 100000)
        input_matrix = jax.random.normal(k1, (N_NODES, d_in), dtype=jnp.float32)
        adjacency_coo_matrix = jax.random.randint(k2, (2, n_edges), 0, N_NODES, dtype=jnp.int64)
        W = jax.random.normal(k3, (2 * d_in, d_out), dtype=jnp.float32) * (1.0 / np.sqrt(2 * d_in))
        b = jnp.zeros((d_out,), dtype=jnp.float32)
        return {'input_matrix': input_matrix, 'adjacency_coo_matrix': adjacency_coo_matrix, 'W': W, 'b': b}
    _L0_gnn_all = _L0_gnn_setup()
    _L0_gnn_in = {k: v for k, v in _L0_gnn_all.items() if k in ('W', 'b')}
    del _L0_gnn_all

    def _L0_mix_setup():
        import jax, jax.numpy as jnp
        import numpy as np
        HEADS = 8
        DIM_HEAD = 32
        SCALE = DIM_HEAD ** (-0.5)
        EPS = 1e-05

        def _layernorm_gamma(x, gamma):
            mu = jnp.mean(x, axis=-1, keepdims=True)
            var = jnp.var(x, axis=-1, keepdims=True)
            return (x - mu) * jax.lax.rsqrt(var + EPS) * gamma
        key = jax.random.key(seed)
        k1, k2, k3 = jax.random.split(key, 3)
        B, N, D = (8, 2048, 256)
        hidden = HEADS * DIM_HEAD
        x = jax.random.normal(k1, (B, N, D), dtype=jnp.float32)
        Wqkv = jax.random.normal(k2, (D, 3 * hidden), dtype=jnp.float32) * D ** (-0.5)
        Wout = jax.random.normal(k3, (hidden, D), dtype=jnp.float32) * hidden ** (-0.5)
        gamma = jnp.ones((D,), dtype=jnp.float32)
        return {'x': x, 'Wqkv': Wqkv, 'Wout': Wout, 'gamma': gamma}
    _L0_mix_all = _L0_mix_setup()
    _L0_mix_in = {k: v for k, v in _L0_mix_all.items() if k in ('Wqkv', 'Wout', 'gamma')}
    del _L0_mix_all

    def _L0_ffn_setup():
        import jax, jax.numpy as jnp
        import numpy as np
        NUM_EXPERTS = 8
        TOP_K = 2
        B, S, D = (8, 1024, 256)

        def _moe(tokens, router_w, w1, b1, w2, b2):
            N = tokens.shape[0]
            E = router_w.shape[0]
            logits = tokens.astype(jnp.float32) @ router_w.astype(jnp.float32).T
            probs = jax.nn.softmax(logits, axis=-1)
            rw, re = jax.lax.top_k(probs, TOP_K)
            if TOP_K > 1:
                rw = rw / jnp.maximum(rw.sum(-1, keepdims=True), 1e-12)
            rw = rw.astype(tokens.dtype)
            combine = jnp.zeros((N, E), tokens.dtype).at[jnp.arange(N)[:, None], re].set(rw)
            out = tokens
            for e in range(E):
                h = jax.nn.gelu(tokens @ w1[e] + b1[e], approximate=False)
                y = h @ w2[e] + b2[e]
                out = out + combine[:, e:e + 1] * y
            return out
        key = jax.random.key(seed)
        ks = jax.random.split(key, 4)
        scale = 1.0 / np.sqrt(D).astype(np.float32)
        return {'input_embeddings': jax.random.normal(ks[0], (B, S, D), jnp.float32), 'router_w': jax.random.normal(ks[1], (NUM_EXPERTS, D), jnp.float32) * scale, 'w1': jax.random.normal(ks[2], (NUM_EXPERTS, D, D), jnp.float32) * scale, 'b1': jnp.zeros((NUM_EXPERTS, D), jnp.float32), 'w2': jax.random.normal(ks[3], (NUM_EXPERTS, D, D), jnp.float32) * scale, 'b2': jnp.zeros((NUM_EXPERTS, D), jnp.float32)}
    _L0_ffn_all = _L0_ffn_setup()
    _L0_ffn_in = {k: v for k, v in _L0_ffn_all.items() if k in ('router_w', 'w1', 'b1', 'w2', 'b2')}
    del _L0_ffn_all
    return {'x': x, 'src': src, 'dst': dst, 'L0_gnn_W': _L0_gnn_in['W'], 'L0_gnn_b': _L0_gnn_in['b'], 'L0_mix_Wqkv': _L0_mix_in['Wqkv'], 'L0_mix_Wout': _L0_mix_in['Wout'], 'L0_mix_gamma': _L0_mix_in['gamma'], 'L0_ffn_router_w': _L0_ffn_in['router_w'], 'L0_ffn_w1': _L0_ffn_in['w1'], 'L0_ffn_b1': _L0_ffn_in['b1'], 'L0_ffn_w2': _L0_ffn_in['w2'], 'L0_ffn_b2': _L0_ffn_in['b2']}

def reference(x, src, dst, L0_gnn_W, L0_gnn_b, L0_mix_Wqkv, L0_mix_Wout, L0_mix_gamma, L0_ffn_router_w, L0_ffn_w1, L0_ffn_b1, L0_ffn_w2, L0_ffn_b2):
    import jax
    import jax.numpy as jnp

    def _L0_gnn_ref(input_matrix, adjacency_coo_matrix, W, b):
        import jax, jax.numpy as jnp
        import numpy as np
        N_NODES = 6250
        EPS = 1e-12
        src = adjacency_coo_matrix[0]
        dst = adjacency_coo_matrix[1]
        neigh_sum = jax.ops.segment_sum(input_matrix[src], dst, num_segments=N_NODES)
        deg = jax.ops.segment_sum(jnp.ones_like(dst, dtype=input_matrix.dtype), dst, num_segments=N_NODES)
        neigh_mean = neigh_sum / jnp.maximum(deg, 1.0)[:, None]
        h = jnp.concatenate([input_matrix, neigh_mean], axis=-1)
        out = jax.nn.relu(h @ W + b)
        norm = jnp.maximum(jnp.linalg.norm(out, axis=-1, keepdims=True), EPS)
        return out / norm

    def _L0_mix_ref(x, Wqkv, Wout, gamma):
        import jax, jax.numpy as jnp
        import numpy as np
        HEADS = 8
        DIM_HEAD = 32
        SCALE = DIM_HEAD ** (-0.5)
        EPS = 1e-05

        def _layernorm_gamma(x, gamma):
            mu = jnp.mean(x, axis=-1, keepdims=True)
            var = jnp.var(x, axis=-1, keepdims=True)
            return (x - mu) * jax.lax.rsqrt(var + EPS) * gamma
        B, N, D = x.shape
        qkv = x @ Wqkv
        q, k, v = jnp.split(qkv, 3, axis=-1)

        def to_heads(t):
            return t.reshape(B, N, HEADS, DIM_HEAD).transpose(0, 2, 1, 3)
        q, k, v = map(to_heads, (q, k, v))
        q = jax.nn.softmax(q, axis=-1) * SCALE
        k = jax.nn.softmax(k, axis=2)
        context = jnp.einsum('bhnd,bhne->bhde', k, v)
        out = jnp.einsum('bhde,bhnd->bhne', context, q)
        out = out.transpose(0, 2, 1, 3).reshape(B, N, HEADS * DIM_HEAD)
        out = out @ Wout
        return _layernorm_gamma(out, gamma)

    def _L0_ffn_ref(input_embeddings, router_w, w1, b1, w2, b2):
        import jax, jax.numpy as jnp
        import numpy as np
        NUM_EXPERTS = 8
        TOP_K = 2
        B, S, D = (8, 1024, 256)

        def _moe(tokens, router_w, w1, b1, w2, b2):
            N = tokens.shape[0]
            E = router_w.shape[0]
            logits = tokens.astype(jnp.float32) @ router_w.astype(jnp.float32).T
            probs = jax.nn.softmax(logits, axis=-1)
            rw, re = jax.lax.top_k(probs, TOP_K)
            if TOP_K > 1:
                rw = rw / jnp.maximum(rw.sum(-1, keepdims=True), 1e-12)
            rw = rw.astype(tokens.dtype)
            combine = jnp.zeros((N, E), tokens.dtype).at[jnp.arange(N)[:, None], re].set(rw)
            out = tokens
            for e in range(E):
                h = jax.nn.gelu(tokens @ w1[e] + b1[e], approximate=False)
                y = h @ w2[e] + b2[e]
                out = out + combine[:, e:e + 1] * y
            return out
        b, s, d = input_embeddings.shape
        tokens = input_embeddings.reshape(b * s, d)
        return _moe(tokens, router_w, w1, b1, w2, b2).reshape(b, s, d)
    edge_index = jnp.stack([src, dst])
    xn = _layernorm(x, axis=-1)
    x = x + _L0_gnn_ref(xn, edge_index, L0_gnn_W, L0_gnn_b) + _L0_mix_ref(xn[None], L0_mix_Wqkv, L0_mix_Wout, L0_mix_gamma)[0]
    x = x + _L0_ffn_ref(_layernorm(x, axis=-1)[None], L0_ffn_router_w, L0_ffn_w1, L0_ffn_b1, L0_ffn_w2, L0_ffn_b2)[0]
    return x

_drawn_inputs = setup_inputs


def setup_inputs(seed=0):
    import zlib

    import numpy as np

    out = dict(_drawn_inputs(seed))
    spreads = {'L0_gnn_b': (0.0, 0.579),
     'L0_mix_gamma': (1.0, 0.2),
     'L0_ffn_b1': (0.0, 0.363),
     'L0_ffn_b2': (0.0, 0.1)}
    factors = {}
    for name, (base, spread) in spreads.items():
        noise = np.random.default_rng([zlib.crc32(name.encode()), seed]).standard_normal(out[name].shape)
        drawn = base * np.exp(spread * noise) if base else spread * noise
        out[name] = jnp.asarray(drawn.astype(out[name].dtype))
    for name, factor in factors.items():
        out[name] = (out[name] * factor).astype(out[name].dtype)
    return out
```

```python
from contextlib import ExitStack

import concourse.bass as bass
from concourse import mybir

F32 = mybir.dt.float32
F16 = mybir.dt.float16
I32 = mybir.dt.int32
U32 = mybir.dt.uint32
ALU = mybir.AluOpType
ACT = mybir.ActivationFunctionType
AX = mybir.AxisListType

P = 128
NODES = 6250
EDGES = 200000
D = 256
KC = D // P
HEADS = 8
DH = D // HEADS
EXPERTS = 8
LN_EPS = 1e-5
NORM_FLOOR = 1e-12
SCALE = DH ** -0.5
RSQRT_MAGIC = 0x5F3759DF

BLOCKS = -(-NODES // P)
LAST_ROWS = NODES - (BLOCKS - 1) * P
NODES_PAD = BLOCKS * P
EDGES_PER_NODE = EDGES // NODES
ZONE_TILES = 16
ZONE_NODES = ZONE_TILES * P // EDGES_PER_NODE
ZONE_BACK = (P - ZONE_NODES) // 2
TILES = BLOCKS * P * EDGES_PER_NODE // P
ZONES = TILES // ZONE_TILES
SUM_COLS = NODES_PAD + P

GROUP = 7
GROUPS = BLOCKS // GROUP
RING = 32
OH_RING = 16
GATHERS_PER_WAIT = 8
LEAD = 8

B1_TILES = 2 * ZONE_TILES
TURN_TILES = 14 * ZONE_TILES
TURN_PERIODS = 8
TURNS = 5
LAST_PERIODS = 6
TAIL_BLOCKS = (46, 47, 48)
IDX_CHUNK = TURN_TILES // 4
assert BLOCKS == GROUP * GROUPS and GROUPS * B1_TILES == TURN_TILES
assert TILES == (TURNS + 2) * TURN_TILES and TURNS * TURN_PERIODS + LAST_PERIODS == TAIL_BLOCKS[0]

C_EYE = P
C_IOTA = 384
C_MASK = 512
C_COLS = 640

WEIGHT_LOADS = 10
Q_LINKS, HEAD_LINKS, ROUTE_LINKS = 3, 37, 9


def b1_tiles(k):
    return range(k * B1_TILES // GROUP, (k + 1) * B1_TILES // GROUP)


def steps(periods, rate):
    count = [min(TURN_TILES, -(-int(4 * rate) * k // 4)) for k in range(periods * EXPERTS)] + [TURN_TILES]
    return [range(a, b) for a, b in zip(count, count[1:])]


TURN_STEPS = steps(TURN_PERIODS, 3.75)
LAST_STEPS = steps(LAST_PERIODS, 5.5)
TAIL_STEPS = [range(0)] * (len(TAIL_BLOCKS) * EXPERTS)


def zones_ended(tiles):
    return [j // ZONE_TILES for j in tiles if j % ZONE_TILES == ZONE_TILES - 1]


def b1_order():
    order = []
    for k in range(GROUP):
        order.append(("xn", k))
        order += [("zone", z) for z in zones_ended(b1_tiles(k))]
    return order


def main_order(plan, heads):
    order = []
    for k, tiles in enumerate(plan):
        m, e = divmod(k, EXPERTS)
        if e == 0:
            order.append(("logits", m))
        if e == 2:
            order.append(("combine", m))
        if e == 3:
            order.append(("bias", m))
            if m in heads:
                order.append(("q", m + 1))
        order += [("zone", z) for z in zones_ended(tiles)]
        if e == EXPERTS - 1 and m in heads:
            order.append(("tokens", m + 1))
    return order


def stand_alone(engine, passed):
    engine.sem_inc(passed, 1)


class Uses:

    def __init__(self, base, order):
        self.base, self.at, self.count = base, {name: n for n, name in enumerate(order)}, len(order)

    def __getitem__(self, name):
        return self.base + self.at[name]


USES_B1 = len(b1_order())
USES_TURN = len(main_order(TURN_STEPS, range(TURN_PERIODS)))
USE_FLAG = 0
BASE_B1 = 1
USE_KMAX_COL = BASE_B1 + GROUPS * USES_B1
USE_KMAX_ROW = USE_KMAX_COL + 1
USE_CONTEXT = USE_KMAX_COL + 2
BASE_HEAD0 = USE_KMAX_COL + 3
HEAD0 = [("q", 0), ("tokens", 0)]
BASE_MAIN = BASE_HEAD0 + len(HEAD0)
BASE_LAST = BASE_MAIN + TURNS * USES_TURN
LAST_ORDER = main_order(LAST_STEPS, range(LAST_PERIODS))
BASE_TAIL = BASE_LAST + len(LAST_ORDER)
TAIL_ORDER = main_order(TAIL_STEPS, range(len(TAIL_BLOCKS) - 1))


class Block_:

    def __init__(self, number, half, parity):
        self.n, self.half, self.par = number, half, parity
        self.first = isinstance(number, int) and number == 0


def block_at(first, first_half, m):
    return Block_(first + m, first_half + m // 2, m % 2)


def gps_kernel(nc, x, src, dst, gnn_w, gnn_b, wqkv, wout, gamma, router_wt, w1, b1t, w2, b2, consts, out):
    with ExitStack() as ctx:
        def sb(name, cols, dt=F32, rows=P):
            return ctx.enter_context(nc.sbuf_tensor("sb_" + name, [rows, cols], dt))

        def bank(name):
            return ctx.enter_context(nc.psum_tensor("ps_" + name, [P, 512], F32))

        def sem(name):
            return ctx.enter_context(nc.semaphore(name))

        table = nc.dram_tensor("xn_table", [NODES_PAD, 2 * D], F16, kind="Internal").ap()
        xnt_dram = nc.dram_tensor("xn_transposed", [BLOCKS * P, D], F32, kind="Internal").ap()
        kv_dram = nc.dram_tensor("keys_values", [NODES_PAD, 2 * D], F32, kind="Internal").ap()

        zone_sum = [bank("zone0"), bank("zone1")]
        turned = bank("turned")
        proj = bank("proj")
        hidden = [bank("hidden0"), bank("hidden1")]
        expert = [bank("expert0"), bank("expert1")]

        cst = sb("consts", C_COLS)
        eye = cst[:, C_EYE:C_EYE + P]
        head_mask = cst[:, C_MASK:C_MASK + P]
        iota_e = cst[:, C_IOTA:C_IOTA + EXPERTS]
        iota16 = sb("iota16", P, F16)
        ones = sb("ones", P)
        w_kv = sb("w_kv", KC * 2 * D)
        w_aq = sb("w_aq", KC * 2 * D)
        w_nb = sb("w_nb", KC * D)
        w_out = sb("w_out", KC * D)
        w_mix = sb("w_mix", KC * D)
        bias_row = sb("bias_row", D)
        gamma_row = sb("gamma_row", D)
        router = sb("router", KC * EXPERTS)
        b1_col = sb("b1_col", EXPERTS * KC)
        b2_row = sb("b2_row", D, rows=EXPERTS)
        ring = sb("ring", RING * (2 * D + 1), F16)
        onehot = sb("onehot", OH_RING * P, F16)
        idx = sb("idx", TILES, I32)
        idx_now = sb("idx_now", TURN_TILES, I32)
        rel = sb("rel", TILES)
        rel_now = sb("rel_now", TURN_TILES)
        far = sb("far", TILES)
        far_now = sb("far_now", ZONE_TILES)
        sums = sb("sums", KC * SUM_COLS)
        zone_deg = sb("zone_deg", ZONES + 3)
        far_deg = sb("far_deg", BLOCKS)
        zone_sb = [sb("zone_sb0", D + 1), sb("zone_sb1", D + 1)]
        zeros = sb("zeros", P + 1)
        small = sb("small", 256)
        small_i = sb("small_i", 32, I32)
        flag = sb("flag", 2, I32, rows=2)
        arena = sb("arena", BLOCKS * D)
        stage = sb("stage", GROUP * 2 * D)

        ring3 = ring[:, :].rearrange("p (r c) -> p r c", r=RING)
        onehot3 = onehot[:, :].rearrange("p (r c) -> p r c", r=OH_RING)
        sums3 = sums[:, :].rearrange("p (k c) -> p k c", k=KC)
        w_kv3 = w_kv[:, :].rearrange("p (k c) -> p k c", k=KC)
        w_aq3 = w_aq[:, :].rearrange("p (k c) -> p k c", k=KC)
        w_nb3 = w_nb[:, :].rearrange("p (k c) -> p k c", k=KC)
        w_out3 = w_out[:, :].rearrange("p (k c) -> p k c", k=KC)
        w_mix3 = w_mix[:, :].rearrange("p (k c) -> p k c", k=KC)
        router3 = router[:, :].rearrange("p (k c) -> p k c", k=KC)
        turned3 = turned[:, 0:D].rearrange("p (k c) -> p k c", k=KC)

        xn_all = arena[:, :].rearrange("p (b d) -> p b d", d=D)
        WE = EXPERTS * KC * D
        w1_sb = arena[:, 0:WE].rearrange("p (e k h) -> p e k h", e=EXPERTS, k=KC)
        w2_sb = arena[:, WE:2 * WE].rearrange("p (e k h) -> p e k h", e=EXPERTS, k=KC)

        def buf(tensor, n, first=0):
            return tensor[:, first + n * D:first + (n + 1) * D]

        def halves(ap):
            return ap.rearrange("p (k c) -> p k c", k=KC)

        def by_head(ap):
            return ap.rearrange("p (h c) -> p h c", h=HEADS)

        late = 2 * WE
        xnt = [buf(arena, n, late) for n in (0, 1)]
        x_in = [buf(arena, n, late) for n in (2, 3)]
        out_sb = [buf(arena, n, late) for n in (4, 5)]
        self_part, q_soft, gathered = (buf(arena, n, late) for n in (6, 7, 8))
        g_out, g_square, mixed, partly, x_mid = (buf(arena, n, late) for n in (9, 10, 11, 12, 13))
        tokens = buf(arena, 14, late)
        tokens_t = [buf(arena, n, late) for n in (15, 16)]
        act_h = [buf(stage, 0), buf(stage, 1)]
        q_turned = stage[:, 2 * D:3 * D + 1]
        combine_t = stage[0:EXPERTS, 4 * D:4 * D + P]

        rows16 = stage[:, :].bitcast(F16).rearrange("p (b c) -> p b c", c=2 * D)

        def rows16_of(g):
            return rows16[:, g % 2 * GROUP:(g % 2 + 1) * GROUP, :]

        xn_b = buf(stage, 0)
        xnt_b = [buf(stage, 1), buf(stage, 2)]
        kv_b = [stage[:, 3 * D:5 * D], stage[:, 5 * D:7 * D]]
        k_max = buf(stage, 7)
        k_max_row = buf(stage, 8)
        k_exp = [buf(stage, 9), buf(stage, 10)]
        v_first = 11 * D
        v_b = [stage[:, v_first + n * (D + 2):v_first + (n + 1) * (D + 2)].rearrange("p (k c) -> p k c", k=KC)
               for n in (0, 1)]
        k_b = [buf(stage, 1), buf(stage, 2)]
        ctx_sb = buf(stage, 3)
        ctx_t = buf(stage, 4)

        stats = small[:, 0:6 * GROUP]
        mean_var = small[:, 42:56].rearrange("p (b c) -> p b c", c=2)
        var_eps = small[:, 56:63]
        half_v = small[:, 63:70]
        rstd7 = [small[:, 216:223], small[:, 223:230]]
        shift7 = [small[:, 230:237], small[:, 237:244]]
        far_count = small[:, 84:85]
        k_col = small[:, 85:87]
        ctx_scale = small[:, 87:89]
        q_max = small[:, 89:97]
        q_sum = small[:, 97:105]
        deg4 = small[:, 105:109]
        inv_deg = small[:, 109:110]
        st6 = small[:, 110:116]
        mv = small[:, 116:118]
        sq_var = small[:, 118:120]
        inv_norms = small[:, 120:122]
        h2 = small[:, 122:124]
        st6b = small[:, 124:130]
        mvb = small[:, 130:132]
        var_b = small[:, 132:133]
        inv_b = small[:, 133:134]
        h_b = small[:, 134:135]
        logits = small[:, 136:144]
        top8 = small[:, 144:152]
        pick1 = small[:, 152:160]
        rest = small[:, 160:168]
        top8b = small[:, 168:176]
        pick2 = small[:, 176:184]
        gap = small[:, 184:185]
        tanh_gap = small[:, 185:186]
        route1 = small[:, 186:187]
        route2 = small[:, 187:188]
        combine = [small[:, 192:200], small[:, 200:208]]
        comb_part = small[:, 208:216]
        tile_i = small_i[:, 0:7]
        top_i = small_i[:, 8:16].bitcast(U32)
        top_ib = small_i[:, 16:24].bitcast(U32)

        const_landed, dst_landed, idx_landed = sem("const_landed"), sem("dst_landed"), sem("idx_landed")
        x_landed = [sem(f"x_landed{g}") for g in range(GROUPS)]
        weights_landed = sem("weights_landed")
        experts_landed = sem("experts_landed")
        passed = sem("passed")
        cleared, base_made = sem("cleared"), sem("base_made")
        stat_chain, rstd_made = sem("stat_chain"), sem("rstd_made")
        xn_made, hi_made, lo_made = sem("xn_made"), sem("hi_made"), sem("lo_made")
        rows_stored = [sem("rows_stored0"), sem("rows_stored1")]
        far_chain, far_counted, flag_made = sem("far_chain"), sem("far_counted"), sem("flag_made")
        idx_copied = sem("idx_copied")
        landed = [sem(f"gather_landed{r}") for r in range(RING)]
        tiles_used = sem("tiles_used")
        onehot_made = sem("onehot_made")
        rel_copied = sem("rel_copied")
        zone_copied = sem("zone_copied")
        zone_added = sem("zone_added")
        turn_filled, turn_read = sem("turn_filled"), sem("turn_read")
        pre_idx, pre_landed = sem("pre_idx"), sem("pre_landed")
        pre_chain, pre_onehots, pre_summed = sem("pre_chain"), sem("pre_onehots"), sem("pre_summed")
        pre_copied, pre_turned, pre_added = sem("pre_copied"), sem("pre_turned"), sem("pre_added")
        xn_copied = sem("xn_copied")
        kv_filled, kv_copied = sem("kv_filled"), sem("kv_copied")
        xnt_stored = [sem("xnt_stored0"), sem("xnt_stored1")]
        kv_stored = [sem("kv_stored0"), sem("kv_stored1")]
        k_maxed = sem("k_maxed")
        k_chain = sem("k_chain")
        k_landed = [sem("k_landed0"), sem("k_landed1")]
        k_shifted, k_exped, context_summed = sem("k_shifted"), sem("k_exped"), sem("context_summed")
        mix_filled, mix_ready = sem("mix_filled"), sem("mix_ready")
        xnt_landed = [sem("xnt_landed0"), sem("xnt_landed1")]
        xin_landed = [sem("xin_landed0"), sem("xin_landed1")]
        proj_filled, proj_read = sem("proj_filled"), sem("proj_read")
        q_chain, q_exped, q_ready = sem("q_chain"), sem("q_exped"), sem("q_ready")
        sums_staged = sem("sums_staged")
        head_chain = sem("head_chain")
        tokens_ready = sem("tokens_ready")
        route_chain, gap_made, tanh_made, combine_made = (
            sem("route_chain"), sem("gap_made"), sem("tanh_made"), sem("combine_made"))
        hidden_filled = sem("hidden_filled")
        hidden_act = sem("hidden_act")
        expert_filled = sem("expert_filled")
        expert_added = sem("expert_added")
        out_stored = [sem("out_stored0"), sem("out_stored1")]

        block = ctx.enter_context(nc.Block())

        def kv_uses(i, k):
            return (4 * i if k % 2 == 0 else 3 * i) + k // 2

        @block.sync
        def _(sp):
            for s in out_stored + kv_stored + xnt_stored:
                sp.sem_inc(s, 16)
            x_rows = x.rearrange("(b p) d -> p b d", p=P)
            for g in range(GROUPS):
                sp.dma_start(xn_all[:, g * GROUP:(g + 1) * GROUP, :],
                             x_rows[:, g * GROUP:(g + 1) * GROUP, :]).then_inc(x_landed[g], 16)
                if g == 0:
                    sp.dma_start(cst[:, :], consts).then_inc(const_landed, 16)
                    sp.dma_start(far[:, :].bitcast(I32), dst).then_inc(dst_landed, 16)
                    sp.dma_start(idx[:, :], src).then_inc(idx_landed, 16)
            loads = [
                (w_kv3, wqkv.rearrange("(k p) c -> p k c", p=P)[:, :, D:3 * D]),
                (w_aq3[:, :, 0:D], gnn_w[0:D].rearrange("(k p) c -> p k c", p=P)),
                (w_aq3[:, :, D:2 * D], wqkv.rearrange("(k p) c -> p k c", p=P)[:, :, 0:D]),
                (w_nb3, gnn_w[D:2 * D].rearrange("(k p) c -> p k c", p=P)),
                (w_out3, wout.rearrange("(k p) c -> p k c", p=P)),
                (bias_row[:, :], gnn_b.to_broadcast([P, D])),
                (gamma_row[:, :], gamma.to_broadcast([P, D])),
                (router3, router_wt.rearrange("(k p) c -> p k c", p=P)),
                (b1_col[:, :], b1t),
                (b2_row[:, :], b2),
            ]
            assert len(loads) == WEIGHT_LOADS
            for to, of in loads:
                sp.dma_start(to, of).then_inc(weights_landed, 16)
            table_rows = table.rearrange("(b p) c -> p b c", p=P)
            for g in range(GROUPS):
                sp.wait_ge(lo_made, g + 1)
                sp.dma_start(table_rows[:, g * GROUP:(g + 1) * GROUP, :],
                             rows16_of(g)).then_inc(rows_stored[g % 2], 16)
            with sp.Fori(0, GROUPS) as i:
                uses = Uses(i * USES_B1 + BASE_B1, b1_order())
                for k in range(GROUP):
                    sp.wait_ge(turn_read, uses["xn", k] + 1)
                    sp.dma_start(xnt_dram[bass.ds((i * GROUP + k) * P, P), :],
                                 xnt_b[k % 2]).then_inc(xnt_stored[k % 2], 16)
                    sp.wait_ge(kv_copied, i * GROUP + k + 1)
                    sp.dma_start(kv_dram[bass.ds((i * GROUP + k) * P, P), :],
                                 kv_b[k % 2]).then_inc(kv_stored[k % 2], 16)
            sp.wait_ge(turn_read, BASE_B1 + GROUPS * USES_B1)
            sp.dma_start(w1_sb, w1.rearrange("e (k p) h -> p e k h", p=P)).then_inc(experts_landed, 16)
            sp.dma_start(w2_sb, w2.rearrange("e (k p) h -> p e k h", p=P)).then_inc(experts_landed, 16)
            for n, uses_n in ((0, 4 * GROUPS), (1, 3 * GROUPS)):
                sp.wait_ge(kv_stored[n], 16 + 16 * uses_n)
                sp.wait_ge(xnt_stored[n], 16 + 16 * uses_n)

            def load_kv(b, parity, rows=P):
                keys = kv_dram[bass.ds(b * P, rows), 0:D]
                values = kv_dram[bass.ds(b * P, rows), D:2 * D].rearrange("p (k c) -> p k c", k=KC)
                sp.dma_start(k_b[parity][0:rows], keys).then_inc(k_landed[parity], 16)
                sp.dma_start(v_b[parity][0:rows, :, 0:P], values).then_inc(k_landed[parity], 16)

            sp.wait_ge(k_chain, 1)
            load_kv(0, 0)
            load_kv(1, 1)
            with sp.Fori(0, (BLOCKS - 1) // 8 - 1) as i:
                for k in range(8):
                    sp.wait_ge(context_summed, i * 8 + k + 1)
                    load_kv(i * 8 + k + 2, k % 2)
            for b in range(BLOCKS - 1 - 8, BLOCKS - 2):
                sp.wait_ge(context_summed, b + 1)
                load_kv(b + 2, b % 2, LAST_ROWS if b + 2 == BLOCKS - 1 else P)
            sp.wait_ge(mix_ready, 1)

            def load_block(b):
                sp.dma_start(xnt[b.par], xnt_dram[bass.ds(b.n * P, P), :]).then_inc(xnt_landed[b.par], 16)
                sp.dma_start(x_in[b.par], x[bass.ds(b.n * P, P), :]).then_inc(xin_landed[b.par], 16)

            load_block(Block_(0, 0, 0))
            load_block(Block_(1, 0, 1))

            def period(b, rows, load):
                if load:
                    sp.wait_ge(proj_filled, 2 * b.n + 1)
                    stand_alone(sp, passed)
                    sp.wait_ge(tokens_ready, b.n + 1)
                    load_block(Block_(b.n + 2, b.half + 1, b.par))
                sp.wait_ge(expert_added, (b.n + 1) * EXPERTS + 2)
                sp.dma_start(out[bass.ds(b.n * P, rows), :],
                             out_sb[b.par][0:rows]).then_inc(out_stored[b.par], 16)

            with sp.Fori(0, TURNS) as s:
                for m in range(TURN_PERIODS):
                    period(block_at(s * TURN_PERIODS, s * (TURN_PERIODS // 2), m), P, True)
            first = TURNS * TURN_PERIODS
            for m in range(LAST_PERIODS + len(TAIL_BLOCKS)):
                b = block_at(first, first // 2, m)
                period(b, LAST_ROWS if b.n == BLOCKS - 1 else P, b.n + 2 < BLOCKS)
            for n in (0, 1):
                sp.wait_ge(out_stored[n], 16 + 16 * ((BLOCKS + 1 - n) // 2))

        @block.gpsimd
        def _(pool):
            pool.iota(rel[:, :].bitcast(I32), [[ZONE_NODES, ZONES], [0, ZONE_TILES]], base=-ZONE_BACK,
                      channel_multiplier=0).then_inc(base_made, 1)
            for g in range(GROUPS):
                pool.wait_ge(hi_made, g + 1)
                rows = rows16_of(g)
                pool.tensor_tensor(rows[:, :, D:2 * D], xn_all[:, g * GROUP:(g + 1) * GROUP, :],
                                   rows[:, :, 0:D], ALU.subtract).then_inc(lo_made, 1)
            pool.wait_ge(idx_landed, 16)
            pool.wait_ge(cleared, 1)
            for n in (0, 1):
                pool.wait_ge(rows_stored[n], 16 * ((GROUPS + 1 - n) // 2))

            def gather(tile_idx, place, signal):
                pool.indirect_dma_start(ring3[:, place, 0:2 * D], None, table,
                                        bass.IndirectOffsetOnAxis(tile_idx, 0)).then_inc(signal, 16)

            pool.wait_ge(flag_made, 1)
            some_far = pool.value_load(flag[0:1, 0:1], min_val=0, max_val=EDGES)
            with pool.If(some_far > 0):
                with pool.Fori(0, ZONES) as z:
                    pool.wait_ge(pre_summed, z * BLOCKS + 1)
                    pool.tensor_copy(idx_now[:, 0:ZONE_TILES],
                                     idx[:, bass.ds(z * ZONE_TILES, ZONE_TILES)]).then_inc(pre_idx, 1)
                    pool.wait_ge(pre_idx, z + 1)
                    stand_alone(pool, passed)
                    for j in range(ZONE_TILES):
                        gather(idx_now[:, j:j + 1], j, pre_landed)
                pool.wait_ge(pre_summed, ZONES * BLOCKS + 1)
            with pool.Fori(0, TILES // TURN_TILES) as s:
                for j in range(TURN_TILES):
                    if j % IDX_CHUNK == 0:
                        pool.tensor_copy(idx_now[:, j:j + IDX_CHUNK],
                                         idx[:, bass.ds(s * TURN_TILES + j, IDX_CHUNK)]).then_inc(idx_copied, 1)
                        pool.wait_ge(idx_copied, s * (TURN_TILES // IDX_CHUNK) + j // IDX_CHUNK + 1)
                    if j % GATHERS_PER_WAIT == 0:
                        pool.wait_ge(tiles_used, s * TURN_TILES + j + GATHERS_PER_WAIT)
                        stand_alone(pool, passed)
                    gather(idx_now[:, j:j + 1], j % RING, landed[j % RING])

        @block.tensor
        def _(pe):
            pe.sem_inc(tiles_used, RING)
            pe.sem_inc(expert_filled, 2)
            pe.sem_inc(pre_summed, 1)

            def sum_tile(tile0, ring0, zone0, j):
                bank_ = zone_sum[(j // ZONE_TILES) % 2]
                oh = onehot3[:, j % OH_RING, :]
                rows = ring3[:, j % RING, :]
                first, last = j % ZONE_TILES == 0, j % ZONE_TILES == ZONE_TILES - 1
                if first:
                    pe.wait_ge(zone_copied, zone0 + j // ZONE_TILES + 1)
                pe.wait_ge(landed[j % RING], (ring0 + j // RING + 1) * 16)
                pe.wait_ge(onehot_made, tile0 + j + 1)
                pe.matmul(bank_[:, 0:D], oh, rows[:, 0:D], start=first, stop=False, skip_group_check=True)
                pe.matmul(bank_[:, 0:D + 1], oh, rows[:, D:2 * D + 1], start=False, stop=last,
                          skip_group_check=True).then_inc(tiles_used, 1)

            def turn(use, ins, width):
                pe.wait_ge(turn_read, use)
                for k in range(KC):
                    t = pe.transpose(turned[:, k * P:(k + 1) * P], ins[:, k * P:(k + 1) * P], eye)
                return t

            def turn_zone(uses, zone0, z):
                pe.wait_ge(zone_copied, zone0 + z + 3)
                turn(uses["zone", z], zone_sb[z % 2], D).then_inc(turn_filled, 1)

            pe.wait_ge(far_counted, 1)
            pe.matmul(turned[0:1, 0:1], far_count, ones[:, 0:1], start=True, stop=True).then_inc(turn_filled, 1)

            pe.wait_ge(flag_made, 1)
            some_far = pe.value_load(flag[0:1, 0:1], min_val=0, max_val=EDGES)
            with pe.If(some_far > 0):
                with pe.Fori(0, ZONES) as z:
                    pe.wait_ge(pre_landed, (z + 1) * (16 * ZONE_TILES))
                    stand_alone(pe, passed)
                    with pe.Fori(0, BLOCKS) as w:
                        n = z * BLOCKS + w
                        pe.wait_ge(pre_onehots, n + 1)
                        for j in range(ZONE_TILES):
                            oh, rows = onehot3[:, j, :], ring3[:, j, :]
                            pe.matmul(zone_sum[0][:, 0:D], oh, rows[:, 0:D], start=j == 0, stop=False,
                                      skip_group_check=True)
                            mm = pe.matmul(zone_sum[0][:, 0:D + 1], oh, rows[:, D:2 * D + 1], start=False,
                                           stop=j == ZONE_TILES - 1, skip_group_check=True)
                        mm.then_inc(pre_summed, 1)
                        pe.wait_ge(pre_copied, n + 1)
                        pe.wait_ge(pre_added, n + 1)
                        for k in range(KC):
                            t = pe.transpose(turned[:, k * P:(k + 1) * P], zone_sb[0][:, k * P:(k + 1) * P], eye)
                        t.then_inc(pre_turned, 1)
                pe.wait_ge(pre_added, ZONES * BLOCKS + 1)

            pe.wait_ge(weights_landed, 16 * WEIGHT_LOADS)
            with pe.Fori(0, GROUPS) as i:
                uses = Uses(i * USES_B1 + BASE_B1, b1_order())
                for k in range(GROUP):
                    for j in b1_tiles(k):
                        sum_tile(i * B1_TILES, i, i * 2, j)
                    pe.wait_ge(xn_copied, i * GROUP + k + 1)
                    turn(uses["xn", k], xn_b, D).then_inc(turn_filled, 1)
                    pe.wait_ge(turn_read, uses["xn", k] + 1)
                    if k > 0:
                        pe.wait_ge(kv_copied, i * GROUP + k)
                    for c in range(KC):
                        mm = pe.matmul(proj[:, :], halves(xnt_b[k % 2])[:, c, :], w_kv3[:, c, :],
                                       start=c == 0, stop=c == KC - 1)
                    mm.then_inc(kv_filled, 1)
                    for z in zones_ended(b1_tiles(k)):
                        turn_zone(uses, i * 2, z)
                    if k == GROUP - 1:
                        pe.wait_ge(kv_copied, i * GROUP + k + 1)

            pe.wait_ge(k_maxed, BLOCKS + 1)
            turn(USE_KMAX_COL, k_max, D).then_inc(turn_filled, 1)
            pe.wait_ge(k_chain, 3)
            turn(USE_KMAX_ROW, k_exp[0], D).then_inc(turn_filled, 1)

            pe.wait_ge(turn_read, USE_KMAX_ROW + 1)
            for c in range(KC):
                pe.matmul(expert[c][:, 0:P + 1], zeros[:, 0:P], zeros[:, :], start=True, stop=False,
                          skip_group_check=True)

            def add_context(b, parity, rows=P, stop=False):
                pe.wait_ge(k_exped, b + 1)
                for c in range(KC):
                    mm = pe.matmul(expert[c][:, 0:P + 1], k_exp[parity][0:rows, c * P:(c + 1) * P],
                                   v_b[parity][0:rows, c, :], start=False, stop=stop, skip_group_check=True)
                mm.then_inc(context_summed, 1)

            with pe.Fori(0, (BLOCKS - 1) // 8) as i:
                for k in range(8):
                    add_context(i * 8 + k, k % 2)
            add_context(BLOCKS - 1, 0, LAST_ROWS, True)
            pe.wait_ge(k_chain, 6)
            turn(USE_CONTEXT, ctx_sb, D).then_inc(turn_filled, 1)
            pe.wait_ge(turn_read, USE_CONTEXT + 1)
            for c in range(KC):
                mm = pe.matmul(proj[:, c * D:(c + 1) * D], halves(ctx_t)[:, c, :], w_out3[:, c, :],
                               start=True, stop=True, skip_group_check=True)
            mm.then_inc(mix_filled, 1)
            pe.wait_ge(mix_ready, 1)

            def project(b):
                pe.wait_ge(xnt_landed[b.par], b.half * 16 + 16)
                if not b.first:
                    pe.wait_ge(proj_read, 2 * b.n)
                for c in range(KC):
                    mm = pe.matmul(proj[:, :], halves(xnt[b.par])[:, c, :], w_aq3[:, c, :],
                                   start=c == 0, stop=c == KC - 1)
                mm.then_inc(proj_filled, 1)

            def turn_q(b, use):
                pe.wait_ge(q_ready, b.n + 1)
                pe.wait_ge(sums_staged, b.n + 1)
                turn(use, q_soft, D)
                for n in range(4):
                    move = (n - 1) * ZONE_NODES - ZONE_BACK
                    mm = pe.matmul(turned[:, D:D + 1], cst[:, P - move:2 * P - move], deg4[:, n:n + 1],
                                   start=n == 0, stop=n == 3, skip_group_check=True)
                mm.then_inc(turn_filled, 1)

            def mix(b, use):
                pe.wait_ge(turn_read, use + 1)
                pe.wait_ge(proj_read, 2 * b.n + 1)
                for c in range(KC):
                    pe.matmul(proj[:, 0:D], halves(gathered)[:, c, :], w_nb3[:, c, :],
                              start=c == 0, stop=c == KC - 1, skip_group_check=True)
                for c in range(KC):
                    mm = pe.matmul(proj[:, D:2 * D], halves(q_turned[:, 0:D])[:, c, :], w_mix3[:, c, :],
                                   start=c == 0, stop=c == KC - 1, skip_group_check=True)
                mm.then_inc(proj_filled, 1)

            def turn_tokens(b, use):
                pe.wait_ge(tokens_ready, b.n + 1)
                turn(use, tokens, D).then_inc(turn_filled, 1)

            def route(b, use):
                pe.wait_ge(turn_read, use)
                for c in range(KC):
                    mm = pe.matmul(turned[:, 0:EXPERTS], halves(tokens_t[b.par])[:, c, :], router3[:, c, :],
                                   start=c == 0, stop=c == KC - 1, skip_group_check=True)
                mm.then_inc(turn_filled, 1)

            def turn_combine(b, use):
                pe.wait_ge(turn_read, use)
                pe.wait_ge(combine_made, b.n + 1)
                pe.transpose(turned[0:EXPERTS, 0:P], combine[b.par], eye).then_inc(turn_filled, 1)

            def add_b2(b, use):
                pe.wait_ge(turn_read, use)
                pe.matmul(turned[:, 0:D], combine_t, b2_row[:, :], start=True, stop=True,
                          skip_group_check=True).then_inc(turn_filled, 1)

            def up(b, e):
                pe.wait_ge(hidden_act, b.n * EXPERTS + e + 1)
                for j in range(KC):
                    for c in range(KC):
                        mm = pe.matmul(hidden[e % 2][:, j * P:(j + 1) * P],
                                       w1_sb[:, e, c, j * P:(j + 1) * P], halves(tokens_t[b.par])[:, c, :],
                                       start=c == 0, stop=c == KC - 1, skip_group_check=True)
                mm.then_inc(hidden_filled, 1)

            def down(b, e):
                pe.wait_ge(hidden_act, b.n * EXPERTS + e + 3)
                pe.wait_ge(expert_added, b.n * EXPERTS + e + 1)
                for c in range(KC):
                    mm = pe.matmul(expert[e % 2][:, 0:D], halves(act_h[e % 2])[:, c, :], w2_sb[:, e, c, :],
                                   start=c == 0, stop=c == KC - 1, skip_group_check=True)
                mm.then_inc(expert_filled, 1)

            def period(b, nxt, m, e, tiles, uses, tile0, ring0, zone0, first_use=None):
                for j in tiles:
                    sum_tile(tile0, ring0, zone0, j)
                if e == 0:
                    pe.wait_ge(turn_read, uses["logits", m])
                up(b, e)
                if e == 0:
                    route(b, uses["logits", m])
                    if nxt:
                        project(nxt)
                if e == 2:
                    turn_combine(b, uses["combine", m])
                if e == 3:
                    add_b2(b, uses["bias", m])
                    if nxt:
                        turn_q(nxt, uses["q", m + 1])
                if e == 4 and nxt:
                    mix(nxt, uses["q", m + 1])
                if e > 0:
                    down(b, e - 1)
                for z in zones_ended(tiles):
                    turn_zone(uses, zone0, z)
                if e == EXPERTS - 1:
                    down(b, e)
                    if nxt:
                        turn_tokens(nxt, uses["tokens", m + 1])

            b0 = Block_(0, 0, 0)
            uses0 = Uses(BASE_HEAD0, HEAD0)
            project(b0)
            turn_q(b0, uses0["q", 0])
            mix(b0, uses0["q", 0])
            turn_tokens(b0, uses0["tokens", 0])
            pe.wait_ge(experts_landed, 32)
            with pe.Fori(0, TURNS) as s:
                uses = Uses(s * USES_TURN + BASE_MAIN, main_order(TURN_STEPS, range(TURN_PERIODS)))
                for k, tiles in enumerate(TURN_STEPS):
                    m, e = divmod(k, EXPERTS)
                    b, nxt = (block_at(s * TURN_PERIODS, s * (TURN_PERIODS // 2), n) for n in (m, m + 1))
                    period(b, nxt, m, e, tiles, uses, s * TURN_TILES + TURN_TILES,
                           s * (TURN_TILES // RING) + TURN_TILES // RING,
                           s * (TURN_TILES // ZONE_TILES) + TURN_TILES // ZONE_TILES)
            n = TURNS + 1
            first = TURNS * TURN_PERIODS
            for plan, start, base, order, heads in (
                    (LAST_STEPS, first, BASE_LAST, LAST_ORDER, LAST_PERIODS),
                    (TAIL_STEPS, TAIL_BLOCKS[0], BASE_TAIL, TAIL_ORDER, len(TAIL_BLOCKS) - 1)):
                for k, tiles in enumerate(plan):
                    m, e = divmod(k, EXPERTS)
                    b, nxt = (block_at(start, start // 2, i) for i in (m, m + 1))
                    period(b, nxt if m < heads else None, m, e, tiles, Uses(base, order), n * TURN_TILES,
                           n * (TURN_TILES // RING), n * (TURN_TILES // ZONE_TILES))

        @block.scalar
        def _(act):
            act.sem_inc(zone_copied, 2)
            act.sem_inc(hidden_act, 2)
            for g in range(GROUPS):
                act.wait_ge(rstd_made, g + 1)
                for b in range(GROUP):
                    xb = xn_all[:, g * GROUP + b, :]
                    ins = act.activation(xb, xb, ACT.Identity, bias=shift7[g % 2][:, b:b + 1],
                                         scale=rstd7[g % 2][:, b:b + 1])
                ins.then_inc(xn_made, 1)
                act.wait_ge(xn_made, g + 1)
                if g >= 2:
                    act.wait_ge(rows_stored[g % 2], 16 * (g // 2))
                act.activation(rows16_of(g)[:, :, 0:D], xn_all[:, g * GROUP:(g + 1) * GROUP, :],
                               ACT.Copy).then_inc(hi_made, 1)

            act.wait_ge(flag_made, 1)
            some_far = act.value_load(flag[0:1, 0:1], min_val=0, max_val=EDGES)
            with act.If(some_far > 0):
                with act.Fori(0, ZONES * BLOCKS) as n:
                    act.wait_ge(pre_summed, n + 2)
                    act.wait_ge(pre_added, n + 1)
                    act.activation(zone_sb[0][:, :], zone_sum[0][:, 0:D + 1], ACT.Copy).then_inc(pre_copied, 1)
                act.wait_ge(pre_added, ZONES * BLOCKS + 1)

            def copy_zone(tile0, zone0, z):
                act.wait_ge(tiles_used, tile0 + (z + 1) * ZONE_TILES + RING)
                act.wait_ge(zone_added, zone0 + z + 1)
                act.activation(zone_sb[z % 2][:, :], zone_sum[z % 2][:, 0:D + 1],
                               ACT.Copy).then_inc(zone_copied, 1)

            for n in (0, 1):
                act.wait_ge(rows_stored[n], 16 * ((GROUPS + 1 - n) // 2))
            with act.Fori(0, GROUPS) as i:
                uses = Uses(i * USES_B1 + BASE_B1, b1_order())
                for k in range(GROUP):
                    act.wait_ge(turn_filled, uses["xn", k - 1] + 1 if k else i * USES_B1 + BASE_B1)
                    act.activation(xn_b, xn_all[:, bass.ds(i * GROUP + k, 1), :].rearrange("p b d -> p (b d)"),
                                   ACT.Copy).then_inc(xn_copied, 1)
                    for z in zones_ended(b1_tiles(k)):
                        copy_zone(i * B1_TILES, i * 2, z)
                    act.wait_ge(turn_filled, uses["xn", k] + 1)
                    act.wait_ge(xnt_stored[k % 2], kv_uses(i, k) * 16 + 16)
                    act.activation(xnt_b[k % 2], turned[:, 0:D], ACT.Copy).then_inc(turn_read, 1)
                    act.wait_ge(kv_filled, i * GROUP + k + 1)
                    act.wait_ge(kv_stored[k % 2], kv_uses(i, k) * 16 + 16)
                    act.wait_ge(k_maxed, i * GROUP + k + 1)
                    act.activation(kv_b[k % 2], proj[:, :], ACT.Copy).then_inc(kv_copied, 1)

            def exp_keys(b, parity, rows=P):
                act.wait_ge(k_shifted, b + 1)
                act.activation(k_exp[parity][0:rows], k_exp[parity][0:rows], ACT.Exp).then_inc(k_exped, 1)

            with act.Fori(0, (BLOCKS - 1) // 8) as i:
                for k in range(8):
                    exp_keys(i * 8 + k, k % 2)
            exp_keys(BLOCKS - 1, 0, LAST_ROWS)
            act.wait_ge(mix_ready, 1)

            def exp_q(b):
                act.wait_ge(proj_read, 2 * b.n + 1)
                act.activation(q_soft, q_soft, ACT.Exp).then_inc(q_exped, 1)

            def copy_q(b, use):
                act.wait_ge(turn_filled, use + 1)
                act.activation(q_turned, turned[:, 0:D + 1], ACT.Copy).then_inc(turn_read, 1)

            def copy_tokens(b, use):
                act.wait_ge(turn_filled, use + 1)
                act.activation(tokens_t[b.par], turned[:, 0:D], ACT.Copy).then_inc(turn_read, 1)

            def gelu(b, e):
                act.wait_ge(hidden_filled, b.n * EXPERTS + e + 1)
                act.wait_ge(expert_filled, b.n * EXPERTS + e + 1)
                for j in range(KC):
                    ins = act.activation(halves(act_h[e % 2])[:, j, :], hidden[e % 2][:, j * P:(j + 1) * P],
                                         ACT.Gelu, bias=b1_col[:, e * KC + j:e * KC + j + 1])
                ins.then_inc(hidden_act, 1)

            def period(b, nxt, m, e, tiles, uses, tile0, zone0):
                for z in zones_ended(tiles):
                    copy_zone(tile0, zone0, z)
                gelu(b, e)
                if e == 0 and nxt:
                    exp_q(nxt)
                if e == 1:
                    act.wait_ge(gap_made, b.n + 1)
                    act.activation(tanh_gap, gap, ACT.Tanh, scale=0.5).then_inc(tanh_made, 1)
                if e == 2:
                    act.wait_ge(turn_filled, uses["combine", m] + 1)
                    act.activation(combine_t, turned[0:EXPERTS, 0:P], ACT.Copy).then_inc(turn_read, 1)
                if e == 3 and nxt:
                    copy_q(nxt, uses["q", m + 1])
                if e == EXPERTS - 1 and nxt:
                    copy_tokens(nxt, uses["tokens", m + 1])

            b0 = Block_(0, 0, 0)
            uses0 = Uses(BASE_HEAD0, HEAD0)
            exp_q(b0)
            copy_q(b0, uses0["q", 0])
            copy_tokens(b0, uses0["tokens", 0])
            with act.Fori(0, TURNS) as s:
                uses = Uses(s * USES_TURN + BASE_MAIN, main_order(TURN_STEPS, range(TURN_PERIODS)))
                for k, tiles in enumerate(TURN_STEPS):
                    m, e = divmod(k, EXPERTS)
                    b, nxt = (block_at(s * TURN_PERIODS, s * (TURN_PERIODS // 2), n) for n in (m, m + 1))
                    period(b, nxt, m, e, tiles, uses, s * TURN_TILES + TURN_TILES,
                           s * (TURN_TILES // ZONE_TILES) + TURN_TILES // ZONE_TILES)
            n = TURNS + 1
            first = TURNS * TURN_PERIODS
            for plan, start, base, order, heads in (
                    (LAST_STEPS, first, BASE_LAST, LAST_ORDER, LAST_PERIODS),
                    (TAIL_STEPS, TAIL_BLOCKS[0], BASE_TAIL, TAIL_ORDER, len(TAIL_BLOCKS) - 1)):
                for k, tiles in enumerate(plan):
                    m, e = divmod(k, EXPERTS)
                    b, nxt = (block_at(start, start // 2, i) for i in (m, m + 1))
                    period(b, nxt if m < heads else None, m, e, tiles, Uses(base, order), n * TURN_TILES,
                           n * (TURN_TILES // ZONE_TILES))

        @block.vector
        def _(dve):
            dve.sem_inc(zone_added, 2)
            dve.sem_inc(expert_added, 2)
            dve.sem_inc(pre_added, 1)

            class Chain:

                def __init__(self, done, before):
                    self.done, self.before, self.links = done, before, 0

                def link(self, ins):
                    self.links += 1
                    ins.then_inc(self.done, 1)
                    dve.wait_ge(self.done, self.before + self.links)

            def rsqrt(chain, v, y, h, bits):
                chain.link(dve.tensor_scalar(bits, v.bitcast(I32), 1, None, ALU.logical_shift_right))
                chain.link(dve.tensor_scalar(y.bitcast(I32), bits, -1.0, float(RSQRT_MAGIC), ALU.mult, ALU.add))
                for _ in range(3):
                    chain.link(dve.tensor_tensor(h, v, y, ALU.mult))
                    chain.link(dve.scalar_tensor_tensor(out=h, in0=h, scalar=-0.5, in1=y, op0=ALU.mult, op1=ALU.mult))
                    chain.link(dve.scalar_tensor_tensor(out=y, in0=h, scalar=1.5, in1=y, op0=ALU.add, op1=ALU.mult))

            dve.memset(ones[:, :], 1.0)
            dve.memset(zeros[:, :], 0.0)
            dve.memset(zone_deg[:, :], 0.0)
            dve.memset(far_deg[:, :], 0.0)
            dve.memset(ring3[:, :, 2 * D:2 * D + 1], 1.0).then_inc(cleared, 1)

            chain = Chain(stat_chain, 0)
            for g in range(GROUPS):
                dve.wait_ge(x_landed[g], 16)
                if g >= 2:
                    dve.wait_ge(xn_made, g - 1)
                for b in range(GROUP):
                    ins = dve.bn_stats(stats[:, 6 * b:6 * b + 6], xn_all[:, g * GROUP + b, :])
                chain.link(ins)
                for b in range(GROUP):
                    ins = dve.bn_aggr(mean_var[:, b, :], stats[:, 6 * b:6 * b + 6])
                chain.link(ins)
                chain.link(dve.tensor_scalar(var_eps, mean_var[:, :, 1], LN_EPS, None, ALU.add))
                rsqrt(chain, var_eps, rstd7[g % 2], half_v, tile_i)
                dve.scalar_tensor_tensor(out=shift7[g % 2], in0=mean_var[:, :, 0], scalar=-1.0, in1=rstd7[g % 2],
                                         op0=ALU.mult, op1=ALU.mult).then_inc(rstd_made, 1)
                dve.wait_ge(rstd_made, g + 1)

            dve.wait_ge(const_landed, 16)
            chain = Chain(far_chain, 0)
            dve.tensor_copy(iota16[:, :], cst[:, C_IOTA:C_IOTA + P])
            dve.wait_ge(base_made, 1)
            dve.wait_ge(dst_landed, 16)
            dst_i = far[:, :].bitcast(I32)
            dst_f, inside, tmp = (sums[:, n * TILES:(n + 1) * TILES] for n in (0, 1, 2))
            chain.link(dve.tensor_copy(dst_f, dst_i))
            chain.link(dve.tensor_tensor(rel[:, :], dst_f, rel[:, :].bitcast(I32), ALU.subtract))
            chain.link(dve.tensor_scalar(tmp, rel[:, :], 0.0, None, ALU.is_ge))
            chain.link(dve.scalar_tensor_tensor(out=inside, in0=rel[:, :], scalar=float(P - 1), in1=tmp,
                                                op0=ALU.is_le, op1=ALU.mult))
            chain.link(dve.scalar_tensor_tensor(out=tmp, in0=dst_f, scalar=0.0, in1=inside,
                                                op0=ALU.is_ge, op1=ALU.subtract))
            chain.link(dve.scalar_tensor_tensor(out=far[:, :], in0=dst_f, scalar=1.0, in1=tmp,
                                                op0=ALU.add, op1=ALU.mult))
            dve.tensor_reduce(far_count, tmp, AX.X, ALU.add).then_inc(far_counted, 1)
            dve.wait_ge(far_counted, 1)
            chain.link(dve.memset(sums[:, :], 0.0))
            dve.wait_ge(turn_filled, USE_FLAG + 1)
            dve.tensor_copy(small[0:1, 244:245], turned[0:1, 0:1]).then_inc(turn_read, 1)
            dve.wait_ge(turn_read, USE_FLAG + 1)
            dve.tensor_copy(flag[0:1, 0:1], small[0:1, 244:245]).then_inc(flag_made, 1)
            dve.wait_ge(flag_made, 1)

            def make_onehot(place, rel_col):
                return dve.tensor_scalar(onehot3[:, place, :], iota16[:, :], rel_col, None, ALU.is_equal)

            some_far = dve.value_load(flag[0:1, 0:1], min_val=0, max_val=EDGES)
            with dve.If(some_far > 0):
                with dve.Fori(0, ZONES) as z:
                    dve.tensor_scalar(far_now[:, :], far[:, bass.ds(z * ZONE_TILES, ZONE_TILES)], -1.0, None,
                                      ALU.add).then_inc(pre_chain, 1)
                    with dve.Fori(0, BLOCKS) as w:
                        n = z * BLOCKS + w
                        dve.wait_ge(pre_chain, n + z + 1)
                        dve.wait_ge(pre_summed, n + 1)
                        for j in range(ZONE_TILES):
                            ins = make_onehot(j, far_now[:, j:j + 1])
                        ins.then_inc(pre_onehots, 1)
                        dve.wait_ge(pre_onehots, n + 1)
                        dve.tensor_scalar(far_now[:, :], far_now[:, :], -float(P), None,
                                          ALU.add).then_inc(pre_chain, 1)
                        dve.wait_ge(pre_turned, n + 1)
                        window = sums3[:, :, bass.ds(w * P + ZONE_BACK, P)]
                        dve.tensor_tensor(window, turned3, window, ALU.add)
                        dve.tensor_tensor(far_deg[:, bass.ds(w, 1)], zone_sb[0][:, D:D + 1],
                                          far_deg[:, bass.ds(w, 1)], ALU.add).then_inc(pre_added, 1)
                        dve.wait_ge(pre_added, n + 2)
                    dve.wait_ge(pre_chain, z * (BLOCKS + 1) + BLOCKS + 1)

            def tile_onehot(tile, rel_col, place):
                dve.wait_ge(tiles_used, tile + RING - OH_RING + 1)
                make_onehot(place, rel_col).then_inc(onehot_made, 1)

            def add_zone(uses, zone0, z, zone_expr):
                dve.wait_ge(turn_filled, uses["zone", z] + 1)
                dve.wait_ge(zone_added, zone0 + z + 2)
                window = sums3[:, :, bass.ds(zone_expr * ZONE_NODES, P)]
                dve.tensor_tensor(window, turned3, window, ALU.add).then_inc(turn_read, 1)
                dve.tensor_copy(zone_deg[:, bass.ds(zone_expr + 1, 1)],
                                zone_sb[z % 2][:, D:D + 1]).then_inc(zone_added, 1)

            for t in range(LEAD):
                tile_onehot(t, rel[:, t:t + 1], t)
            for n in (0, 1):
                dve.wait_ge(rows_stored[n], 16 * ((GROUPS + 1 - n) // 2))
            dve.memset(k_max, -3.0e38).then_inc(k_maxed, 1)
            with dve.Fori(0, GROUPS) as i:
                uses = Uses(i * USES_B1 + BASE_B1, b1_order())
                dve.wait_ge(onehot_made, i * B1_TILES + LEAD)
                dve.tensor_copy(rel_now[:, 0:B1_TILES],
                                rel[:, bass.ds(i * B1_TILES + LEAD, B1_TILES)]).then_inc(rel_copied, 1)
                dve.wait_ge(rel_copied, i + 1)
                for k in range(GROUP):
                    for j in b1_tiles(k):
                        tile_onehot(i * B1_TILES + j + LEAD, rel_now[:, j:j + 1], (j + LEAD) % OH_RING)
                    dve.wait_ge(kv_copied, i * GROUP + k + 1)
                    dve.wait_ge(k_maxed, i * GROUP + k + 1)
                    dve.tensor_tensor(k_max, k_max, kv_b[k % 2][:, 0:D], ALU.max).then_inc(k_maxed, 1)
                    for z in zones_ended(b1_tiles(k)):
                        add_zone(uses, i * 2, z, i * 2 + z)

            chain = Chain(k_chain, 0)
            for n in (0, 1):
                ins = dve.memset(v_b[n][:, :, P:P + 1], 1.0)
            chain.link(ins)
            dve.wait_ge(turn_filled, USE_KMAX_COL + 1)
            dve.tensor_reduce(k_col, turned3, AX.X, ALU.max).then_inc(turn_read, 1)
            dve.wait_ge(turn_read, USE_KMAX_COL + 1)
            for c in range(KC):
                chain.link(dve.tensor_scalar(halves(k_exp[0])[:, c, :], ones[:, :], k_col[:, c:c + 1], None, ALU.mult))
            dve.wait_ge(turn_filled, USE_KMAX_ROW + 1)
            dve.tensor_copy(k_max_row, turned[:, 0:D]).then_inc(turn_read, 1)
            dve.wait_ge(turn_read, USE_KMAX_ROW + 1)

            def shift_keys(b, half, parity, rows=P, first=False):
                dve.wait_ge(k_landed[parity], half * 32 + 32)
                if not first:
                    dve.wait_ge(context_summed, b - 1)
                dve.tensor_tensor(k_exp[parity][0:rows], k_b[parity][0:rows], k_max_row[0:rows],
                                  ALU.subtract).then_inc(k_shifted, 1)

            shift_keys(0, 0, 0, first=True)
            shift_keys(1, 0, 1, first=True)
            with dve.Fori(0, (BLOCKS - 1) // 8 - 1) as i:
                for k in range(2, 10):
                    shift_keys(i * 8 + k, i * 4 + k // 2, k % 2)
            for b in range(BLOCKS - 1 - 6, BLOCKS - 1):
                shift_keys(b, b // 2, b % 2)
            shift_keys(BLOCKS - 1, (BLOCKS - 1) // 2, 0, LAST_ROWS)
            dve.wait_ge(context_summed, BLOCKS)
            for c in range(KC):
                ins = dve.reciprocal(ctx_scale[:, c:c + 1], expert[c][:, P:P + 1])
            chain.link(ins)
            chain.link(dve.tensor_scalar(ctx_scale, ctx_scale, SCALE, None, ALU.mult))
            for c in range(KC):
                ins = dve.scalar_tensor_tensor(out=halves(ctx_sb)[:, c, :], in0=expert[c][:, 0:P],
                                               scalar=ctx_scale[:, c:c + 1], in1=head_mask,
                                               op0=ALU.mult, op1=ALU.mult)
            chain.link(ins)
            dve.wait_ge(turn_filled, USE_CONTEXT + 1)
            dve.tensor_copy(ctx_t, turned[:, 0:D]).then_inc(turn_read, 1)
            dve.wait_ge(mix_filled, 1)
            dve.tensor_copy(w_mix[:, :], proj[:, :]).then_inc(mix_ready, 1)
            dve.wait_ge(mix_ready, 1)

            def split_projection(b):
                chain = Chain(q_chain, b.n * Q_LINKS)
                dve.wait_ge(proj_filled, 2 * b.n + 1)
                dve.tensor_tensor(self_part, proj[:, 0:D], bias_row[:, :], ALU.add)
                chain.link(dve.tensor_reduce(q_max, by_head(proj[:, D:2 * D]), AX.X, ALU.max))
                dve.tensor_tensor(by_head(q_soft), by_head(proj[:, D:2 * D]),
                                  q_max.unsqueeze(2).to_broadcast([P, HEADS, DH]),
                                  ALU.subtract).then_inc(proj_read, 1)
                return chain

            def soften_q(b, chain):
                dve.wait_ge(q_exped, b.n + 1)
                chain.link(dve.tensor_reduce(q_sum, by_head(q_soft), AX.X, ALU.add))
                chain.link(dve.reciprocal(q_sum, q_sum))
                dve.tensor_tensor(by_head(q_soft), by_head(q_soft),
                                  q_sum.unsqueeze(2).to_broadcast([P, HEADS, DH]), ALU.mult).then_inc(q_ready, 1)

            def stage_sums(b):
                dve.wait_ge(zone_added, ZONES + 2 if isinstance(b.n, int) and b.n == BLOCKS - 1 else b.n * 2 + 5)
                if not b.first:
                    dve.wait_ge(proj_filled, b.n * 2)
                dve.tensor_copy(halves(gathered), sums3[:, :, bass.ds(b.n * P + ZONE_BACK, P)])
                dve.tensor_copy(deg4, zone_deg[:, bass.ds(b.n * 2, 4)]).then_inc(sums_staged, 1)

            def join(b, use):
                chain = Chain(head_chain, b.n * HEAD_LINKS)
                dve.wait_ge(turn_read, use + 1)
                chain.link(dve.tensor_tensor(inv_deg, q_turned[:, D:D + 1], far_deg[:, bass.ds(b.n, 1)], ALU.add))
                chain.link(dve.tensor_scalar(inv_deg, inv_deg, 1.0, None, ALU.max))
                chain.link(dve.reciprocal(inv_deg, inv_deg))
                dve.wait_ge(proj_filled, 2 * b.n + 2)
                dve.scalar_tensor_tensor(out=g_out, in0=proj[:, 0:D], scalar=inv_deg, in1=self_part,
                                         op0=ALU.mult, op1=ALU.add)
                chain.link(dve.bn_stats(st6, proj[:, D:2 * D]))
                stand_alone(dve, passed)
                chain.link(dve.bn_aggr(mv, st6))
                dve.scalar_tensor_tensor(out=mixed, in0=proj[:, D:2 * D], scalar=mv[:, 0:1], in1=gamma_row[:, :],
                                         op0=ALU.subtract, op1=ALU.mult).then_inc(proj_read, 1)
                chain.link(dve.tensor_scalar(g_out, g_out, 0.0, None, ALU.max))
                chain.link(dve.tensor_tensor_reduce(g_square, g_out, g_out, 1.0, 0.0, ALU.mult, ALU.add,
                                                    sq_var[:, 0:1]))
                chain.link(dve.tensor_scalar(sq_var[:, 1:2], mv[:, 1:2], LN_EPS, None, ALU.add))
                rsqrt(chain, sq_var, inv_norms, h2, small_i[:, 24:26])
                chain.link(dve.tensor_scalar(inv_norms[:, 0:1], inv_norms[:, 0:1], 1.0 / NORM_FLOOR, None, ALU.min))
                dve.wait_ge(xin_landed[b.par], b.half * 16 + 16)
                chain.link(dve.scalar_tensor_tensor(out=partly, in0=g_out, scalar=inv_norms[:, 0:1],
                                                    in1=x_in[b.par], op0=ALU.mult, op1=ALU.add))
                chain.link(dve.scalar_tensor_tensor(out=x_mid, in0=mixed, scalar=inv_norms[:, 1:2], in1=partly,
                                                    op0=ALU.mult, op1=ALU.add))
                chain.link(dve.bn_stats(st6b, x_mid))
                stand_alone(dve, passed)
                chain.link(dve.bn_aggr(mvb, st6b))
                chain.link(dve.tensor_scalar(var_b, mvb[:, 1:2], LN_EPS, None, ALU.add))
                rsqrt(chain, var_b, inv_b, h_b, small_i[:, 26:27])
                dve.tensor_scalar(tokens, x_mid, mvb[:, 0:1], inv_b, ALU.subtract, ALU.mult).then_inc(tokens_ready, 1)
                dve.wait_ge(tokens_ready, b.n + 1)
                dve.wait_ge(out_stored[b.par], b.half * 16 + 16)
                chain.link(dve.tensor_tensor(out_sb[b.par], x_mid, tokens, ALU.add))
                assert chain.links == HEAD_LINKS

            def pick(b, use):
                chain = Chain(route_chain, b.n * ROUTE_LINKS)
                dve.wait_ge(turn_filled, use + 1)
                dve.tensor_copy(logits, turned[:, 0:EXPERTS]).then_inc(turn_read, 1)
                dve.wait_ge(turn_read, use + 1)
                stand_alone(dve, passed)
                chain.link(dve.max(top8, logits))
                stand_alone(dve, passed)
                chain.link(dve.max_index(top_i, top8, logits))
                chain.link(dve.tensor_scalar(pick1, iota_e, top_i[:, 0:1], None, ALU.is_equal))
                chain.link(dve.scalar_tensor_tensor(out=rest, in0=pick1, scalar=-3.0e38, in1=logits,
                                                    op0=ALU.mult, op1=ALU.add))
                stand_alone(dve, passed)
                chain.link(dve.max(top8b, rest))
                dve.tensor_tensor(gap, top8[:, 0:1], top8b[:, 0:1], ALU.subtract).then_inc(gap_made, 1)
                chain.link(dve.max_index(top_ib, top8b, rest))
                chain.link(dve.tensor_scalar(pick2, iota_e, top_ib[:, 0:1], None, ALU.is_equal))
                return chain

            def weigh(b, chain):
                dve.wait_ge(tanh_made, b.n + 1)
                dve.tensor_scalar(route1, tanh_gap, 0.5, 0.5, ALU.mult, ALU.add)
                chain.link(dve.tensor_scalar(route2, tanh_gap, -0.5, 0.5, ALU.mult, ALU.add))
                chain.link(dve.tensor_scalar(comb_part, pick1, route1, None, ALU.mult))
                dve.scalar_tensor_tensor(out=combine[b.par], in0=pick2, scalar=route2, in1=comb_part,
                                         op0=ALU.mult, op1=ALU.add).then_inc(combine_made, 1)
                assert chain.links == ROUTE_LINKS
                dve.wait_ge(combine_made, b.n + 1)

            def add_expert(b, e):
                dve.wait_ge(expert_filled, b.n * EXPERTS + e + 3)
                dve.wait_ge(expert_added, b.n * EXPERTS + e + 2)
                dve.scalar_tensor_tensor(out=out_sb[b.par], in0=expert[e % 2][:, 0:D],
                                         scalar=combine[b.par][:, e:e + 1], in1=out_sb[b.par],
                                         op0=ALU.mult, op1=ALU.add).then_inc(expert_added, 1)

            def add_bias(b, use, e):
                dve.wait_ge(turn_filled, use + 1)
                dve.wait_ge(expert_added, b.n * EXPERTS + e + 2)
                dve.tensor_tensor(out_sb[b.par], turned[:, 0:D], out_sb[b.par], ALU.add).then_inc(turn_read, 1)
                dve.wait_ge(turn_read, use + 1)

            def period(b, nxt, m, e, tiles, uses, tile0, zone0, zone_expr, route_state):
                for j in tiles:
                    if not isinstance(tile0, int) or tile0 + j + LEAD < TILES:
                        tile_onehot(tile0 + j + LEAD, rel_now[:, j:j + 1], (j + LEAD) % OH_RING)
                if e == 0:
                    route_state["pick"] = pick(b, uses["logits", m])
                    if nxt:
                        route_state["q"] = split_projection(nxt)
                if e == 1:
                    weigh(b, route_state["pick"])
                    if nxt:
                        soften_q(nxt, route_state["q"])
                if e == 3:
                    if nxt:
                        stage_sums(nxt)
                    add_bias(b, uses["bias", m], 2)
                if e > 0:
                    add_expert(b, e - 1)
                if e == 5 and nxt:
                    join(nxt, uses["q", m + 1])
                for z in zones_ended(tiles):
                    add_zone(uses, zone0, z, zone_expr + z)
                if e == EXPERTS - 1:
                    add_expert(b, e)

            b0 = Block_(0, 0, 0)
            uses0 = Uses(BASE_HEAD0, HEAD0)
            q_state = split_projection(b0)
            soften_q(b0, q_state)
            stage_sums(b0)
            join(b0, uses0["q", 0])
            state = {}

            def copy_rel(tile0, tiles, made, copies):
                dve.wait_ge(onehot_made, made)
                dve.tensor_copy(rel_now[:, 0:tiles], rel[:, bass.ds(tile0 + LEAD, tiles)]).then_inc(rel_copied, 1)
                dve.wait_ge(rel_copied, copies)

            with dve.Fori(0, TURNS) as s:
                uses = Uses(s * USES_TURN + BASE_MAIN, main_order(TURN_STEPS, range(TURN_PERIODS)))
                tile0 = s * TURN_TILES + TURN_TILES
                zone0 = s * (TURN_TILES // ZONE_TILES) + TURN_TILES // ZONE_TILES
                copy_rel(tile0, TURN_TILES, tile0 + LEAD, s + GROUPS + 1)
                for k, tiles in enumerate(TURN_STEPS):
                    m, e = divmod(k, EXPERTS)
                    b, nxt = (block_at(s * TURN_PERIODS, s * (TURN_PERIODS // 2), n) for n in (m, m + 1))
                    period(b, nxt, m, e, tiles, uses, tile0, zone0, zone0, state)
            n = TURNS + 1
            first = TURNS * TURN_PERIODS
            copy_rel(n * TURN_TILES, TURN_TILES - LEAD, n * TURN_TILES + LEAD, GROUPS + TURNS + 1)
            for plan, start, base, order, heads in (
                    (LAST_STEPS, first, BASE_LAST, LAST_ORDER, LAST_PERIODS),
                    (TAIL_STEPS, TAIL_BLOCKS[0], BASE_TAIL, TAIL_ORDER, len(TAIL_BLOCKS) - 1)):
                for k, tiles in enumerate(plan):
                    m, e = divmod(k, EXPERTS)
                    b, nxt = (block_at(start, start // 2, i) for i in (m, m + 1))
                    zones = n * (TURN_TILES // ZONE_TILES)
                    period(b, nxt if m < heads else None, m, e, tiles, Uses(base, order), n * TURN_TILES,
                           zones, zones, state)


def constants():
    import numpy as np

    c = np.zeros((P, C_COLS), np.float32)
    c[np.arange(P), C_EYE + np.arange(P)] = 1.0
    c[:, C_IOTA:C_IOTA + P] = np.arange(P)
    c[:, C_MASK:C_MASK + P] = np.kron(np.eye(P // DH), np.ones((DH, DH)))
    return c


def kernel(x, src, dst, L0_gnn_W, L0_gnn_b, L0_mix_Wqkv, L0_mix_Wout, L0_mix_gamma, L0_ffn_router_w,
           L0_ffn_w1, L0_ffn_b1, L0_ffn_w2, L0_ffn_b2):
    import numpy as np

    import concourse.bacc as bacc
    from concourse.bass_utils import run_bass_kernel_spmd

    x = np.asarray(x)
    src, dst = np.asarray(src), np.asarray(dst)
    spare = TILES * P - EDGES

    def by_tile(edges, filler):
        filled = np.concatenate([edges, np.full(spare, filler, edges.dtype)])
        return np.ascontiguousarray(filled.reshape(TILES, P).T)

    arrays = {
        "x": np.concatenate([x, np.repeat(x[-1:], NODES_PAD - NODES, axis=0)]),
        "src": by_tile(src, 0),
        "dst": by_tile(dst, -1),
        "gnn_w": np.asarray(L0_gnn_W),
        "gnn_b": np.asarray(L0_gnn_b).reshape(1, D),
        "wqkv": np.asarray(L0_mix_Wqkv),
        "wout": np.asarray(L0_mix_Wout),
        "gamma": np.asarray(L0_mix_gamma).reshape(1, D),
        "router_wt": np.ascontiguousarray(np.asarray(L0_ffn_router_w).T),
        "w1": np.asarray(L0_ffn_w1),
        "b1t": np.ascontiguousarray(np.asarray(L0_ffn_b1).reshape(EXPERTS * KC, P).T),
        "w2": np.asarray(L0_ffn_w2),
        "b2": np.asarray(L0_ffn_b2),
        "consts": constants(),
    }
    nc = bacc.Bacc("TRN2", target_bir_lowering=False, num_devices=1)
    args = [nc.dram_tensor(name, a.shape, mybir.dt.from_np(a.dtype), kind="ExternalInput").ap()
            for name, a in arrays.items()]
    out = nc.dram_tensor("out", (NODES, D), F32, kind="ExternalOutput").ap()
    gps_kernel(nc, *args, out)
    result = run_bass_kernel_spmd(nc, [arrays], core_ids=[0])
    return result.results[0]["out"]
```

```python
from contextlib import ExitStack

import concourse.bass as bass
from concourse import mybir

F32 = mybir.dt.float32
F16 = mybir.dt.float16
I32 = mybir.dt.int32
U32 = mybir.dt.uint32
ALU = mybir.AluOpType
ACT = mybir.ActivationFunctionType
AX = mybir.AxisListType

P = 128
NODES = 6250
EDGES = 200000
D = 256
KC = D // P
HEADS = 8
DH = D // HEADS
EXPERTS = 8
LN_EPS = 1e-5
NORM_FLOOR = 1e-12
SCALE = DH ** -0.5
RSQRT_MAGIC = 0x5F3759DF

BLOCKS = -(-NODES // P)
LAST_ROWS = NODES - (BLOCKS - 1) * P
NODES_PAD = BLOCKS * P
EDGES_PER_NODE = EDGES // NODES
ZONE_TILES = 16
ZONE_NODES = ZONE_TILES * P // EDGES_PER_NODE
ZONE_BACK = (P - ZONE_NODES) // 2
TILES = BLOCKS * P * EDGES_PER_NODE // P
ZONES = TILES // ZONE_TILES
SUM_COLS = NODES_PAD + P

GROUP = 7
GROUPS = BLOCKS // GROUP
RING = 32
OH_RING = 16
GATHERS_PER_WAIT = 8
LEAD = 8

B1_TILES = 2 * ZONE_TILES
B2_BLOCKS, B2_TURNS = 24, 2
B2_TILES = 2 * ZONE_TILES
KV_BUFS = 4
MAIN_TILE = GROUPS * B1_TILES + B2_TURNS * B2_TILES
TURN_TILES = 14 * ZONE_TILES
TURN_PERIODS = 8
TURNS = 5
LAST_PERIODS = BLOCKS - TURNS * TURN_PERIODS
LAST_TILES = TILES - MAIN_TILE - TURNS * TURN_TILES
IDX_CHUNK = TURN_TILES // 4
assert BLOCKS == GROUP * GROUPS == B2_BLOCKS * B2_TURNS + 1 and B2_BLOCKS % KV_BUFS == 0
assert TILES % TURN_TILES == 0 and MAIN_TILE % RING == 0

C_EYE = P
C_IOTA = 384
C_MASK = 512
C_COLS = 640

WEIGHT_LOADS = 10
Q_LINKS, SPLIT_LINKS = 3, 1
HEAD_LINKS = 37
ROUTE_LINKS, PICK_LINKS = 9, 7


def b1_tiles(k):
    return range(k * B1_TILES // GROUP, (k + 1) * B1_TILES // GROUP)


def b2_tiles(k):
    return range(k * B2_TILES // B2_BLOCKS, (k + 1) * B2_TILES // B2_BLOCKS)


def steps(periods, tiles, rate):
    count = [min(tiles, int(rate * k)) for k in range(periods * EXPERTS)] + [tiles]
    return [(*divmod(k + 1, EXPERTS), range(count[k], count[k + 1])) for k in range(periods * EXPERTS)]


TURN_STEPS = steps(TURN_PERIODS, TURN_TILES, TURN_TILES / (TURN_PERIODS * EXPERTS))
LAST_STEPS = steps(LAST_PERIODS, LAST_TILES, 3.5)[:-1]


def zones_ended(tiles):
    return [j // ZONE_TILES for j in tiles if j % ZONE_TILES == ZONE_TILES - 1]


def b1_order():
    order = []
    for k in range(GROUP):
        order.append(("xn", k))
        order += [("zone", z) for z in zones_ended(b1_tiles(k))]
    return order


def b2_order():
    return [("zone", z) for k in range(B2_BLOCKS) for z in zones_ended(b2_tiles(k))]


def main_order(plan, heads):
    order = []
    for m, e, tiles in plan:
        if e == 0:
            order.append(("logits", m))
        if e == 2:
            order.append(("combine", m))
            if m in heads:
                order.append(("q", m + 1))
        if e == 3:
            order.append(("bias", m))
        if e == EXPERTS - 1 and m in heads:
            order.append(("tokens", m + 1))
        order += [("zone", z) for z in zones_ended(tiles)]
    return order


def stand_alone(engine, passed):
    engine.sem_inc(passed, 1)


class Uses:

    def __init__(self, base, order):
        self.base, self.at, self.count = base, {name: n for n, name in enumerate(order)}, len(order)

    def __getitem__(self, name):
        return self.base + self.at[name]


USES_B1 = len(b1_order())
USES_B2 = len(b2_order())
USES_TURN = len(main_order(TURN_STEPS, range(TURN_PERIODS)))
USE_FLAG = 0
BASE_B1 = 1
USE_KMAX_COL = BASE_B1 + GROUPS * USES_B1
USE_KMAX_ROW = USE_KMAX_COL + 1
BASE_B2 = USE_KMAX_COL + 2
USE_CONTEXT = BASE_B2 + B2_TURNS * USES_B2
BASE_HEAD0 = USE_CONTEXT + 1
HEAD0 = [("q", 0), ("tokens", 0), ("logits", 0)]
BASE_MAIN = BASE_HEAD0 + len(HEAD0)
BASE_LAST = BASE_MAIN + TURNS * USES_TURN
LAST_ORDER = main_order(LAST_STEPS, range(LAST_PERIODS - 1))


class Block_:

    def __init__(self, number, half, parity):
        self.n, self.half, self.par = number, half, parity
        self.first = isinstance(number, int) and number == 0


def block_at(first, first_half, m):
    return Block_(first + m, first_half + m // 2, m % 2)


def gps_kernel(nc, x, src, dst, gnn_w, gnn_b, wqkv, wout, gamma, router_wt, w1, b1t, w2, b2, consts, out):
    with ExitStack() as ctx:
        def sb(name, cols, dt=F32, rows=P):
            return ctx.enter_context(nc.sbuf_tensor("sb_" + name, [rows, cols], dt))

        def bank(name):
            return ctx.enter_context(nc.psum_tensor("ps_" + name, [P, 512], F32))

        def sem(name):
            return ctx.enter_context(nc.semaphore(name))

        table = nc.dram_tensor("xn_table", [NODES_PAD, 2 * D], F16, kind="Internal").ap()
        xnt_dram = nc.dram_tensor("xn_transposed", [BLOCKS * P, D], F32, kind="Internal").ap()
        kv_dram = nc.dram_tensor("keys_values", [NODES_PAD, 2 * D], F32, kind="Internal").ap()

        zone_sum = [bank("zone0"), bank("zone1")]
        turned = bank("turned")
        proj = bank("proj")
        hidden = [bank("hidden0"), bank("hidden1")]
        expert = [bank("expert0"), bank("expert1")]

        cst = sb("consts", C_COLS)
        eye = cst[:, C_EYE:C_EYE + P]
        head_mask = cst[:, C_MASK:C_MASK + P]
        iota_e = cst[:, C_IOTA:C_IOTA + EXPERTS]
        iota16 = sb("iota16", P, F16)
        ones = sb("ones", P)
        w_kv = sb("w_kv", KC * 2 * D)
        w_aq = sb("w_aq", KC * 2 * D)
        w_nb = sb("w_nb", KC * D)
        w_out = sb("w_out", KC * D)
        w_mix = sb("w_mix", KC * D)
        bias_row = sb("bias_row", D)
        gamma_row = sb("gamma_row", D)
        router = sb("router", KC * EXPERTS)
        b1_col = sb("b1_col", EXPERTS * KC)
        b2_row = sb("b2_row", D, rows=EXPERTS)
        ring = sb("ring", RING * (2 * D + 1), F16)
        onehot = sb("onehot", OH_RING * P, F16)
        idx = sb("idx", TILES, I32)
        idx_now = sb("idx_now", TURN_TILES, I32)
        rel = sb("rel", TILES)
        rel_now = sb("rel_now", TURN_TILES)
        far = sb("far", TILES)
        far_now = sb("far_now", ZONE_TILES)
        sums = sb("sums", KC * SUM_COLS)
        zone_deg = sb("zone_deg", ZONES + 3)
        far_deg = sb("far_deg", BLOCKS)
        zone_sb = [sb("zone_sb0", D + 1), sb("zone_sb1", D + 1)]
        zeros = sb("zeros", P + 1)
        small = sb("small", 256)
        small_i = sb("small_i", 32, I32)
        flag = sb("flag", 2, I32, rows=2)
        arena = sb("arena", BLOCKS * D)
        stage = sb("stage", GROUP * 2 * D)
        stats = [sb("stats0", 6 * GROUP), sb("stats1", 6 * GROUP)]

        ring3 = ring[:, :].rearrange("p (r c) -> p r c", r=RING)
        onehot3 = onehot[:, :].rearrange("p (r c) -> p r c", r=OH_RING)
        sums3 = sums[:, :].rearrange("p (k c) -> p k c", k=KC)
        w_kv3 = w_kv[:, :].rearrange("p (k c) -> p k c", k=KC)
        w_aq3 = w_aq[:, :].rearrange("p (k c) -> p k c", k=KC)
        w_nb3 = w_nb[:, :].rearrange("p (k c) -> p k c", k=KC)
        w_out3 = w_out[:, :].rearrange("p (k c) -> p k c", k=KC)
        w_mix3 = w_mix[:, :].rearrange("p (k c) -> p k c", k=KC)
        router3 = router[:, :].rearrange("p (k c) -> p k c", k=KC)
        turned3 = turned[:, 0:D].rearrange("p (k c) -> p k c", k=KC)

        xn_all = arena[:, :].rearrange("p (b d) -> p b d", d=D)
        WE = EXPERTS * KC * D
        w1_sb = arena[:, 0:WE].rearrange("p (e k h) -> p e k h", e=EXPERTS, k=KC)
        w2_sb = arena[:, WE:2 * WE].rearrange("p (e k h) -> p e k h", e=EXPERTS, k=KC)

        def buf(tensor, n, first=0):
            return tensor[:, first + n * D:first + (n + 1) * D]

        def halves(ap):
            return ap.rearrange("p (k c) -> p k c", k=KC)

        def by_head(ap):
            return ap.rearrange("p (h c) -> p h c", h=HEADS)

        late = 2 * WE
        xnt = [buf(arena, n, late) for n in (0, 1)]
        x_in = [buf(arena, n, late) for n in (2, 3)]
        out_sb = [buf(arena, n, late) for n in (4, 5)]
        self_part, q_soft, gathered = (buf(arena, n, late) for n in (6, 7, 8))
        g_out, g_square, mixed, partly, x_mid = (buf(arena, n, late) for n in (9, 10, 11, 12, 13))
        tokens = buf(arena, 14, late)
        tokens_t = [buf(arena, n, late) for n in (15, 16)]
        act_h = [buf(stage, 0), buf(stage, 1)]
        q_turned = stage[:, 2 * D:3 * D + 1]
        combine_t = stage[0:EXPERTS, 4 * D:4 * D + P]

        rows16 = stage[:, :].bitcast(F16).rearrange("p (b c) -> p b c", c=2 * D)

        def rows16_of(g):
            return rows16[:, g % 2 * GROUP:(g % 2 + 1) * GROUP, :]

        xn_b = buf(stage, 0)
        xnt_b = [buf(stage, 1), buf(stage, 2)]
        kv_b = [stage[:, 3 * D:5 * D], stage[:, 5 * D:7 * D]]
        k_max = buf(stage, 7)
        k_max_row = buf(stage, 8)
        k_max_wide = buf(stage, 9)
        ctx_sb = buf(stage, 10)
        ctx_t = buf(stage, 11)
        k_b = [buf(arena, n, late) for n in range(4, 4 + KV_BUFS)]
        v_first = late + (4 + KV_BUFS) * D
        v_b = [arena[:, v_first + n * (D + KC):v_first + (n + 1) * (D + KC)].rearrange("p (k c) -> p k c", k=KC)
               for n in range(KV_BUFS)]

        mean_var = small[:, 42:56].rearrange("p (b c) -> p b c", c=2)
        var_eps = small[:, 56:63]
        half_v = small[:, 63:70]
        rstd7 = [small[:, 216:223], small[:, 223:230]]
        shift7 = [small[:, 230:237], small[:, 237:244]]
        far_count = small[:, 84:85]
        k_col = small[:, 85:87]
        ctx_scale = small[:, 87:89]
        q_max = small[:, 89:97]
        q_sum = small[:, 97:105]
        deg4 = small[:, 105:109]
        inv_deg = small[:, 109:110]
        st6 = small[:, 110:116]
        mv = small[:, 116:118]
        sq_var = small[:, 118:120]
        inv_norms = small[:, 120:122]
        h2 = small[:, 122:124]
        st6b = small[:, 124:130]
        mvb = small[:, 130:132]
        var_b = small[:, 132:133]
        inv_b = small[:, 133:134]
        h_b = small[:, 134:135]
        logits = small[:, 136:144]
        top8 = small[:, 144:152]
        pick1 = small[:, 152:160]
        rest = small[:, 160:168]
        top8b = small[:, 168:176]
        pick2 = small[:, 176:184]
        gap = small[:, 184:185]
        tanh_gap = small[:, 185:186]
        route1 = small[:, 186:187]
        route2 = small[:, 187:188]
        combine = [small[:, 192:200], small[:, 200:208]]
        comb_part = small[:, 208:216]
        tile_i = small_i[:, 0:7]
        top_i = small_i[:, 8:16].bitcast(U32)
        top_ib = small_i[:, 16:24].bitcast(U32)

        const_landed, dst_landed, idx_landed = sem("const_landed"), sem("dst_landed"), sem("idx_landed")
        x_landed = [sem(f"x_landed{g}") for g in range(GROUPS)]
        weights_landed = sem("weights_landed")
        experts_landed = sem("experts_landed")
        passed = sem("passed")
        cleared, base_made, sums_cleared = sem("cleared"), sem("base_made"), sem("sums_cleared")
        stats_made = sem("stats_made")
        stat_chain, rstd_made = sem("stat_chain"), sem("rstd_made")
        xn_made, hi_made, lo_made = sem("xn_made"), sem("hi_made"), sem("lo_made")
        rows_stored = [sem("rows_stored0"), sem("rows_stored1")]
        far_chain, far_counted, flag_made = sem("far_chain"), sem("far_counted"), sem("flag_made")
        idx_copied = sem("idx_copied")
        landed = [sem(f"gather_landed{r}") for r in range(RING)]
        tiles_used = sem("tiles_used")
        onehot_made = sem("onehot_made")
        rel_copied = sem("rel_copied")
        zone_copied = sem("zone_copied")
        zone_added = sem("zone_added")
        turn_filled, turn_read = sem("turn_filled"), sem("turn_read")
        pre_idx, pre_landed = sem("pre_idx"), sem("pre_landed")
        pre_chain, pre_onehots, pre_summed = sem("pre_chain"), sem("pre_onehots"), sem("pre_summed")
        pre_copied, pre_turned, pre_added = sem("pre_copied"), sem("pre_turned"), sem("pre_added")
        xn_copied = sem("xn_copied")
        kv_filled, kv_copied = sem("kv_filled"), sem("kv_copied")
        xnt_stored = [sem("xnt_stored0"), sem("xnt_stored1")]
        kv_stored = [sem("kv_stored0"), sem("kv_stored1")]
        k_maxed = sem("k_maxed")
        k_chain = sem("k_chain")
        k_landed = [sem(f"k_landed{n}") for n in range(KV_BUFS)]
        k_shifted, k_exped, context_summed = sem("k_shifted"), sem("k_exped"), sem("context_summed")
        mix_filled, mix_ready = sem("mix_filled"), sem("mix_ready")
        xnt_landed = [sem("xnt_landed0"), sem("xnt_landed1")]
        xin_landed = [sem("xin_landed0"), sem("xin_landed1")]
        proj_filled, proj_read = sem("proj_filled"), sem("proj_read")
        q_chain, q_exped, q_ready = sem("q_chain"), sem("q_exped"), sem("q_ready")
        sums_staged = sem("sums_staged")
        head_chain = sem("head_chain")
        tokens_ready = sem("tokens_ready")
        route_chain, gap_made, tanh_made, combine_made = (
            sem("route_chain"), sem("gap_made"), sem("tanh_made"), sem("combine_made"))
        hidden_filled = sem("hidden_filled")
        hidden_act = sem("hidden_act")
        expert_filled = sem("expert_filled")
        expert_added = sem("expert_added")
        out_stored = [sem("out_stored0"), sem("out_stored1")]

        block = ctx.enter_context(nc.Block())

        def kv_uses(i, k):
            return (4 * i if k % 2 == 0 else 3 * i) + k // 2

        @block.sync
        def _(sp):
            for s in out_stored + kv_stored + xnt_stored:
                sp.sem_inc(s, 16)
            x_rows = x.rearrange("(b p) d -> p b d", p=P)
            for g in range(GROUPS):
                sp.dma_start(xn_all[:, g * GROUP:(g + 1) * GROUP, :],
                             x_rows[:, g * GROUP:(g + 1) * GROUP, :]).then_inc(x_landed[g], 16)
                if g == 0:
                    sp.dma_start(cst[:, :], consts).then_inc(const_landed, 16)
                    sp.dma_start(far[:, :].bitcast(I32), dst).then_inc(dst_landed, 16)
                    sp.dma_start(idx[:, :], src).then_inc(idx_landed, 16)
            loads = [
                (w_kv3, wqkv.rearrange("(k p) c -> p k c", p=P)[:, :, D:3 * D]),
                (w_aq3[:, :, 0:D], gnn_w[0:D].rearrange("(k p) c -> p k c", p=P)),
                (w_aq3[:, :, D:2 * D], wqkv.rearrange("(k p) c -> p k c", p=P)[:, :, 0:D]),
                (w_nb3, gnn_w[D:2 * D].rearrange("(k p) c -> p k c", p=P)),
                (w_out3, wout.rearrange("(k p) c -> p k c", p=P)),
                (bias_row[:, :], gnn_b.to_broadcast([P, D])),
                (gamma_row[:, :], gamma.to_broadcast([P, D])),
                (router3, router_wt.rearrange("(k p) c -> p k c", p=P)),
                (b1_col[:, :], b1t),
                (b2_row[:, :], b2),
            ]
            assert len(loads) == WEIGHT_LOADS
            table_rows = table.rearrange("(b p) c -> p b c", p=P)
            for g in range(GROUPS):
                sp.wait_ge(lo_made, g + 1)
                sp.dma_start(table_rows[:, g * GROUP:(g + 1) * GROUP, :],
                             rows16_of(g)).then_inc(rows_stored[g % 2], 16)
                if g == GROUPS // 2:
                    for to, of in loads:
                        sp.dma_start(to, of).then_inc(weights_landed, 16)
            with sp.Fori(0, GROUPS) as i:
                uses = Uses(i * USES_B1 + BASE_B1, b1_order())
                for k in range(GROUP):
                    sp.wait_ge(turn_read, uses["xn", k] + 1)
                    sp.dma_start(xnt_dram[bass.ds((i * GROUP + k) * P, P), :],
                                 xnt_b[k % 2]).then_inc(xnt_stored[k % 2], 16)
                    sp.wait_ge(kv_copied, i * GROUP + k + 1)
                    sp.dma_start(kv_dram[bass.ds((i * GROUP + k) * P, P), :],
                                 kv_b[k % 2]).then_inc(kv_stored[k % 2], 16)
            sp.wait_ge(turn_read, BASE_B1 + GROUPS * USES_B1)
            for n, uses_n in ((0, 4 * GROUPS), (1, 3 * GROUPS)):
                sp.wait_ge(kv_stored[n], 16 + 16 * uses_n)
                sp.wait_ge(xnt_stored[n], 16 + 16 * uses_n)

            def load_kv(b, n, rows=P):
                keys = kv_dram[bass.ds(b * P, rows), 0:D]
                values = kv_dram[bass.ds(b * P, rows), D:2 * D].rearrange("p (k c) -> p k c", k=KC)
                sp.dma_start(k_b[n][0:rows], keys).then_inc(k_landed[n], 16)
                sp.dma_start(v_b[n][0:rows, :, 0:P], values).then_inc(k_landed[n], 16)

            def load_block(b):
                sp.dma_start(xnt[b.par], xnt_dram[bass.ds(b.n * P, P), :]).then_inc(xnt_landed[b.par], 16)
                sp.dma_start(x_in[b.par], x[bass.ds(b.n * P, P), :]).then_inc(xin_landed[b.par], 16)

            for b in range(KV_BUFS):
                load_kv(b, b)
            load_block(Block_(0, 0, 0))
            load_block(Block_(1, 0, 1))
            with sp.Fori(0, B2_TURNS - 1) as i:
                for k in range(B2_BLOCKS):
                    sp.wait_ge(context_summed, i * B2_BLOCKS + k + 1)
                    load_kv(i * B2_BLOCKS + k + KV_BUFS, k % KV_BUFS)
            for b in range(BLOCKS - 1 - B2_BLOCKS, BLOCKS - KV_BUFS):
                sp.wait_ge(context_summed, b + 1)
                load_kv(b + KV_BUFS, b % KV_BUFS, LAST_ROWS if b + KV_BUFS == BLOCKS - 1 else P)

            def period(b, rows, load):
                if load:
                    sp.wait_ge(proj_filled, 2 * b.n + 1)
                    stand_alone(sp, passed)
                    sp.wait_ge(tokens_ready, b.n + 1)
                    load_block(Block_(b.n + 2, b.half + 1, b.par))
                sp.wait_ge(expert_added, (b.n + 1) * EXPERTS + 2)
                sp.dma_start(out[bass.ds(b.n * P, rows), :],
                             out_sb[b.par][0:rows]).then_inc(out_stored[b.par], 16)

            with sp.Fori(0, TURNS) as s:
                for m in range(TURN_PERIODS):
                    period(block_at(s * TURN_PERIODS, s * (TURN_PERIODS // 2), m), P, True)
            first = TURNS * TURN_PERIODS
            for m in range(LAST_PERIODS):
                b = block_at(first, first // 2, m)
                period(b, LAST_ROWS if b.n == BLOCKS - 1 else P, b.n + 2 < BLOCKS)
            for n in (0, 1):
                sp.wait_ge(out_stored[n], 16 + 16 * ((BLOCKS + 1 - n) // 2))

        @block.gpsimd
        def _(pool):
            pool.iota(rel[:, :].bitcast(I32), [[ZONE_NODES, ZONES], [0, ZONE_TILES]], base=-ZONE_BACK,
                      channel_multiplier=0).then_inc(base_made, 1)
            pool.memset(sums[:, :], 0.0).then_inc(sums_cleared, 1)
            for g in range(GROUPS):
                pool.wait_ge(hi_made, g + 1)
                rows = rows16_of(g)
                pool.tensor_tensor(rows[:, :, D:2 * D], xn_all[:, g * GROUP:(g + 1) * GROUP, :],
                                   rows[:, :, 0:D], ALU.subtract).then_inc(lo_made, 1)
            pool.wait_ge(idx_landed, 16)
            pool.wait_ge(cleared, 1)
            for n in (0, 1):
                pool.wait_ge(rows_stored[n], 16 * ((GROUPS + 1 - n) // 2))

            def gather(tile_idx, place, signal):
                pool.indirect_dma_start(ring3[:, place, 0:2 * D], None, table,
                                        bass.IndirectOffsetOnAxis(tile_idx, 0)).then_inc(signal, 16)

            pool.wait_ge(flag_made, 1)
            some_far = pool.value_load(flag[0:1, 0:1], min_val=0, max_val=EDGES)
            with pool.If(some_far > 0):
                with pool.Fori(0, ZONES) as z:
                    pool.wait_ge(pre_summed, z * BLOCKS + 1)
                    pool.tensor_copy(idx_now[:, 0:ZONE_TILES],
                                     idx[:, bass.ds(z * ZONE_TILES, ZONE_TILES)]).then_inc(pre_idx, 1)
                    pool.wait_ge(pre_idx, z + 1)
                    stand_alone(pool, passed)
                    for j in range(ZONE_TILES):
                        gather(idx_now[:, j:j + 1], j, pre_landed)
                pool.wait_ge(pre_summed, ZONES * BLOCKS + 1)
            with pool.Fori(0, TILES // TURN_TILES) as s:
                for j in range(TURN_TILES):
                    if j % IDX_CHUNK == 0:
                        pool.tensor_copy(idx_now[:, j:j + IDX_CHUNK],
                                         idx[:, bass.ds(s * TURN_TILES + j, IDX_CHUNK)]).then_inc(idx_copied, 1)
                        pool.wait_ge(idx_copied, s * (TURN_TILES // IDX_CHUNK) + j // IDX_CHUNK + 1)
                    if j % GATHERS_PER_WAIT == 0:
                        pool.wait_ge(tiles_used, s * TURN_TILES + j + GATHERS_PER_WAIT)
                        stand_alone(pool, passed)
                    gather(idx_now[:, j:j + 1], j % RING, landed[j % RING])

        @block.tensor
        def _(pe):
            pe.sem_inc(tiles_used, RING)
            pe.sem_inc(expert_filled, 2)
            pe.sem_inc(pre_summed, 1)

            def sum_tile(tile0, ring0, zone0, j):
                bank_ = zone_sum[(j // ZONE_TILES) % 2]
                oh = onehot3[:, j % OH_RING, :]
                rows = ring3[:, j % RING, :]
                first, last = j % ZONE_TILES == 0, j % ZONE_TILES == ZONE_TILES - 1
                if first:
                    pe.wait_ge(zone_copied, zone0 + j // ZONE_TILES + 1)
                pe.wait_ge(landed[j % RING], (ring0 + j // RING + 1) * 16)
                pe.wait_ge(onehot_made, tile0 + j + 1)
                pe.matmul(bank_[:, 0:D], oh, rows[:, 0:D], start=first, stop=False, skip_group_check=True)
                pe.matmul(bank_[:, 0:D + 1], oh, rows[:, D:2 * D + 1], start=False, stop=last,
                          skip_group_check=True).then_inc(tiles_used, 1)

            def turn(use, ins, width):
                pe.wait_ge(turn_read, use)
                for k in range(KC):
                    t = pe.transpose(turned[:, k * P:(k + 1) * P], ins[:, k * P:(k + 1) * P], eye)
                return t

            def turn_zone(uses, zone0, z):
                pe.wait_ge(zone_copied, zone0 + z + 3)
                turn(uses["zone", z], zone_sb[z % 2], D).then_inc(turn_filled, 1)

            pe.wait_ge(far_counted, 1)
            pe.matmul(turned[0:1, 0:1], far_count, ones[:, 0:1], start=True, stop=True).then_inc(turn_filled, 1)

            pe.wait_ge(flag_made, 1)
            some_far = pe.value_load(flag[0:1, 0:1], min_val=0, max_val=EDGES)
            with pe.If(some_far > 0):
                with pe.Fori(0, ZONES) as z:
                    pe.wait_ge(pre_landed, (z + 1) * (16 * ZONE_TILES))
                    stand_alone(pe, passed)
                    with pe.Fori(0, BLOCKS) as w:
                        n = z * BLOCKS + w
                        pe.wait_ge(pre_onehots, n + 1)
                        for j in range(ZONE_TILES):
                            oh, rows = onehot3[:, j, :], ring3[:, j, :]
                            pe.matmul(zone_sum[0][:, 0:D], oh, rows[:, 0:D], start=j == 0, stop=False,
                                      skip_group_check=True)
                            mm = pe.matmul(zone_sum[0][:, 0:D + 1], oh, rows[:, D:2 * D + 1], start=False,
                                           stop=j == ZONE_TILES - 1, skip_group_check=True)
                        mm.then_inc(pre_summed, 1)
                        pe.wait_ge(pre_copied, n + 1)
                        pe.wait_ge(pre_added, n + 1)
                        for k in range(KC):
                            t = pe.transpose(turned[:, k * P:(k + 1) * P], zone_sb[0][:, k * P:(k + 1) * P], eye)
                        t.then_inc(pre_turned, 1)
                pe.wait_ge(pre_added, ZONES * BLOCKS + 1)

            pe.wait_ge(weights_landed, 16 * WEIGHT_LOADS)
            with pe.Fori(0, GROUPS) as i:
                uses = Uses(i * USES_B1 + BASE_B1, b1_order())
                for k in range(GROUP):
                    pe.wait_ge(xn_copied, i * GROUP + k + 1)
                    turn(uses["xn", k], xn_b, D).then_inc(turn_filled, 1)
                    for j in b1_tiles(k):
                        sum_tile(i * B1_TILES, i, i * 2, j)
                    pe.wait_ge(turn_read, uses["xn", k] + 1)
                    if k > 0:
                        pe.wait_ge(kv_copied, i * GROUP + k)
                    for c in range(KC):
                        mm = pe.matmul(proj[:, :], halves(xnt_b[k % 2])[:, c, :], w_kv3[:, c, :],
                                       start=c == 0, stop=c == KC - 1)
                    mm.then_inc(kv_filled, 1)
                    for z in zones_ended(b1_tiles(k)):
                        turn_zone(uses, i * 2, z)
                    if k == GROUP - 1:
                        pe.wait_ge(kv_copied, i * GROUP + k + 1)

            pe.wait_ge(k_maxed, BLOCKS + 1)
            turn(USE_KMAX_COL, k_max, D).then_inc(turn_filled, 1)
            pe.wait_ge(k_chain, 3)
            turn(USE_KMAX_ROW, k_max_wide, D).then_inc(turn_filled, 1)

            pe.wait_ge(turn_read, USE_KMAX_ROW + 1)
            for c in range(KC):
                pe.matmul(expert[c][:, 0:P + 1], zeros[:, 0:P], zeros[:, :], start=True, stop=False,
                          skip_group_check=True)

            def add_context(b, n, rows=P, stop=False):
                pe.wait_ge(k_exped, b + 1)
                for c in range(KC):
                    mm = pe.matmul(expert[c][:, 0:P + 1], k_b[n][0:rows, c * P:(c + 1) * P],
                                   v_b[n][0:rows, c, :], start=False, stop=stop, skip_group_check=True)
                mm.then_inc(context_summed, 1)

            with pe.Fori(0, B2_TURNS) as i:
                uses = Uses(i * USES_B2 + BASE_B2, b2_order())
                tile0, zone0 = i * B2_TILES + GROUPS * B1_TILES, i * 2 + 2 * GROUPS
                for k in range(B2_BLOCKS):
                    for j in b2_tiles(k):
                        sum_tile(tile0, i + GROUPS, zone0, j)
                    add_context(i * B2_BLOCKS + k, k % KV_BUFS)
                    for z in zones_ended(b2_tiles(k)):
                        turn_zone(uses, zone0, z)
            add_context(BLOCKS - 1, 0, LAST_ROWS, True)
            pe.wait_ge(k_chain, 6)
            turn(USE_CONTEXT, ctx_sb, D).then_inc(turn_filled, 1)
            pe.wait_ge(turn_read, USE_CONTEXT + 1)
            for c in range(KC):
                mm = pe.matmul(proj[:, c * D:(c + 1) * D], halves(ctx_t)[:, c, :], w_out3[:, c, :],
                               start=True, stop=True, skip_group_check=True)
            mm.then_inc(mix_filled, 1)
            pe.wait_ge(mix_ready, 1)

            def project(b):
                pe.wait_ge(xnt_landed[b.par], b.half * 16 + 16)
                if not b.first:
                    pe.wait_ge(proj_read, 2 * b.n)
                for c in range(KC):
                    mm = pe.matmul(proj[:, :], halves(xnt[b.par])[:, c, :], w_aq3[:, c, :],
                                   start=c == 0, stop=c == KC - 1)
                mm.then_inc(proj_filled, 1)

            def turn_q(b, use):
                pe.wait_ge(q_ready, b.n + 1)
                pe.wait_ge(sums_staged, b.n + 1)
                turn(use, q_soft, D)
                for n in range(4):
                    move = (n - 1) * ZONE_NODES - ZONE_BACK
                    mm = pe.matmul(turned[:, D:D + 1], cst[:, P - move:2 * P - move], deg4[:, n:n + 1],
                                   start=n == 0, stop=n == 3, skip_group_check=True)
                mm.then_inc(turn_filled, 1)

            def mix(b, use):
                pe.wait_ge(turn_read, use + 1)
                pe.wait_ge(proj_read, 2 * b.n + 1)
                for c in range(KC):
                    pe.matmul(proj[:, 0:D], halves(gathered)[:, c, :], w_nb3[:, c, :],
                              start=c == 0, stop=c == KC - 1, skip_group_check=True)
                for c in range(KC):
                    mm = pe.matmul(proj[:, D:2 * D], halves(q_turned[:, 0:D])[:, c, :], w_mix3[:, c, :],
                                   start=c == 0, stop=c == KC - 1, skip_group_check=True)
                mm.then_inc(proj_filled, 1)

            def turn_tokens(b, use):
                pe.wait_ge(tokens_ready, b.n + 1)
                turn(use, tokens, D).then_inc(turn_filled, 1)

            def route(b, use):
                pe.wait_ge(turn_read, use)
                for c in range(KC):
                    mm = pe.matmul(turned[:, 0:EXPERTS], halves(tokens_t[b.par])[:, c, :], router3[:, c, :],
                                   start=c == 0, stop=c == KC - 1, skip_group_check=True)
                mm.then_inc(turn_filled, 1)

            def turn_combine(b, use):
                pe.wait_ge(turn_read, use)
                pe.wait_ge(combine_made, b.n + 1)
                pe.transpose(turned[0:EXPERTS, 0:P], combine[b.par], eye).then_inc(turn_filled, 1)

            def add_b2(b, use):
                pe.wait_ge(turn_read, use)
                pe.matmul(turned[:, 0:D], combine_t, b2_row[:, :], start=True, stop=True,
                          skip_group_check=True).then_inc(turn_filled, 1)

            def up(b, e):
                pe.wait_ge(hidden_act, b.n * EXPERTS + e + 1)
                for j in range(KC):
                    for c in range(KC):
                        mm = pe.matmul(hidden[e % 2][:, j * P:(j + 1) * P],
                                       w1_sb[:, e, c, j * P:(j + 1) * P], halves(tokens_t[b.par])[:, c, :],
                                       start=c == 0, stop=c == KC - 1, skip_group_check=True)
                mm.then_inc(hidden_filled, 1)

            def down(n, e):
                pe.wait_ge(hidden_act, n + 3)
                pe.wait_ge(expert_added, n + 1)
                for c in range(KC):
                    mm = pe.matmul(expert[e % 2][:, 0:D], halves(act_h[e % 2])[:, c, :], w2_sb[:, e, c, :],
                                   start=c == 0, stop=c == KC - 1, skip_group_check=True)
                mm.then_inc(expert_filled, 1)

            def step(b, nxt, m, e, tiles, uses, tile0, ring0, zone0):
                for j in tiles:
                    sum_tile(tile0, ring0, zone0, j)
                if e == 0:
                    pe.wait_ge(turn_read, uses["logits", m])
                    route(b, uses["logits", m])
                if e == 2:
                    turn_combine(b, uses["combine", m])
                if e == 3:
                    add_b2(b, uses["bias", m])
                up(b, e)
                if nxt:
                    if e == 0:
                        project(nxt)
                    if e == 2:
                        turn_q(nxt, uses["q", m + 1])
                    if e == 3:
                        mix(nxt, uses["q", m + 1])
                    if e == EXPERTS - 1:
                        turn_tokens(nxt, uses["tokens", m + 1])
                if e > 0 or not b.first:
                    down(b.n * EXPERTS + e - 1, (e - 1) % EXPERTS)
                for z in zones_ended(tiles):
                    turn_zone(uses, zone0, z)

            b0, b1 = Block_(0, 0, 0), Block_(1, 0, 1)
            uses0 = Uses(BASE_HEAD0, HEAD0)
            project(b0)
            turn_q(b0, uses0["q", 0])
            mix(b0, uses0["q", 0])
            turn_tokens(b0, uses0["tokens", 0])
            pe.wait_ge(experts_landed, 32)
            step(b0, b1, 0, 0, range(0), uses0, 0, 0, 0)
            with pe.Fori(0, TURNS) as s:
                uses = Uses(s * USES_TURN + BASE_MAIN, main_order(TURN_STEPS, range(TURN_PERIODS + 1)))
                for m, e, tiles in TURN_STEPS:
                    b, nxt = (block_at(s * TURN_PERIODS, s * (TURN_PERIODS // 2), n) for n in (m, m + 1))
                    step(b, nxt, m, e, tiles, uses, s * TURN_TILES + MAIN_TILE,
                         s * (TURN_TILES // RING) + MAIN_TILE // RING,
                         s * (TURN_TILES // ZONE_TILES) + MAIN_TILE // ZONE_TILES)
            first, tile0 = TURNS * TURN_PERIODS, TILES - LAST_TILES
            for m, e, tiles in LAST_STEPS:
                b, nxt = (block_at(first, first // 2, n) for n in (m, m + 1))
                step(b, nxt if nxt.n < BLOCKS else None, m, e, tiles, Uses(BASE_LAST, LAST_ORDER), tile0,
                     tile0 // RING, tile0 // ZONE_TILES)
            down(BLOCKS * EXPERTS - 1, EXPERTS - 1)

        @block.scalar
        def _(act):
            act.sem_inc(zone_copied, 2)
            act.sem_inc(hidden_act, 2)
            for g in range(GROUPS):
                act.wait_ge(rstd_made, g + 1)
                for b in range(GROUP):
                    xb = xn_all[:, g * GROUP + b, :]
                    ins = act.activation(xb, xb, ACT.Identity, bias=shift7[g % 2][:, b:b + 1],
                                         scale=rstd7[g % 2][:, b:b + 1])
                ins.then_inc(xn_made, 1)
                act.wait_ge(xn_made, g + 1)
                if g >= 2:
                    act.wait_ge(rows_stored[g % 2], 16 * (g // 2))
                act.activation(rows16_of(g)[:, :, 0:D], xn_all[:, g * GROUP:(g + 1) * GROUP, :],
                               ACT.Copy).then_inc(hi_made, 1)

            act.wait_ge(flag_made, 1)
            some_far = act.value_load(flag[0:1, 0:1], min_val=0, max_val=EDGES)
            with act.If(some_far > 0):
                with act.Fori(0, ZONES * BLOCKS) as n:
                    act.wait_ge(pre_summed, n + 2)
                    act.wait_ge(pre_added, n + 1)
                    act.activation(zone_sb[0][:, :], zone_sum[0][:, 0:D + 1], ACT.Copy).then_inc(pre_copied, 1)
                act.wait_ge(pre_added, ZONES * BLOCKS + 1)

            def copy_zone(tile0, zone0, z):
                act.wait_ge(tiles_used, tile0 + (z + 1) * ZONE_TILES + RING)
                act.wait_ge(zone_added, zone0 + z + 1)
                act.activation(zone_sb[z % 2][:, :], zone_sum[z % 2][:, 0:D + 1],
                               ACT.Copy).then_inc(zone_copied, 1)

            for n in (0, 1):
                act.wait_ge(rows_stored[n], 16 * ((GROUPS + 1 - n) // 2))
            with act.Fori(0, GROUPS) as i:
                uses = Uses(i * USES_B1 + BASE_B1, b1_order())
                for k in range(GROUP):
                    act.wait_ge(turn_filled, uses["xn", k - 1] + 1 if k else i * USES_B1 + BASE_B1)
                    act.activation(xn_b, xn_all[:, bass.ds(i * GROUP + k, 1), :].rearrange("p b d -> p (b d)"),
                                   ACT.Copy).then_inc(xn_copied, 1)
                    act.wait_ge(turn_filled, uses["xn", k] + 1)
                    act.wait_ge(xnt_stored[k % 2], kv_uses(i, k) * 16 + 16)
                    act.activation(xnt_b[k % 2], turned[:, 0:D], ACT.Copy).then_inc(turn_read, 1)
                    for z in zones_ended(b1_tiles(k)):
                        copy_zone(i * B1_TILES, i * 2, z)
                    act.wait_ge(kv_filled, i * GROUP + k + 1)
                    act.wait_ge(kv_stored[k % 2], kv_uses(i, k) * 16 + 16)
                    act.wait_ge(k_maxed, i * GROUP + k + 1)
                    act.activation(kv_b[k % 2], proj[:, :], ACT.Copy).then_inc(kv_copied, 1)

            act.wait_ge(xn_copied, BLOCKS)
            for to, of in ((w1_sb, w1), (w2_sb, w2)):
                act.dma_start(to, of.rearrange("e (k p) h -> p e k h", p=P)).then_inc(experts_landed, 16)

            def exp_keys(b, n, rows=P):
                act.wait_ge(k_shifted, b + 1)
                act.activation(k_b[n][0:rows], k_b[n][0:rows], ACT.Exp).then_inc(k_exped, 1)

            with act.Fori(0, B2_TURNS) as i:
                for k in range(B2_BLOCKS):
                    exp_keys(i * B2_BLOCKS + k, k % KV_BUFS)
                    for z in zones_ended(b2_tiles(k)):
                        copy_zone(i * B2_TILES + GROUPS * B1_TILES, i * 2 + 2 * GROUPS, z)
            exp_keys(BLOCKS - 1, 0, LAST_ROWS)
            act.wait_ge(mix_ready, 1)

            def exp_q(b):
                act.wait_ge(proj_read, 2 * b.n + 1)
                act.activation(q_soft, q_soft, ACT.Exp).then_inc(q_exped, 1)

            def copy_q(b, use):
                act.wait_ge(turn_filled, use + 1)
                act.activation(q_turned, turned[:, 0:D + 1], ACT.Copy).then_inc(turn_read, 1)

            def copy_tokens(b, use):
                act.wait_ge(turn_filled, use + 1)
                act.activation(tokens_t[b.par], turned[:, 0:D], ACT.Copy).then_inc(turn_read, 1)

            def gelu(b, e):
                act.wait_ge(hidden_filled, b.n * EXPERTS + e + 1)
                act.wait_ge(expert_filled, b.n * EXPERTS + e + 1)
                for j in range(KC):
                    ins = act.activation(halves(act_h[e % 2])[:, j, :], hidden[e % 2][:, j * P:(j + 1) * P],
                                         ACT.Gelu, bias=b1_col[:, e * KC + j:e * KC + j + 1])
                ins.then_inc(hidden_act, 1)

            def step(b, nxt, m, e, tiles, uses, tile0, zone0):
                for z in zones_ended(tiles):
                    copy_zone(tile0, zone0, z)
                if e == 2:
                    act.wait_ge(turn_filled, uses["combine", m] + 1)
                    act.activation(combine_t, turned[0:EXPERTS, 0:P], ACT.Copy).then_inc(turn_read, 1)
                gelu(b, e)
                if e == 0:
                    act.wait_ge(gap_made, b.n + 1)
                    act.activation(tanh_gap, gap, ACT.Tanh, scale=0.5).then_inc(tanh_made, 1)
                if nxt:
                    if e == 0:
                        exp_q(nxt)
                    if e == 2:
                        copy_q(nxt, uses["q", m + 1])
                    if e == EXPERTS - 1:
                        copy_tokens(nxt, uses["tokens", m + 1])

            b0, b1 = Block_(0, 0, 0), Block_(1, 0, 1)
            uses0 = Uses(BASE_HEAD0, HEAD0)
            exp_q(b0)
            copy_q(b0, uses0["q", 0])
            copy_tokens(b0, uses0["tokens", 0])
            step(b0, b1, 0, 0, range(0), uses0, 0, 0)
            with act.Fori(0, TURNS) as s:
                uses = Uses(s * USES_TURN + BASE_MAIN, main_order(TURN_STEPS, range(TURN_PERIODS + 1)))
                for m, e, tiles in TURN_STEPS:
                    b, nxt = (block_at(s * TURN_PERIODS, s * (TURN_PERIODS // 2), n) for n in (m, m + 1))
                    step(b, nxt, m, e, tiles, uses, s * TURN_TILES + MAIN_TILE,
                         s * (TURN_TILES // ZONE_TILES) + MAIN_TILE // ZONE_TILES)
            first, tile0 = TURNS * TURN_PERIODS, TILES - LAST_TILES
            for m, e, tiles in LAST_STEPS:
                b, nxt = (block_at(first, first // 2, n) for n in (m, m + 1))
                step(b, nxt if nxt.n < BLOCKS else None, m, e, tiles, Uses(BASE_LAST, LAST_ORDER), tile0,
                     tile0 // ZONE_TILES)

        @block.vector
        def _(dve):
            dve.sem_inc(zone_added, 2)
            dve.sem_inc(expert_added, 2)
            dve.sem_inc(pre_added, 1)

            class Chain:

                def __init__(self, done, before, links=0):
                    self.done, self.before, self.links = done, before, links

                def link(self, ins, meanwhile=None):
                    self.links += 1
                    ins.then_inc(self.done, 1)
                    if meanwhile:
                        next(meanwhile, None)
                    dve.wait_ge(self.done, self.before + self.links)

            def rsqrt(chain, v, y, h, bits, meanwhile=None):
                chain.link(dve.tensor_scalar(bits, v.bitcast(I32), 1, None, ALU.logical_shift_right), meanwhile)
                chain.link(dve.tensor_scalar(y.bitcast(I32), bits, -1.0, float(RSQRT_MAGIC), ALU.mult, ALU.add),
                           meanwhile)
                for _ in range(3):
                    chain.link(dve.tensor_tensor(h, v, y, ALU.mult), meanwhile)
                    chain.link(dve.scalar_tensor_tensor(out=h, in0=h, scalar=-0.5, in1=y, op0=ALU.mult,
                                                        op1=ALU.mult), meanwhile)
                    chain.link(dve.scalar_tensor_tensor(out=y, in0=h, scalar=1.5, in1=y, op0=ALU.add,
                                                        op1=ALU.mult), meanwhile)

            dve.memset(ones[:, :], 1.0)
            dve.memset(zeros[:, :], 0.0)
            dve.memset(zone_deg[:, :], 0.0)
            dve.memset(far_deg[:, :], 0.0)

            def take_stats(g):
                dve.wait_ge(x_landed[g], 16)
                for b in range(GROUP):
                    ins = dve.bn_stats(stats[g % 2][:, 6 * b:6 * b + 6], xn_all[:, g * GROUP + b, :])
                    if b == GROUP - 1:
                        ins.then_inc(stats_made, 1)
                    yield

            dst_f, inside, tmp = (ring[:, :].bitcast(F32)[:, n * TILES:(n + 1) * TILES] for n in (0, 1, 2))

            def place_edges():
                dve.wait_ge(dst_landed, 16)
                dve.tensor_copy(dst_f, far[:, :].bitcast(I32)).then_inc(far_chain, 1)
                yield
                dve.wait_ge(far_chain, 1)
                dve.wait_ge(base_made, 1)
                dve.tensor_tensor(rel[:, :], dst_f, rel[:, :].bitcast(I32), ALU.subtract).then_inc(far_chain, 1)
                yield
                dve.wait_ge(far_chain, 2)
                dve.tensor_scalar(tmp, rel[:, :], 0.0, None, ALU.is_ge).then_inc(far_chain, 1)
                yield
                dve.wait_ge(far_chain, 3)
                dve.scalar_tensor_tensor(out=inside, in0=rel[:, :], scalar=float(P - 1), in1=tmp,
                                         op0=ALU.is_le, op1=ALU.mult).then_inc(far_chain, 1)
                yield
                dve.wait_ge(far_chain, 4)
                dve.scalar_tensor_tensor(out=tmp, in0=dst_f, scalar=0.0, in1=inside,
                                         op0=ALU.is_ge, op1=ALU.subtract).then_inc(far_chain, 1)
                yield
                dve.wait_ge(far_chain, 5)
                dve.scalar_tensor_tensor(out=far[:, :], in0=dst_f, scalar=1.0, in1=tmp,
                                         op0=ALU.add, op1=ALU.mult).then_inc(far_chain, 1)
                yield
                dve.tensor_reduce(far_count, tmp, AX.X, ALU.add).then_inc(far_counted, 1)
                yield

            def beside(g, edges):
                if g + 1 < GROUPS:
                    yield from take_stats(g + 1)
                next(edges, None)
                yield

            chain = Chain(stat_chain, 0)
            edges = place_edges()
            for _ in take_stats(0):
                pass
            for g in range(GROUPS):
                meanwhile = beside(g, edges)
                dve.wait_ge(stats_made, g + 1)
                if g >= 1:
                    dve.wait_ge(rstd_made, g)
                if g >= 2:
                    dve.wait_ge(xn_made, g - 1)
                for b in range(GROUP):
                    ins = dve.bn_aggr(mean_var[:, b, :], stats[g % 2][:, 6 * b:6 * b + 6])
                chain.link(ins, meanwhile)
                chain.link(dve.tensor_scalar(var_eps, mean_var[:, :, 1], LN_EPS, None, ALU.add), meanwhile)
                rsqrt(chain, var_eps, rstd7[g % 2], half_v, tile_i, meanwhile)
                dve.scalar_tensor_tensor(out=shift7[g % 2], in0=mean_var[:, :, 0], scalar=-1.0, in1=rstd7[g % 2],
                                         op0=ALU.mult, op1=ALU.mult).then_inc(rstd_made, 1)
                for _ in meanwhile:
                    pass
            for _ in edges:
                pass
            dve.wait_ge(const_landed, 16)
            dve.tensor_copy(iota16[:, :], cst[:, C_IOTA:C_IOTA + P]).then_inc(far_chain, 1)
            dve.wait_ge(far_counted, 1)
            dve.memset(ring3[:, :, 2 * D:2 * D + 1], 1.0).then_inc(cleared, 1)
            dve.wait_ge(turn_filled, USE_FLAG + 1)
            dve.tensor_copy(small[0:1, 244:245], turned[0:1, 0:1]).then_inc(turn_read, 1)
            dve.wait_ge(turn_read, USE_FLAG + 1)
            dve.tensor_copy(flag[0:1, 0:1], small[0:1, 244:245]).then_inc(flag_made, 1)
            dve.wait_ge(flag_made, 1)
            dve.wait_ge(sums_cleared, 1)
            dve.wait_ge(far_chain, 7)

            def make_onehot(place, rel_col):
                return dve.tensor_scalar(onehot3[:, place, :], iota16[:, :], rel_col, None, ALU.is_equal)

            some_far = dve.value_load(flag[0:1, 0:1], min_val=0, max_val=EDGES)
            with dve.If(some_far > 0):
                with dve.Fori(0, ZONES) as z:
                    dve.tensor_scalar(far_now[:, :], far[:, bass.ds(z * ZONE_TILES, ZONE_TILES)], -1.0, None,
                                      ALU.add).then_inc(pre_chain, 1)
                    with dve.Fori(0, BLOCKS) as w:
                        n = z * BLOCKS + w
                        dve.wait_ge(pre_chain, n + z + 1)
                        dve.wait_ge(pre_summed, n + 1)
                        for j in range(ZONE_TILES):
                            ins = make_onehot(j, far_now[:, j:j + 1])
                        ins.then_inc(pre_onehots, 1)
                        dve.wait_ge(pre_onehots, n + 1)
                        dve.tensor_scalar(far_now[:, :], far_now[:, :], -float(P), None,
                                          ALU.add).then_inc(pre_chain, 1)
                        dve.wait_ge(pre_turned, n + 1)
                        window = sums3[:, :, bass.ds(w * P + ZONE_BACK, P)]
                        dve.tensor_tensor(window, turned3, window, ALU.add)
                        dve.tensor_tensor(far_deg[:, bass.ds(w, 1)], zone_sb[0][:, D:D + 1],
                                          far_deg[:, bass.ds(w, 1)], ALU.add).then_inc(pre_added, 1)
                        dve.wait_ge(pre_added, n + 2)
                    dve.wait_ge(pre_chain, z * (BLOCKS + 1) + BLOCKS + 1)

            def tile_onehot(tile, rel_col, place):
                dve.wait_ge(tiles_used, tile + RING - OH_RING + 1)
                make_onehot(place, rel_col).then_inc(onehot_made, 1)

            def add_zone(uses, zone0, z, zone_expr):
                dve.wait_ge(turn_filled, uses["zone", z] + 1)
                dve.wait_ge(zone_added, zone0 + z + 2)
                window = sums3[:, :, bass.ds(zone_expr * ZONE_NODES, P)]
                dve.tensor_tensor(window, turned3, window, ALU.add).then_inc(turn_read, 1)
                dve.tensor_copy(zone_deg[:, bass.ds(zone_expr + 1, 1)],
                                zone_sb[z % 2][:, D:D + 1]).then_inc(zone_added, 1)

            def copy_rel(tile0, tiles, copies):
                dve.wait_ge(onehot_made, tile0 + LEAD)
                dve.tensor_copy(rel_now[:, 0:tiles], rel[:, bass.ds(tile0 + LEAD, tiles)]).then_inc(rel_copied, 1)
                dve.wait_ge(rel_copied, copies)

            for t in range(LEAD):
                tile_onehot(t, rel[:, t:t + 1], t)
            for n in (0, 1):
                dve.wait_ge(rows_stored[n], 16 * ((GROUPS + 1 - n) // 2))
            dve.memset(k_max, -3.0e38).then_inc(k_maxed, 1)
            with dve.Fori(0, GROUPS) as i:
                uses = Uses(i * USES_B1 + BASE_B1, b1_order())
                copy_rel(i * B1_TILES, B1_TILES, i + 1)
                for k in range(GROUP):
                    for j in b1_tiles(k):
                        tile_onehot(i * B1_TILES + j + LEAD, rel_now[:, j:j + 1], (j + LEAD) % OH_RING)
                    dve.wait_ge(kv_copied, i * GROUP + k + 1)
                    dve.wait_ge(k_maxed, i * GROUP + k + 1)
                    dve.tensor_tensor(k_max, k_max, kv_b[k % 2][:, 0:D], ALU.max).then_inc(k_maxed, 1)
                    for z in zones_ended(b1_tiles(k)):
                        add_zone(uses, i * 2, z, i * 2 + z)

            chain = Chain(k_chain, 0)
            dve.wait_ge(xn_copied, BLOCKS)
            for n in range(KV_BUFS):
                ins = dve.memset(v_b[n][:, :, P:P + 1], 1.0)
            chain.link(ins)
            dve.wait_ge(turn_filled, USE_KMAX_COL + 1)
            dve.tensor_reduce(k_col, turned3, AX.X, ALU.max).then_inc(turn_read, 1)
            dve.wait_ge(turn_read, USE_KMAX_COL + 1)
            for c in range(KC):
                chain.link(dve.tensor_scalar(halves(k_max_wide)[:, c, :], ones[:, :], k_col[:, c:c + 1], None,
                                             ALU.mult))
            dve.wait_ge(turn_filled, USE_KMAX_ROW + 1)
            dve.tensor_copy(k_max_row, turned[:, 0:D]).then_inc(turn_read, 1)
            dve.wait_ge(turn_read, USE_KMAX_ROW + 1)

            def shift_keys(b, uses_before, n, rows=P):
                dve.wait_ge(k_landed[n], uses_before * 32 + 32)
                dve.tensor_tensor(k_b[n][0:rows], k_b[n][0:rows], k_max_row[0:rows],
                                  ALU.subtract).then_inc(k_shifted, 1)

            with dve.Fori(0, B2_TURNS) as i:
                uses = Uses(i * USES_B2 + BASE_B2, b2_order())
                tile0, zone0 = i * B2_TILES + GROUPS * B1_TILES, i * 2 + 2 * GROUPS
                copy_rel(tile0, B2_TILES, i + GROUPS + 1)
                for k in range(B2_BLOCKS):
                    shift_keys(i * B2_BLOCKS + k, i * (B2_BLOCKS // KV_BUFS) + k // KV_BUFS, k % KV_BUFS)
                    for j in b2_tiles(k):
                        tile_onehot(tile0 + j + LEAD, rel_now[:, j:j + 1], (j + LEAD) % OH_RING)
                    for z in zones_ended(b2_tiles(k)):
                        add_zone(uses, zone0, z, zone0 + z)
            shift_keys(BLOCKS - 1, (BLOCKS - 1) // KV_BUFS, 0, LAST_ROWS)
            dve.wait_ge(context_summed, BLOCKS)
            for c in range(KC):
                ins = dve.reciprocal(ctx_scale[:, c:c + 1], expert[c][:, P:P + 1])
            chain.link(ins)
            chain.link(dve.tensor_scalar(ctx_scale, ctx_scale, SCALE, None, ALU.mult))
            for c in range(KC):
                ins = dve.scalar_tensor_tensor(out=halves(ctx_sb)[:, c, :], in0=expert[c][:, 0:P],
                                               scalar=ctx_scale[:, c:c + 1], in1=head_mask,
                                               op0=ALU.mult, op1=ALU.mult)
            chain.link(ins)
            dve.wait_ge(turn_filled, USE_CONTEXT + 1)
            dve.tensor_copy(ctx_t, turned[:, 0:D]).then_inc(turn_read, 1)
            dve.wait_ge(mix_filled, 1)
            dve.tensor_copy(w_mix[:, :], proj[:, :]).then_inc(mix_ready, 1)
            dve.wait_ge(mix_ready, 1)

            def split_projection(b):
                chain = Chain(q_chain, b.n * Q_LINKS)
                dve.wait_ge(proj_filled, 2 * b.n + 1)
                dve.tensor_tensor(self_part, proj[:, 0:D], bias_row[:, :], ALU.add)
                chain.link(dve.tensor_reduce(q_max, by_head(proj[:, D:2 * D]), AX.X, ALU.max))
                dve.tensor_tensor(by_head(q_soft), by_head(proj[:, D:2 * D]),
                                  q_max.unsqueeze(2).to_broadcast([P, HEADS, DH]),
                                  ALU.subtract).then_inc(proj_read, 1)
                assert chain.links == SPLIT_LINKS

            def soften_q(b):
                chain = Chain(q_chain, b.n * Q_LINKS, SPLIT_LINKS)
                dve.wait_ge(q_exped, b.n + 1)
                chain.link(dve.tensor_reduce(q_sum, by_head(q_soft), AX.X, ALU.add))
                chain.link(dve.reciprocal(q_sum, q_sum))
                dve.tensor_tensor(by_head(q_soft), by_head(q_soft),
                                  q_sum.unsqueeze(2).to_broadcast([P, HEADS, DH]), ALU.mult).then_inc(q_ready, 1)

            def stage_sums(b):
                dve.wait_ge(zone_added, ZONES + 2 if isinstance(b.n, int) and b.n == BLOCKS - 1 else b.n * 2 + 5)
                if not b.first:
                    dve.wait_ge(proj_filled, b.n * 2)
                dve.tensor_copy(halves(gathered), sums3[:, :, bass.ds(b.n * P + ZONE_BACK, P)])
                dve.tensor_copy(deg4, zone_deg[:, bass.ds(b.n * 2, 4)]).then_inc(sums_staged, 1)

            def invert_degrees(b, use, meanwhile=None):
                chain = Chain(head_chain, b.n * HEAD_LINKS)
                dve.wait_ge(turn_read, use + 1)
                chain.link(dve.tensor_tensor(inv_deg, q_turned[:, D:D + 1], far_deg[:, bass.ds(b.n, 1)], ALU.add),
                           meanwhile)
                chain.link(dve.tensor_scalar(inv_deg, inv_deg, 1.0, None, ALU.max), meanwhile)
                chain.link(dve.reciprocal(inv_deg, inv_deg), meanwhile)
                return chain

            def take_parts(b, chain, meanwhile=None):
                dve.wait_ge(proj_filled, 2 * b.n + 2)
                dve.scalar_tensor_tensor(out=g_out, in0=proj[:, 0:D], scalar=inv_deg, in1=self_part,
                                         op0=ALU.mult, op1=ALU.add)
                chain.link(dve.bn_stats(st6, proj[:, D:2 * D]), meanwhile)
                stand_alone(dve, passed)
                chain.link(dve.bn_aggr(mv, st6), meanwhile)
                dve.scalar_tensor_tensor(out=mixed, in0=proj[:, D:2 * D], scalar=mv[:, 0:1], in1=gamma_row[:, :],
                                         op0=ALU.subtract, op1=ALU.mult).then_inc(proj_read, 1)
                chain.link(dve.tensor_scalar(g_out, g_out, 0.0, None, ALU.max), meanwhile)
                chain.link(dve.tensor_tensor_reduce(g_square, g_out, g_out, 1.0, 0.0, ALU.mult, ALU.add,
                                                    sq_var[:, 0:1]), meanwhile)
                chain.link(dve.tensor_scalar(sq_var[:, 1:2], mv[:, 1:2], LN_EPS, None, ALU.add), meanwhile)

            def join_parts(b, chain, meanwhile=None):
                rsqrt(chain, sq_var, inv_norms, h2, small_i[:, 24:26], meanwhile)
                chain.link(dve.tensor_scalar(inv_norms[:, 0:1], inv_norms[:, 0:1], 1.0 / NORM_FLOOR, None, ALU.min),
                           meanwhile)
                dve.wait_ge(xin_landed[b.par], b.half * 16 + 16)
                chain.link(dve.scalar_tensor_tensor(out=partly, in0=g_out, scalar=inv_norms[:, 0:1],
                                                    in1=x_in[b.par], op0=ALU.mult, op1=ALU.add), meanwhile)
                chain.link(dve.scalar_tensor_tensor(out=x_mid, in0=mixed, scalar=inv_norms[:, 1:2], in1=partly,
                                                    op0=ALU.mult, op1=ALU.add), meanwhile)

            def make_tokens(b, chain, meanwhile=None):
                chain.link(dve.bn_stats(st6b, x_mid), meanwhile)
                stand_alone(dve, passed)
                chain.link(dve.bn_aggr(mvb, st6b), meanwhile)
                chain.link(dve.tensor_scalar(var_b, mvb[:, 1:2], LN_EPS, None, ALU.add), meanwhile)
                rsqrt(chain, var_b, inv_b, h_b, small_i[:, 26:27], meanwhile)
                dve.tensor_scalar(tokens, x_mid, mvb[:, 0:1], inv_b, ALU.subtract, ALU.mult).then_inc(tokens_ready, 1)
                dve.wait_ge(tokens_ready, b.n + 1)
                dve.wait_ge(out_stored[b.par], b.half * 16 + 16)
                chain.link(dve.tensor_tensor(out_sb[b.par], x_mid, tokens, ALU.add), meanwhile)
                assert chain.links == HEAD_LINKS

            def pick(b, use, meanwhile):
                chain = Chain(route_chain, b.n * ROUTE_LINKS)
                dve.wait_ge(turn_filled, use + 1)
                dve.tensor_copy(logits, turned[:, 0:EXPERTS]).then_inc(turn_read, 1)
                dve.wait_ge(turn_read, use + 1)
                stand_alone(dve, passed)
                chain.link(dve.max(top8, logits), meanwhile)
                stand_alone(dve, passed)
                chain.link(dve.max_index(top_i, top8, logits), meanwhile)
                chain.link(dve.tensor_scalar(pick1, iota_e, top_i[:, 0:1], None, ALU.is_equal), meanwhile)
                chain.link(dve.scalar_tensor_tensor(out=rest, in0=pick1, scalar=-3.0e38, in1=logits,
                                                    op0=ALU.mult, op1=ALU.add), meanwhile)
                stand_alone(dve, passed)
                chain.link(dve.max(top8b, rest), meanwhile)
                dve.tensor_tensor(gap, top8[:, 0:1], top8b[:, 0:1], ALU.subtract).then_inc(gap_made, 1)
                chain.link(dve.max_index(top_ib, top8b, rest), meanwhile)
                chain.link(dve.tensor_scalar(pick2, iota_e, top_ib[:, 0:1], None, ALU.is_equal), meanwhile)
                assert chain.links == PICK_LINKS

            def weigh(b):
                chain = Chain(route_chain, b.n * ROUTE_LINKS, PICK_LINKS)
                dve.wait_ge(tanh_made, b.n + 1)
                dve.tensor_scalar(route1, tanh_gap, 0.5, 0.5, ALU.mult, ALU.add)
                chain.link(dve.tensor_scalar(route2, tanh_gap, -0.5, 0.5, ALU.mult, ALU.add))
                chain.link(dve.tensor_scalar(comb_part, pick1, route1, None, ALU.mult))
                dve.scalar_tensor_tensor(out=combine[b.par], in0=pick2, scalar=route2, in1=comb_part,
                                         op0=ALU.mult, op1=ALU.add).then_inc(combine_made, 1)
                assert chain.links == ROUTE_LINKS
                dve.wait_ge(combine_made, b.n + 1)

            def add_expert(n, e, par):
                dve.wait_ge(expert_filled, n + 3)
                dve.wait_ge(expert_added, n + 2)
                dve.scalar_tensor_tensor(out=out_sb[par], in0=expert[e % 2][:, 0:D],
                                         scalar=combine[par][:, e:e + 1], in1=out_sb[par],
                                         op0=ALU.mult, op1=ALU.add).then_inc(expert_added, 1)

            def add_bias(b, use):
                dve.wait_ge(turn_filled, use + 1)
                dve.wait_ge(expert_added, b.n * EXPERTS + 4)
                dve.tensor_tensor(out_sb[b.par], turned[:, 0:D], out_sb[b.par], ALU.add).then_inc(turn_read, 1)
                dve.wait_ge(turn_read, use + 1)

            def onehots(tiles, tile0):
                for j in tiles:
                    if not isinstance(tile0, int) or tile0 + j + LEAD < TILES:
                        tile_onehot(tile0 + j + LEAD, rel_now[:, j:j + 1], (j + LEAD) % OH_RING)
                        yield

            def step(b, nxt, m, e, tiles, uses, tile0, zone0, heads):
                meanwhile = onehots(tiles, tile0)
                if e == 0:
                    pick(b, uses["logits", m], meanwhile)
                if e == 1:
                    weigh(b)
                if e == 3:
                    add_bias(b, uses["bias", m])
                if nxt:
                    if e == 0:
                        split_projection(nxt)
                    if e == 1:
                        soften_q(nxt)
                        stage_sums(nxt)
                    if e == 3:
                        heads[m] = invert_degrees(nxt, uses["q", m + 1], meanwhile)
                    if e == 4:
                        take_parts(nxt, heads[m], meanwhile)
                    if e == 5:
                        join_parts(nxt, heads[m], meanwhile)
                    if e == 6:
                        make_tokens(nxt, heads[m], meanwhile)
                for _ in meanwhile:
                    pass
                if e > 0 or not b.first:
                    add_expert(b.n * EXPERTS + e - 1, (e - 1) % EXPERTS, b.par if e > 0 else 1 - b.par)
                for z in zones_ended(tiles):
                    add_zone(uses, zone0, z, zone0 + z)

            b0, b1 = Block_(0, 0, 0), Block_(1, 0, 1)
            uses0 = Uses(BASE_HEAD0, HEAD0)
            split_projection(b0)
            soften_q(b0)
            stage_sums(b0)
            chain = invert_degrees(b0, uses0["q", 0])
            take_parts(b0, chain)
            join_parts(b0, chain)
            make_tokens(b0, chain)
            heads = {}
            step(b0, b1, 0, 0, range(0), uses0, 0, 0, heads)
            with dve.Fori(0, TURNS) as s:
                uses = Uses(s * USES_TURN + BASE_MAIN, main_order(TURN_STEPS, range(TURN_PERIODS + 1)))
                tile0 = s * TURN_TILES + MAIN_TILE
                zone0 = s * (TURN_TILES // ZONE_TILES) + MAIN_TILE // ZONE_TILES
                copy_rel(tile0, TURN_TILES, s + GROUPS + B2_TURNS + 1)
                for m, e, tiles in TURN_STEPS:
                    b, nxt = (block_at(s * TURN_PERIODS, s * (TURN_PERIODS // 2), n) for n in (m, m + 1))
                    step(b, nxt, m, e, tiles, uses, tile0, zone0, heads)
            first, tile0 = TURNS * TURN_PERIODS, TILES - LAST_TILES
            copy_rel(tile0, LAST_TILES - LEAD, GROUPS + B2_TURNS + TURNS + 1)
            for m, e, tiles in LAST_STEPS:
                b, nxt = (block_at(first, first // 2, n) for n in (m, m + 1))
                step(b, nxt if nxt.n < BLOCKS else None, m, e, tiles, Uses(BASE_LAST, LAST_ORDER), tile0,
                     tile0 // ZONE_TILES, heads)
            add_expert(BLOCKS * EXPERTS - 1, EXPERTS - 1, (BLOCKS - 1) % 2)


def constants():
    import numpy as np

    c = np.zeros((P, C_COLS), np.float32)
    c[np.arange(P), C_EYE + np.arange(P)] = 1.0
    c[:, C_IOTA:C_IOTA + P] = np.arange(P)
    c[:, C_MASK:C_MASK + P] = np.kron(np.eye(P // DH), np.ones((DH, DH)))
    return c


def kernel(x, src, dst, L0_gnn_W, L0_gnn_b, L0_mix_Wqkv, L0_mix_Wout, L0_mix_gamma, L0_ffn_router_w,
           L0_ffn_w1, L0_ffn_b1, L0_ffn_w2, L0_ffn_b2):
    import numpy as np

    import concourse.bacc as bacc
    from concourse.bass_utils import run_bass_kernel_spmd

    x = np.asarray(x)
    src, dst = np.asarray(src), np.asarray(dst)
    spare = TILES * P - EDGES

    def by_tile(edges, filler):
        filled = np.concatenate([edges, np.full(spare, filler, edges.dtype)])
        return np.ascontiguousarray(filled.reshape(TILES, P).T)

    arrays = {
        "x": np.concatenate([x, np.repeat(x[-1:], NODES_PAD - NODES, axis=0)]),
        "src": by_tile(src, 0),
        "dst": by_tile(dst, -1),
        "gnn_w": np.asarray(L0_gnn_W),
        "gnn_b": np.asarray(L0_gnn_b).reshape(1, D),
        "wqkv": np.asarray(L0_mix_Wqkv),
        "wout": np.asarray(L0_mix_Wout),
        "gamma": np.asarray(L0_mix_gamma).reshape(1, D),
        "router_wt": np.ascontiguousarray(np.asarray(L0_ffn_router_w).T),
        "w1": np.asarray(L0_ffn_w1),
        "b1t": np.ascontiguousarray(np.asarray(L0_ffn_b1).reshape(EXPERTS * KC, P).T),
        "w2": np.asarray(L0_ffn_w2),
        "b2": np.asarray(L0_ffn_b2),
        "consts": constants(),
    }
    nc = bacc.Bacc("TRN2", target_bir_lowering=False, num_devices=1)
    args = [nc.dram_tensor(name, a.shape, mybir.dt.from_np(a.dtype), kind="ExternalInput").ap()
            for name, a in arrays.items()]
    out = nc.dram_tensor("out", (NODES, D), F32, kind="ExternalOutput").ap()
    gps_kernel(nc, *args, out)
    result = run_bass_kernel_spmd(nc, [arrays], core_ids=[0])
    return result.results[0]["out"]
```

```python
from contextlib import ExitStack

import concourse.bass as bass
from concourse import mybir

F32 = mybir.dt.float32
F16 = mybir.dt.float16
I32 = mybir.dt.int32
U32 = mybir.dt.uint32
ALU = mybir.AluOpType
ACT = mybir.ActivationFunctionType
AX = mybir.AxisListType

P = 128
NODES = 6250
EDGES = 200000
D = 256
KC = D // P
HEADS = 8
DH = D // HEADS
EXPERTS = 8
LN_EPS = 1e-5
NORM_FLOOR = 1e-12
SCALE = DH ** -0.5
RSQRT_MAGIC = 0x5F3759DF
RSQRT_UNSCALE = -1.0 / 8192

BLOCKS = -(-NODES // P)
LAST_ROWS = NODES - (BLOCKS - 1) * P
NODES_PAD = BLOCKS * P
EDGES_PER_NODE = EDGES // NODES
ZONE_TILES = 16
ZONE_NODES = ZONE_TILES * P // EDGES_PER_NODE
ZONE_BACK = (P - ZONE_NODES) // 2
TILES = BLOCKS * P * EDGES_PER_NODE // P
ZONES = TILES // ZONE_TILES
SUM_COLS = NODES_PAD + P

GROUP = 7
GROUPS = BLOCKS // GROUP
RING = 32
OH_RING = 16
GATHERS_PER_WAIT = 8
LEAD = 8

B1_BLOCKS, B1_TURNS = 12, 4
B1_TILES = 2 * ZONE_TILES
B2_BLOCKS, B2_TURNS = 16, 3
B2_TILES = 2 * ZONE_TILES
KV_BUFS = 4
B2_FIRST = ZONE_TILES
KMAX_TILE = B1_TURNS * B1_TILES
KMAX_PARTS = (range(0, 8), range(8, ZONE_TILES))
HEAD0_TILE = KMAX_TILE + B2_TURNS * B2_TILES
HEAD0_PARTS = (range(B2_FIRST, 20), range(20, 24), range(24, 2 * ZONE_TILES))
MAIN_TILE = HEAD0_TILE + 2 * ZONE_TILES
TURN_TILES = 14 * ZONE_TILES
TURN_PERIODS = 8
TURNS = 5
LAST_PERIODS = BLOCKS - TURNS * TURN_PERIODS
LAST_TILES = TILES - MAIN_TILE - TURNS * TURN_TILES
LAG = 2
ROW_BUFS = 3
HI_ON_VECTOR = GROUPS - 2
IDX_CHUNK = TURN_TILES // 2
assert BLOCKS == GROUP * GROUPS == B1_BLOCKS * B1_TURNS + 1 == B2_BLOCKS * B2_TURNS + 1
assert B1_BLOCKS % 2 == 0 and B2_BLOCKS % KV_BUFS == 0
assert TILES % TURN_TILES == 0 and MAIN_TILE % RING == 0

C_EYE = P
C_IOTA = 384
C_MASK = 512
C_COLS = 640

WEIGHT_LOADS = 10
Q_LINKS, SPLIT_LINKS = 3, 1
HEAD_LINKS = 32
ROUTE_LINKS, PICK_LINKS = 9, 7


def b1_tiles(k):
    return range(k * B1_TILES // B1_BLOCKS, (k + 1) * B1_TILES // B1_BLOCKS)


def b2_tiles(k):
    extra = 8
    count = [B2_FIRST] + [B2_FIRST + extra + (B2_TILES - extra) * n // B2_BLOCKS for n in range(1, B2_BLOCKS + 1)]
    return range(count[k], count[k + 1])


def steps(periods, tiles, rate):
    return plan([min(tiles, int(rate * k)) for k in range(periods * EXPERTS)] + [tiles])


def plan(count):
    return [(*divmod(k + LAG, EXPERTS), range(count[k], count[k + 1])) for k in range(len(count) - 1)]


TURN_STEPS = steps(TURN_PERIODS, TURN_TILES, TURN_TILES / (TURN_PERIODS * EXPERTS))
LAST_RATE = 3.75
LAST_ZONE_RATE = ZONE_TILES // EXPERTS
LAST_ZONE_STEP = (LAST_PERIODS - 3) * EXPERTS - LAG + 1
LAST_STEPS = plan([min(LAST_TILES, int(LAST_RATE * k),
                       LAST_TILES - ZONE_TILES + LAST_ZONE_RATE * max(0, k - LAST_ZONE_STEP))
                   for k in range(LAST_PERIODS * EXPERTS - LAG + 1)])


def zones_ended(tiles):
    return [j // ZONE_TILES for j in tiles if j % ZONE_TILES == ZONE_TILES - 1]


def b1_order():
    order = []
    for k in range(B1_BLOCKS):
        order.append(("xn", k))
        order += [("zone", z) for z in zones_ended(b1_tiles(k))]
    return order


def b2_order():
    return [("zone", z) for k in range(B2_BLOCKS) for z in zones_ended(b2_tiles(k))]


def main_order(plan, heads):
    order = []
    for m, e, tiles in plan:
        if e == 0:
            order.append(("logits", m))
        if e == 1 and m in heads:
            order.append(("q", m + 1))
        if e == 2:
            order.append(("combine", m))
        if e == 3:
            order.append(("bias", m))
        order += [("zone", z) for z in zones_ended(tiles)]
        if e == EXPERTS - 1 and m in heads:
            order.append(("tokens", m + 1))
    return order


def stand_alone(engine, passed):
    engine.sem_inc(passed, 1)


class Uses:

    def __init__(self, base, order):
        self.base, self.at, self.count = base, {name: n for n, name in enumerate(order)}, len(order)

    def __getitem__(self, name):
        return self.base + self.at[name]

    def of_or_before(self, *name):
        return self[name] if name in self.at else self.base - 1


USES_B1 = len(b1_order())
USES_B2 = len(b2_order())
USES_TURN = len(main_order(TURN_STEPS, range(TURN_PERIODS + 1)))
USE_FLAG = 0
BASE_B1 = 1
USE_KMAX_COL = BASE_B1 + B1_TURNS * USES_B1 + 1
USE_KMAX_ROW = USE_KMAX_COL + 1
USE_KMAX_ZONE = USE_KMAX_COL + 2
BASE_B2 = USE_KMAX_COL + 3
BASE_HEAD0 = BASE_B2 + B2_TURNS * USES_B2
HEAD0 = [("q", 0), ("context", 0), ("zone", 1), ("tokens", 0), ("logits", 0), ("q", 1)]
BASE_MAIN = BASE_HEAD0 + len(HEAD0)
assert LAG == 2
BASE_LAST = BASE_MAIN + TURNS * USES_TURN
LAST_ORDER = main_order(LAST_STEPS, range(LAST_PERIODS - 1))


class NodeBlock:

    def __init__(self, number, half, parity):
        self.n, self.half, self.par = number, half, parity
        self.first = isinstance(number, int) and number == 0


def block_at(first, first_half, m):
    return NodeBlock(first + m, first_half + m // 2, m % 2)


def last_blocks(m):
    first = TURNS * TURN_PERIODS
    blocks = [block_at(first, first // 2, m + n) for n in (0, 1, 2)]
    return [b if b.n < BLOCKS else None for b in blocks]


def gps_kernel(nc, x, src, dst, gnn_w, gnn_b, wqkv, wout, gamma, router_wt, w1, b1t, w2, b2, consts, out):
    with ExitStack() as ctx:
        def sb(name, cols, dt=F32, rows=P):
            return ctx.enter_context(nc.sbuf_tensor("sb_" + name, [rows, cols], dt))

        def bank(name):
            return ctx.enter_context(nc.psum_tensor("ps_" + name, [P, 512], F32))

        def sem(name):
            return ctx.enter_context(nc.semaphore(name))

        table = nc.dram_tensor("xn_table", [NODES_PAD, 2 * D], F16, kind="Internal").ap()
        xnt_dram = nc.dram_tensor("xn_transposed", [BLOCKS * P, D], F32, kind="Internal").ap()
        kv_dram = nc.dram_tensor("keys_values", [NODES_PAD, 2 * D], F32, kind="Internal").ap()

        zone_sum = [bank("zone0"), bank("zone1")]
        turned = bank("turned")
        proj = bank("proj")
        hidden = [bank("hidden0"), bank("hidden1")]
        expert = [bank("expert0"), bank("expert1")]
        kv_bank = [proj, hidden[0]]

        cst = sb("consts", C_COLS)
        eye = cst[:, C_EYE:C_EYE + P]
        head_mask = cst[:, C_MASK:C_MASK + P]
        iota_e = cst[:, C_IOTA:C_IOTA + EXPERTS]
        iota16 = sb("iota16", P, F16)
        shifted16 = sb("shifted16", 3 * P, F16)
        deg4 = sb("deg4", 4, F16)
        ones = sb("ones", P)
        w_kv = sb("w_kv", KC * 2 * D)
        w_aq = sb("w_aq", KC * 2 * D)
        w_nb = sb("w_nb", KC * D)
        w_out = sb("w_out", KC * D)
        w_mix = sb("w_mix", KC * D)
        bias_row = sb("bias_row", D)
        gamma_row = sb("gamma_row", D)
        router = sb("router", KC * EXPERTS)
        b1_col = sb("b1_col", EXPERTS * KC)
        b2_row = sb("b2_row", D, rows=EXPERTS)
        ring = sb("ring", RING * (2 * D + 1), F16)
        onehot = sb("onehot", OH_RING * P, F16)
        idx = sb("idx", TILES, I32)
        idx_now = sb("idx_now", TURN_TILES, I32)
        rel = sb("rel", TILES)
        rel_now = sb("rel_now", TURN_TILES)
        far = sb("far", TILES)
        far_now = sb("far_now", ZONE_TILES)
        sums = sb("sums", KC * SUM_COLS)
        zone_deg = sb("zone_deg", ZONES + 3)
        far_deg = sb("far_deg", BLOCKS)
        zone_sb = [sb("zone_sb0", D + 1), sb("zone_sb1", D + 1)]
        zeros = sb("zeros", P + 1)
        small = sb("small", 256)
        small_i = sb("small_i", 32, I32)
        flag = sb("flag", 2, I32, rows=2)
        arena = sb("arena", BLOCKS * D)
        stage = sb("stage", ROW_BUFS * GROUP * D)
        stats = [sb("stats0", 6 * GROUP), sb("stats1", 6 * GROUP)]

        ring3 = ring[:, :].rearrange("p (r c) -> p r c", r=RING)
        onehot3 = onehot[:, :].rearrange("p (r c) -> p r c", r=OH_RING)
        sums3 = sums[:, :].rearrange("p (k c) -> p k c", k=KC)
        w_kv3 = w_kv[:, :].rearrange("p (k c) -> p k c", k=KC)
        w_aq3 = w_aq[:, :].rearrange("p (k c) -> p k c", k=KC)
        w_nb3 = w_nb[:, :].rearrange("p (k c) -> p k c", k=KC)
        w_out3 = w_out[:, :].rearrange("p (k c) -> p k c", k=KC)
        w_mix3 = w_mix[:, :].rearrange("p (k c) -> p k c", k=KC)
        router3 = router[:, :].rearrange("p (k c) -> p k c", k=KC)
        turned3 = turned[:, 0:D].rearrange("p (k c) -> p k c", k=KC)

        xn_all = arena[:, :].rearrange("p (b d) -> p b d", d=D)
        WE = EXPERTS * KC * D
        w1_sb = arena[:, 0:WE].rearrange("p (e k h) -> p e k h", e=EXPERTS, k=KC)
        w2_sb = arena[:, WE:2 * WE].rearrange("p (e k h) -> p e k h", e=EXPERTS, k=KC)

        def buf(tensor, n, first=0):
            return tensor[:, first + n * D:first + (n + 1) * D]

        def halves(ap):
            return ap.rearrange("p (k c) -> p k c", k=KC)

        def by_head(ap):
            return ap.rearrange("p (h c) -> p h c", h=HEADS)

        late = 2 * WE
        xnt = [buf(arena, n, late) for n in (0, 1)]
        x_in = [buf(arena, n, late) for n in (2, 3)]
        out_sb = [buf(arena, n, late) for n in (4, 5)]
        self_part, q_soft, gathered = (buf(arena, n, late) for n in (6, 7, 8))
        g_out, g_square, mixed, partly, x_mid = (buf(arena, n, late) for n in (9, 10, 11, 12, 13))
        tokens = buf(arena, 14, late)
        tokens_t = [buf(arena, n, late) for n in (15, 16)]
        act_h = [buf(stage, n) for n in (0, 1, 12, 13)]
        q_turned = stage[:, 2 * D:3 * D + 1]
        combine_t = stage[0:EXPERTS, 4 * D:4 * D + P]

        rows16 = stage[:, :].bitcast(F16).rearrange("p (b c) -> p b c", c=2 * D)

        def rows16_of(g):
            return rows16[:, g % ROW_BUFS * GROUP:(g % ROW_BUFS + 1) * GROUP, :]

        xn_b = buf(stage, 0)
        xnt_b = [buf(stage, 1), buf(stage, 2)]
        kv_b = [stage[:, 3 * D:5 * D], stage[:, 5 * D:7 * D]]
        k_max = buf(stage, 7)
        k_max_row = buf(stage, 8)
        k_max_wide = buf(stage, 9)
        ctx_sb = buf(stage, 10)
        ctx_t = buf(stage, 11)
        k_b = [buf(arena, n, late) for n in range(4, 4 + KV_BUFS)]
        v_first = late + (5 + KV_BUFS) * D
        v_b = [arena[:, v_first + n * (D + KC):v_first + (n + 1) * (D + KC)].rearrange("p (k c) -> p k c", k=KC)
               for n in range(KV_BUFS)]

        mean_var = small[:, 42:56].rearrange("p (b c) -> p b c", c=2)
        var_eps = small[:, 56:63]
        half_v = small[:, 63:70]
        rstd7 = [small[:, n * GROUP:(n + 1) * GROUP] for n in (0, 1, 2)]
        shift7 = [small[:, n * GROUP:(n + 1) * GROUP] for n in (3, 4, 5)]
        far_max = small[:, 84:85]
        k_col = small[:, 85:87]
        ctx_scale = small[:, 87:89]
        q_max = small[:, 89:97]
        q_sum = small[:, 97:105]
        inv_deg = small[:, 109:110]
        st6 = small[:, 110:116]
        mv = small[:, 116:118]
        sq_var = small[:, 118:120]
        inv_norms = small[:, 120:122]
        h2 = small[:, 122:124]
        st6b = small[:, 124:130]
        mvb = small[:, 130:132]
        var_b = small[:, 132:133]
        inv_b = small[:, 133:134]
        h_b = small[:, 134:135]
        logits = small[:, 136:144]
        top8 = small[:, 144:152]
        pick1 = small[:, 152:160]
        rest = small[:, 160:168]
        top8b = small[:, 168:176]
        pick2 = small[:, 176:184]
        gap = small[:, 184:185]
        tanh_gap = small[:, 185:186]
        route1 = small[:, 186:187]
        route2 = small[:, 187:188]
        combine = [small[:, 192:200], small[:, 200:208]]
        comb_part = small[:, 208:216]
        tile_i = small_i[:, 0:7]
        top_i = small_i[:, 8:16].bitcast(U32)
        top_ib = small_i[:, 16:24].bitcast(U32)

        const_landed, dst_landed, idx_landed = sem("const_landed"), sem("dst_landed"), sem("idx_landed")
        x_landed = [sem(f"x_landed{g}") for g in range(GROUPS)]
        weights_landed = sem("weights_landed")
        experts_landed = sem("experts_landed")
        passed = sem("passed")
        cleared, base_made, sums_cleared = sem("cleared"), sem("base_made"), sem("sums_cleared")
        stats_made = sem("stats_made")
        stat_chain, rstd_made = sem("stat_chain"), sem("rstd_made")
        xn_made, hi_made, lo_made = sem("xn_made"), sem("hi_made"), sem("lo_made")
        rows_stored = [sem(f"rows_stored{n}") for n in range(ROW_BUFS)]
        far_chain, far_reduced, flag_made = sem("far_chain"), sem("far_reduced"), sem("flag_made")
        idx_copied = sem("idx_copied")
        landed = [sem(f"gather_landed{r}") for r in range(RING)]
        tiles_used = sem("tiles_used")
        onehot_made = sem("onehot_made")
        rel_copied = sem("rel_copied")
        zone_copied = sem("zone_copied")
        zone_added = sem("zone_added")
        turn_filled, turn_read = sem("turn_filled"), sem("turn_read")
        pre_idx, pre_landed = sem("pre_idx"), sem("pre_landed")
        pre_chain, pre_onehots, pre_summed = sem("pre_chain"), sem("pre_onehots"), sem("pre_summed")
        pre_copied, pre_turned, pre_added = sem("pre_copied"), sem("pre_turned"), sem("pre_added")
        xn_copied = sem("xn_copied")
        kv_filled = sem("kv_filled")
        kv_copied = sem("kv_copied")
        xnt_stored = [sem("xnt_stored0"), sem("xnt_stored1")]
        kv_stored = [sem("kv_stored0"), sem("kv_stored1")]
        k_maxed = sem("k_maxed")
        k_chain = sem("k_chain")
        k_landed = [sem(f"k_landed{n}") for n in range(KV_BUFS)]
        k_shifted, k_exped, context_summed = sem("k_shifted"), sem("k_exped"), sem("context_summed")
        mix_filled, mix_ready = sem("mix_filled"), sem("mix_ready")
        xnt_landed = [sem("xnt_landed0"), sem("xnt_landed1")]
        xin_landed = [sem("xin_landed0"), sem("xin_landed1")]
        proj_filled, proj_read = sem("proj_filled"), sem("proj_read")
        q_chain, q_exped, q_ready = sem("q_chain"), sem("q_exped"), sem("q_ready")
        sums_staged = sem("sums_staged")
        head_chain = sem("head_chain")
        tokens_ready = sem("tokens_ready")
        route_chain, gap_made, tanh_made, combine_made = (
            sem("route_chain"), sem("gap_made"), sem("tanh_made"), sem("combine_made"))
        hidden_filled = sem("hidden_filled")
        hidden_act = sem("hidden_act")
        expert_filled = sem("expert_filled")
        expert_added = sem("expert_added")
        out_stored = [sem("out_stored0"), sem("out_stored1")]

        block = ctx.enter_context(nc.Block())

        def kv_uses(i, k):
            return i * (B1_BLOCKS // 2) + k // 2

        @block.sync
        def _(sp):
            for s in out_stored + kv_stored + xnt_stored:
                sp.sem_inc(s, 16)
            x_rows = x.rearrange("(b p) d -> p b d", p=P)
            for g in range(GROUPS):
                sp.dma_start(xn_all[:, g * GROUP:(g + 1) * GROUP, :],
                             x_rows[:, g * GROUP:(g + 1) * GROUP, :]).then_inc(x_landed[g], 16)
                if g == 1:
                    sp.dma_start(far[:, :].bitcast(I32), dst).then_inc(dst_landed, 16)
            sp.dma_start(cst[:, :], consts).then_inc(const_landed, 16)
            loads = [
                (w_kv3, wqkv.rearrange("(k p) c -> p k c", p=P)[:, :, D:3 * D]),
                (w_aq3[:, :, 0:D], gnn_w[0:D].rearrange("(k p) c -> p k c", p=P)),
                (w_aq3[:, :, D:2 * D], wqkv.rearrange("(k p) c -> p k c", p=P)[:, :, 0:D]),
                (w_nb3, gnn_w[D:2 * D].rearrange("(k p) c -> p k c", p=P)),
                (w_out3, wout.rearrange("(k p) c -> p k c", p=P)),
                (bias_row[:, :], gnn_b.to_broadcast([P, D])),
                (gamma_row[:, :], gamma.to_broadcast([P, D])),
                (router3, router_wt.rearrange("(k p) c -> p k c", p=P)),
                (b1_col[:, :], b1t),
                (b2_row[:, :], b2),
            ]
            assert len(loads) == WEIGHT_LOADS == 2 * (GROUPS - 2)
            table_rows = table.rearrange("(b p) c -> p b c", p=P)
            for g in range(GROUPS):
                sp.wait_ge(lo_made, g + 1)
                sp.dma_start(table_rows[:, g * GROUP:(g + 1) * GROUP, :],
                             rows16_of(g)).then_inc(rows_stored[g % ROW_BUFS], 16)
                if g == 0:
                    sp.dma_start(idx[:, :], src).then_inc(idx_landed, 16)
                elif g < GROUPS - 1:
                    for to, of in loads[2 * (g - 1):2 * g]:
                        sp.dma_start(to, of).then_inc(weights_landed, 16)
            def store_block(b, k, use):
                sp.wait_ge(turn_read, use + 1)
                sp.dma_start(xnt_dram[bass.ds(b * P, P), :], xnt_b[k % 2]).then_inc(xnt_stored[k % 2], 16)
                sp.wait_ge(kv_copied, b + 3)
                sp.dma_start(kv_dram[bass.ds(b * P, P), :], kv_b[k % 2]).then_inc(kv_stored[k % 2], 16)

            def store_turn(i):
                uses = Uses(i * USES_B1 + BASE_B1, b1_order())
                for k in range(B1_BLOCKS):
                    store_block(i * B1_BLOCKS + k, k, uses["xn", k])

            turns_w1, turns_w2 = (-(-n * EXPERTS * KC // B1_BLOCKS) for n in (1, 2))
            with sp.Fori(0, turns_w1) as i:
                store_turn(i)
            sp.dma_start(w1_sb, w1.rearrange("e (k p) h -> p e k h", p=P)).then_inc(experts_landed, 16)
            with sp.Fori(turns_w1, turns_w2) as i:
                store_turn(i)
            sp.dma_start(w2_sb, w2.rearrange("e (k p) h -> p e k h", p=P)).then_inc(experts_landed, 16)
            with sp.Fori(turns_w2, B1_TURNS) as i:
                store_turn(i)
            store_block(BLOCKS - 1, 0, BASE_B1 + B1_TURNS * USES_B1)
            for n, uses_n in ((0, BLOCKS // 2 + 1), (1, BLOCKS // 2)):
                sp.wait_ge(kv_stored[n], 16 + 16 * uses_n)
                sp.wait_ge(xnt_stored[n], 16 + 16 * uses_n)

            def load_kv(b, n, rows=P):
                keys = kv_dram[bass.ds(b * P, rows), 0:D]
                values = kv_dram[bass.ds(b * P, rows), D:2 * D].rearrange("p (k c) -> p k c", k=KC)
                sp.dma_start(k_b[n][0:rows], keys).then_inc(k_landed[n], 16)
                sp.dma_start(v_b[n][0:rows, :, 0:P], values).then_inc(k_landed[n], 16)

            def load_block(b):
                sp.dma_start(xnt[b.par], xnt_dram[bass.ds(b.n * P, P), :]).then_inc(xnt_landed[b.par], 16)
                sp.dma_start(x_in[b.par], x[bass.ds(b.n * P, P), :]).then_inc(xin_landed[b.par], 16)

            for b in range(KV_BUFS):
                load_kv(b, b)
            load_block(NodeBlock(0, 0, 0))
            load_block(NodeBlock(1, 0, 1))
            with sp.Fori(0, B2_TURNS - 1) as i:
                for k in range(B2_BLOCKS):
                    sp.wait_ge(context_summed, i * B2_BLOCKS + k + 1)
                    load_kv(i * B2_BLOCKS + k + KV_BUFS, k % KV_BUFS)
            for b in range(BLOCKS - 1 - B2_BLOCKS, BLOCKS - KV_BUFS):
                sp.wait_ge(context_summed, b + 1)
                load_kv(b + KV_BUFS, b % KV_BUFS, LAST_ROWS if b + KV_BUFS == BLOCKS - 1 else P)
            def period(b, rows, load):
                if load:
                    sp.wait_ge(proj_filled, 2 * b.n + 1)
                    stand_alone(sp, passed)
                    sp.wait_ge(tokens_ready, b.n + 1)
                    load_block(NodeBlock(b.n + 2, b.half + 1, b.par))
                sp.wait_ge(expert_added, (b.n + 1) * EXPERTS + 2)
                sp.dma_start(out[bass.ds(b.n * P, rows), :],
                             out_sb[b.par][0:rows]).then_inc(out_stored[b.par], 16)

            with sp.Fori(0, TURNS) as s:
                for m in range(TURN_PERIODS):
                    period(block_at(s * TURN_PERIODS, s * (TURN_PERIODS // 2), m), P, True)
            first = TURNS * TURN_PERIODS
            for m in range(LAST_PERIODS):
                b = block_at(first, first // 2, m)
                period(b, LAST_ROWS if b.n == BLOCKS - 1 else P, b.n + 2 < BLOCKS)
            for n in (0, 1):
                sp.wait_ge(out_stored[n], 16 + 16 * ((BLOCKS + 1 - n) // 2))

        @block.gpsimd
        def _(pool):
            pool.iota(rel[:, :].bitcast(I32), [[ZONE_NODES, ZONES], [0, ZONE_TILES]], base=-ZONE_BACK,
                      channel_multiplier=0).then_inc(base_made, 1)
            pool.memset(sums[:, :], 0.0).then_inc(sums_cleared, 1)
            for g in range(GROUPS):
                pool.wait_ge(hi_made, g + 1)
                rows = rows16_of(g)
                pool.tensor_tensor(rows[:, :, D:2 * D], xn_all[:, g * GROUP:(g + 1) * GROUP, :],
                                   rows[:, :, 0:D], ALU.subtract).then_inc(lo_made, 1)
            pool.wait_ge(idx_landed, 16)
            pool.wait_ge(cleared, 1)
            for n in range(ROW_BUFS):
                pool.wait_ge(rows_stored[n], 16 * ((GROUPS + ROW_BUFS - 1 - n) // ROW_BUFS))

            def gather(tile_idx, place, signal):
                pool.indirect_dma_start(ring3[:, place, 0:2 * D], None, table,
                                        bass.IndirectOffsetOnAxis(tile_idx, 0)).then_inc(signal, 16)

            pool.wait_ge(flag_made, 1)
            some_far = pool.value_load(flag[0:1, 0:1], min_val=0, max_val=P * NODES_PAD)
            with pool.If(some_far > 0):
                with pool.Fori(0, ZONES) as z:
                    pool.wait_ge(pre_summed, z * BLOCKS + 1)
                    pool.tensor_copy(idx_now[:, 0:ZONE_TILES],
                                     idx[:, bass.ds(z * ZONE_TILES, ZONE_TILES)]).then_inc(pre_idx, 1)
                    pool.wait_ge(pre_idx, z + 1)
                    stand_alone(pool, passed)
                    for j in range(ZONE_TILES):
                        gather(idx_now[:, j:j + 1], j, pre_landed)
                pool.wait_ge(pre_summed, ZONES * BLOCKS + 1)
            with pool.Fori(0, TILES // TURN_TILES) as s:
                for j in range(TURN_TILES):
                    if j % IDX_CHUNK == 0:
                        pool.tensor_copy(idx_now[:, j:j + IDX_CHUNK],
                                         idx[:, bass.ds(s * TURN_TILES + j, IDX_CHUNK)]).then_inc(idx_copied, 1)
                        pool.wait_ge(idx_copied, s * (TURN_TILES // IDX_CHUNK) + j // IDX_CHUNK + 1)
                    if j % GATHERS_PER_WAIT == 0:
                        pool.wait_ge(tiles_used, s * TURN_TILES + j + GATHERS_PER_WAIT)
                        stand_alone(pool, passed)
                    gather(idx_now[:, j:j + 1], j % RING, landed[j % RING])

        @block.tensor
        def _(pe):
            pe.sem_inc(tiles_used, RING)
            pe.sem_inc(expert_filled, len(act_h))
            pe.sem_inc(pre_summed, 1)

            def sum_tile(tile0, ring0, zone0, j):
                bank_ = zone_sum[(j // ZONE_TILES) % 2]
                oh = onehot3[:, j % OH_RING, :]
                rows = ring3[:, j % RING, :]
                first, last = j % ZONE_TILES == 0, j % ZONE_TILES == ZONE_TILES - 1
                if first:
                    pe.wait_ge(zone_copied, zone0 + j // ZONE_TILES + 1)
                pe.wait_ge(landed[j % RING], (ring0 + j // RING + 1) * 16)
                pe.wait_ge(onehot_made, tile0 + j + 1)
                pe.matmul(bank_[:, 0:D], oh, rows[:, 0:D], start=first, stop=False, skip_group_check=True)
                pe.matmul(bank_[:, 0:D + 1], oh, rows[:, D:2 * D + 1], start=False, stop=last,
                          skip_group_check=True).then_inc(tiles_used, 1)

            def turn(use, ins, width):
                pe.wait_ge(turn_read, use)
                for k in range(KC):
                    t = pe.transpose(turned[:, k * P:(k + 1) * P], ins[:, k * P:(k + 1) * P], eye)
                return t

            def turn_zone(uses, zone0, z):
                pe.wait_ge(zone_copied, zone0 + z + 3)
                turn(uses["zone", z], zone_sb[z % 2], D).then_inc(turn_filled, 1)

            pe.wait_ge(far_reduced, 1)
            pe.matmul(turned[0:1, 0:1], far_max, ones[:, 0:1], start=True, stop=True).then_inc(turn_filled, 1)

            pe.wait_ge(flag_made, 1)
            some_far = pe.value_load(flag[0:1, 0:1], min_val=0, max_val=P * NODES_PAD)
            with pe.If(some_far > 0):
                with pe.Fori(0, ZONES) as z:
                    pe.wait_ge(pre_landed, (z + 1) * (16 * ZONE_TILES))
                    stand_alone(pe, passed)
                    with pe.Fori(0, BLOCKS) as w:
                        n = z * BLOCKS + w
                        pe.wait_ge(pre_onehots, n + 1)
                        for j in range(ZONE_TILES):
                            oh, rows = onehot3[:, j, :], ring3[:, j, :]
                            pe.matmul(zone_sum[0][:, 0:D], oh, rows[:, 0:D], start=j == 0, stop=False,
                                      skip_group_check=True)
                            mm = pe.matmul(zone_sum[0][:, 0:D + 1], oh, rows[:, D:2 * D + 1], start=False,
                                           stop=j == ZONE_TILES - 1, skip_group_check=True)
                        mm.then_inc(pre_summed, 1)
                        pe.wait_ge(pre_copied, n + 1)
                        pe.wait_ge(pre_added, n + 1)
                        for k in range(KC):
                            t = pe.transpose(turned[:, k * P:(k + 1) * P], zone_sb[0][:, k * P:(k + 1) * P], eye)
                        t.then_inc(pre_turned, 1)
                pe.wait_ge(pre_added, ZONES * BLOCKS + 1)

            pe.wait_ge(weights_landed, 16 * WEIGHT_LOADS)
            def transpose_xn(b, use):
                pe.wait_ge(xn_copied, b + 1)
                turn(use, xn_b, D).then_inc(turn_filled, 1)

            def keys_values(b, k, use):
                pe.wait_ge(turn_read, use + 1)
                pe.wait_ge(kv_copied, b + 1)
                for c in range(KC):
                    mm = pe.matmul(kv_bank[k % 2][:, :], halves(xnt_b[k % 2])[:, c, :], w_kv3[:, c, :],
                                   start=c == 0, stop=c == KC - 1)
                mm.then_inc(kv_filled, 1)

            with pe.Fori(0, B1_TURNS) as i:
                uses = Uses(i * USES_B1 + BASE_B1, b1_order())
                for k in range(B1_BLOCKS):
                    transpose_xn(i * B1_BLOCKS + k, uses["xn", k])
                    for j in b1_tiles(k):
                        sum_tile(i * B1_TILES, i, i * 2, j)
                    keys_values(i * B1_BLOCKS + k, k, uses["xn", k])
                    for z in zones_ended(b1_tiles(k)):
                        turn_zone(uses, i * 2, z)
            transpose_xn(BLOCKS - 1, BASE_B1 + B1_TURNS * USES_B1)

            def sum_part(tile0, tiles):
                for j in tiles:
                    sum_tile(tile0, tile0 // RING, tile0 // ZONE_TILES, j)

            sum_part(KMAX_TILE, KMAX_PARTS[0])
            keys_values(BLOCKS - 1, 0, BASE_B1 + B1_TURNS * USES_B1)
            sum_part(KMAX_TILE, KMAX_PARTS[1])

            pe.wait_ge(k_maxed, BLOCKS + 1)
            turn(USE_KMAX_COL, k_max, D).then_inc(turn_filled, 1)
            pe.wait_ge(k_chain, 3)
            turn(USE_KMAX_ROW, k_max_wide, D).then_inc(turn_filled, 1)
            pe.wait_ge(zone_copied, KMAX_TILE // ZONE_TILES + 3)
            turn(USE_KMAX_ZONE, zone_sb[0], D).then_inc(turn_filled, 1)

            pe.wait_ge(turn_read, USE_KMAX_ROW + 1)
            for c in range(KC):
                pe.matmul(expert[c][:, 0:P + 1], zeros[:, 0:P], zeros[:, :], start=True, stop=False,
                          skip_group_check=True)

            def add_context(b, n, rows=P, stop=False):
                pe.wait_ge(k_exped, b + 1)
                for c in range(KC):
                    mm = pe.matmul(expert[c][:, 0:P + 1], k_b[n][0:rows, c * P:(c + 1) * P],
                                   v_b[n][0:rows, c, :], start=False, stop=stop, skip_group_check=True)
                mm.then_inc(context_summed, 1)

            with pe.Fori(0, B2_TURNS) as i:
                uses = Uses(i * USES_B2 + BASE_B2, b2_order())
                tile0, zone0 = i * B2_TILES + B1_TURNS * B1_TILES, i * 2 + 2 * B1_TURNS
                for k in range(B2_BLOCKS):
                    for j in b2_tiles(k):
                        sum_tile(tile0, i + B1_TURNS, zone0, j)
                    add_context(i * B2_BLOCKS + k, k % KV_BUFS)
                    for z in zones_ended(b2_tiles(k)):
                        turn_zone(uses, zone0, z)
            def project(b):
                pe.wait_ge(xnt_landed[b.par], b.half * 16 + 16)
                if not b.first:
                    pe.wait_ge(proj_read, 2 * b.n)
                for c in range(KC):
                    mm = pe.matmul(proj[:, :], halves(xnt[b.par])[:, c, :], w_aq3[:, c, :],
                                   start=c == 0, stop=c == KC - 1)
                mm.then_inc(proj_filled, 1)

            def turn_q(b, use):
                pe.wait_ge(q_ready, b.n + 1)
                pe.wait_ge(sums_staged, b.n + 1)
                turn(use, q_soft, D)
                for n in range(4):
                    move = (n - 1) * ZONE_NODES - ZONE_BACK
                    mm = pe.matmul(turned[:, D:D + 1], shifted16[:, P - move:2 * P - move], deg4[:, n:n + 1],
                                   start=n == 0, stop=n == 3, skip_group_check=True)
                mm.then_inc(turn_filled, 1)

            def mix(b, q_use):
                pe.wait_ge(turn_read, q_use + 1)
                pe.wait_ge(proj_read, 2 * b.n + 1)
                for c in range(KC):
                    pe.matmul(proj[:, 0:D], halves(gathered)[:, c, :], w_nb3[:, c, :],
                              start=c == 0, stop=c == KC - 1, skip_group_check=True)
                for c in range(KC):
                    mm = pe.matmul(proj[:, D:2 * D], halves(q_turned[:, 0:D])[:, c, :], w_mix3[:, c, :],
                                   start=c == 0, stop=c == KC - 1, skip_group_check=True)
                mm.then_inc(proj_filled, 1)

            def turn_tokens(b, use):
                pe.wait_ge(tokens_ready, b.n + 1)
                turn(use, tokens, D).then_inc(turn_filled, 1)

            def route(b, use):
                pe.wait_ge(turn_read, use)
                for c in range(KC):
                    mm = pe.matmul(turned[:, 0:EXPERTS], halves(tokens_t[b.par])[:, c, :], router3[:, c, :],
                                   start=c == 0, stop=c == KC - 1, skip_group_check=True)
                mm.then_inc(turn_filled, 1)

            def turn_combine(b, use):
                pe.wait_ge(turn_read, use)
                pe.wait_ge(combine_made, b.n + 1)
                pe.transpose(turned[0:EXPERTS, 0:P], combine[b.par], eye).then_inc(turn_filled, 1)

            def add_b2(b, use):
                pe.wait_ge(turn_read, use)
                pe.matmul(turned[:, 0:D], combine_t, b2_row[:, :], start=True, stop=True,
                          skip_group_check=True).then_inc(turn_filled, 1)

            def up(b, e):
                pe.wait_ge(hidden_act, b.n * EXPERTS + e + 1)
                for j in range(KC):
                    for c in range(KC):
                        mm = pe.matmul(hidden[e % 2][:, j * P:(j + 1) * P],
                                       w1_sb[:, e, c, j * P:(j + 1) * P], halves(tokens_t[b.par])[:, c, :],
                                       start=c == 0, stop=c == KC - 1, skip_group_check=True)
                mm.then_inc(hidden_filled, 1)

            def down(n, e):
                pe.wait_ge(hidden_act, n + 3)
                pe.wait_ge(expert_added, n + 1)
                for c in range(KC):
                    mm = pe.matmul(expert[e % 2][:, 0:D], halves(act_h[e % len(act_h)])[:, c, :], w2_sb[:, e, c, :],
                                   start=c == 0, stop=c == KC - 1, skip_group_check=True)
                mm.then_inc(expert_filled, 1)

            def step(b, nxt, after, m, e, tiles, uses, tile0, ring0, zone0):
                for j in tiles:
                    sum_tile(tile0, ring0, zone0, j)
                if e == 0:
                    pe.wait_ge(turn_read, uses["logits", m])
                    route(b, uses["logits", m])
                if e == 2:
                    if nxt:
                        mix(nxt, uses.of_or_before("q", m + 1))
                    turn_combine(b, uses["combine", m])
                if e == 3:
                    add_b2(b, uses["bias", m])
                up(b, e)
                if e >= LAG or not b.first:
                    down(b.n * EXPERTS + e - LAG, (e - LAG) % EXPERTS)
                if e == 1 and nxt:
                    turn_q(nxt, uses["q", m + 1])
                for z in zones_ended(tiles):
                    turn_zone(uses, zone0, z)
                if e == EXPERTS - 1:
                    if after:
                        project(after)
                    if nxt:
                        turn_tokens(nxt, uses["tokens", m + 1])

            b0, b1, b2 = NodeBlock(0, 0, 0), NodeBlock(1, 0, 1), NodeBlock(2, 1, 0)
            uses0 = Uses(BASE_HEAD0, HEAD0)
            project(b0)
            add_context(BLOCKS - 1, 0, LAST_ROWS, True)
            sum_part(HEAD0_TILE, HEAD0_PARTS[0])
            turn_q(b0, uses0["q", 0])
            pe.wait_ge(k_chain, 6)
            turn(uses0["context", 0], ctx_sb, D).then_inc(turn_filled, 1)
            sum_part(HEAD0_TILE, HEAD0_PARTS[1])
            pe.wait_ge(turn_read, uses0["context", 0] + 1)
            pe.wait_ge(proj_read, 1)
            for c in range(KC):
                mm = pe.matmul(proj[:, c * D:(c + 1) * D], halves(ctx_t)[:, c, :], w_out3[:, c, :],
                               start=True, stop=True, skip_group_check=True)
            mm.then_inc(mix_filled, 1)
            pe.wait_ge(mix_ready, 1)
            mix(b0, uses0["q", 0])
            sum_part(HEAD0_TILE, HEAD0_PARTS[2])
            turn_zone(uses0, HEAD0_TILE // ZONE_TILES, 1)
            turn_tokens(b0, uses0["tokens", 0])
            project(b1)
            pe.wait_ge(experts_landed, 32)
            for e in range(LAG):
                step(b0, b1, b2, 0, e, range(0), uses0, 0, 0, 0)
            with pe.Fori(0, TURNS) as s:
                uses = Uses(s * USES_TURN + BASE_MAIN, main_order(TURN_STEPS, range(TURN_PERIODS + 1)))
                for m, e, tiles in TURN_STEPS:
                    b, nxt, after = (block_at(s * TURN_PERIODS, s * (TURN_PERIODS // 2), m + n) for n in (0, 1, 2))
                    step(b, nxt, after, m, e, tiles, uses, s * TURN_TILES + MAIN_TILE,
                         s * (TURN_TILES // RING) + MAIN_TILE // RING,
                         s * (TURN_TILES // ZONE_TILES) + MAIN_TILE // ZONE_TILES)
            tile0 = TILES - LAST_TILES
            for m, e, tiles in LAST_STEPS:
                b, nxt, after = last_blocks(m)
                step(b, nxt, after, m, e, tiles, Uses(BASE_LAST, LAST_ORDER), tile0,
                     tile0 // RING, tile0 // ZONE_TILES)
            for e in range(EXPERTS - LAG, EXPERTS):
                down((BLOCKS - 1) * EXPERTS + e, e)

        @block.scalar
        def _(act):
            act.sem_inc(zone_copied, 2)
            act.sem_inc(hidden_act, 2)
            act.sem_inc(kv_copied, 2)
            for g in range(GROUPS):
                act.wait_ge(rstd_made, g + 1)
                for b in range(GROUP):
                    xb = xn_all[:, g * GROUP + b, :]
                    ins = act.activation(xb, xb, ACT.Identity, bias=shift7[g % 3][:, b:b + 1],
                                         scale=rstd7[g % 3][:, b:b + 1])
                ins.then_inc(xn_made, 1)
                if g >= HI_ON_VECTOR:
                    continue
                act.wait_ge(xn_made, g + 1)
                if g >= ROW_BUFS:
                    act.wait_ge(rows_stored[g % ROW_BUFS], 16 * (g // ROW_BUFS))
                act.activation(rows16_of(g)[:, :, 0:D], xn_all[:, g * GROUP:(g + 1) * GROUP, :],
                               ACT.Copy).then_inc(hi_made, 1)

            act.wait_ge(flag_made, 1)
            some_far = act.value_load(flag[0:1, 0:1], min_val=0, max_val=P * NODES_PAD)
            with act.If(some_far > 0):
                with act.Fori(0, ZONES * BLOCKS) as n:
                    act.wait_ge(pre_summed, n + 2)
                    act.wait_ge(pre_added, n + 1)
                    act.activation(zone_sb[0][:, :], zone_sum[0][:, 0:D + 1], ACT.Copy).then_inc(pre_copied, 1)
                act.wait_ge(pre_added, ZONES * BLOCKS + 1)

            def copy_zone(tile0, zone0, z):
                act.wait_ge(tiles_used, tile0 + (z + 1) * ZONE_TILES + RING)
                act.wait_ge(zone_added, zone0 + z + 1)
                act.activation(zone_sb[z % 2][:, :], zone_sum[z % 2][:, 0:D + 1],
                               ACT.Copy).then_inc(zone_copied, 1)

            for n in range(ROW_BUFS):
                act.wait_ge(rows_stored[n], 16 * ((GROUPS + ROW_BUFS - 1 - n) // ROW_BUFS))
            def copy_xn(b):
                act.activation(xn_b, xn_all[:, bass.ds(b, 1), :].rearrange("p b d -> p (b d)"),
                               ACT.Copy).then_inc(xn_copied, 1)

            def copy_xnt(i, k, use):
                act.wait_ge(turn_filled, use + 1)
                act.wait_ge(xnt_stored[k % 2], kv_uses(i, k) * 16 + 16)
                act.activation(xnt_b[k % 2], turned[:, 0:D], ACT.Copy).then_inc(turn_read, 1)

            def copy_kv(i, k):
                b = i * B1_BLOCKS + k
                act.wait_ge(kv_filled, b + 1)
                act.wait_ge(kv_stored[k % 2], kv_uses(i, k) * 16 + 16)
                act.wait_ge(k_maxed, b + 1)
                act.activation(kv_b[k % 2], kv_bank[k % 2][:, :], ACT.Copy).then_inc(kv_copied, 1)

            copy_xn(0)
            with act.Fori(0, B1_TURNS) as i:
                uses = Uses(i * USES_B1 + BASE_B1, b1_order())
                for k in range(B1_BLOCKS):
                    copy_xnt(i, k, uses["xn", k])
                    copy_xn(i * B1_BLOCKS + k + 1)
                    for z in zones_ended(b1_tiles(k)):
                        copy_zone(i * B1_TILES, i * 2, z)
                    copy_kv(i, k)
            copy_xnt(B1_TURNS, 0, BASE_B1 + B1_TURNS * USES_B1)
            copy_kv(B1_TURNS, 0)
            copy_zone(KMAX_TILE, KMAX_TILE // ZONE_TILES, 0)

            def exp_keys(b, n, rows=P):
                act.wait_ge(k_shifted, b + 1)
                act.activation(k_b[n][0:rows], k_b[n][0:rows], ACT.Exp).then_inc(k_exped, 1)

            with act.Fori(0, B2_TURNS) as i:
                for k in range(B2_BLOCKS):
                    exp_keys(i * B2_BLOCKS + k, k % KV_BUFS)
                    for z in zones_ended(b2_tiles(k)):
                        copy_zone(i * B2_TILES + B1_TURNS * B1_TILES, i * 2 + 2 * B1_TURNS, z)
            exp_keys(BLOCKS - 1, 0, LAST_ROWS)

            def exp_q(b):
                act.wait_ge(proj_read, 2 * b.n + 1)
                act.activation(q_soft, q_soft, ACT.Exp).then_inc(q_exped, 1)

            def copy_q(b, use):
                act.wait_ge(turn_filled, use + 1)
                act.activation(q_turned, turned[:, 0:D + 1], ACT.Copy).then_inc(turn_read, 1)

            def copy_tokens(b, use):
                act.wait_ge(turn_filled, use + 1)
                act.activation(tokens_t[b.par], turned[:, 0:D], ACT.Copy).then_inc(turn_read, 1)

            def gelu(b, e):
                act.wait_ge(hidden_filled, b.n * EXPERTS + e + 1)
                act.wait_ge(expert_filled, b.n * EXPERTS + e + 1)
                for j in range(KC):
                    ins = act.activation(halves(act_h[e % len(act_h)])[:, j, :], hidden[e % 2][:, j * P:(j + 1) * P],
                                         ACT.Gelu, bias=b1_col[:, e * KC + j:e * KC + j + 1])
                ins.then_inc(hidden_act, 1)

            def step(b, nxt, after, m, e, tiles, uses, tile0, zone0):
                for z in zones_ended(tiles):
                    copy_zone(tile0, zone0, z)
                if e == 2:
                    act.wait_ge(turn_filled, uses["combine", m] + 1)
                    act.activation(combine_t, turned[0:EXPERTS, 0:P], ACT.Copy).then_inc(turn_read, 1)
                gelu(b, e)
                if e == 0:
                    act.wait_ge(gap_made, b.n + 1)
                    act.activation(tanh_gap, gap, ACT.Tanh, scale=0.5).then_inc(tanh_made, 1)
                if nxt:
                    if e == 1:
                        copy_q(nxt, uses["q", m + 1])
                    if e == EXPERTS - 1:
                        copy_tokens(nxt, uses["tokens", m + 1])
                if e == EXPERTS - 1 and after:
                    exp_q(after)

            b0, b1, b2 = NodeBlock(0, 0, 0), NodeBlock(1, 0, 1), NodeBlock(2, 1, 0)
            uses0 = Uses(BASE_HEAD0, HEAD0)
            exp_q(b0)
            copy_q(b0, uses0["q", 0])
            copy_zone(HEAD0_TILE, HEAD0_TILE // ZONE_TILES, 1)
            copy_tokens(b0, uses0["tokens", 0])
            exp_q(b1)
            for e in range(LAG):
                step(b0, b1, b2, 0, e, range(0), uses0, 0, 0)
            with act.Fori(0, TURNS) as s:
                uses = Uses(s * USES_TURN + BASE_MAIN, main_order(TURN_STEPS, range(TURN_PERIODS + 1)))
                for m, e, tiles in TURN_STEPS:
                    b, nxt, after = (block_at(s * TURN_PERIODS, s * (TURN_PERIODS // 2), m + n) for n in (0, 1, 2))
                    step(b, nxt, after, m, e, tiles, uses, s * TURN_TILES + MAIN_TILE,
                         s * (TURN_TILES // ZONE_TILES) + MAIN_TILE // ZONE_TILES)
            tile0 = TILES - LAST_TILES
            for m, e, tiles in LAST_STEPS:
                b, nxt, after = last_blocks(m)
                step(b, nxt, after, m, e, tiles, Uses(BASE_LAST, LAST_ORDER), tile0,
                     tile0 // ZONE_TILES)

        @block.vector
        def _(dve):
            dve.sem_inc(zone_added, 2)
            dve.sem_inc(expert_added, 2)
            dve.sem_inc(pre_added, 1)

            class Chain:

                def __init__(self, done, before, links=0):
                    self.done, self.before, self.links = done, before, links

                def link(self, ins, meanwhile=None):
                    self.links += 1
                    ins.then_inc(self.done, 1)
                    if meanwhile:
                        next(meanwhile, None)
                    dve.wait_ge(self.done, self.before + self.links)

            def rsqrt(chain, v, y, h, bits, meanwhile=None):
                chain.link(dve.tensor_scalar(bits, v.bitcast(I32), 1, None, ALU.logical_shift_right), meanwhile)
                chain.link(dve.tensor_scalar(y.bitcast(I32), bits, -1.0, float(RSQRT_MAGIC), ALU.mult, ALU.add),
                           meanwhile)
                for _ in range(3):
                    chain.link(dve.tensor_tensor(h, v, y, ALU.mult), meanwhile)
                    chain.link(dve.scalar_tensor_tensor(out=h, in0=h, scalar=-0.5, in1=y, op0=ALU.mult,
                                                        op1=ALU.mult), meanwhile)
                    chain.link(dve.scalar_tensor_tensor(out=y, in0=h, scalar=1.5, in1=y, op0=ALU.add,
                                                        op1=ALU.mult), meanwhile)

            def rsqrt_scaled(chain, v, z, h, bits, meanwhile=None):
                chain.link(dve.tensor_scalar(bits, v.bitcast(I32), 1, None, ALU.logical_shift_right), meanwhile)
                chain.link(dve.tensor_scalar(z.bitcast(I32), bits, -1.0, float(RSQRT_MAGIC), ALU.mult, ALU.add),
                           meanwhile)
                cols = [slice(n, n + 1) for n in range(v.shape[1])]
                for three in (3.0, 3.0 * 2 ** 2, 3.0 * 16 ** 2):
                    for n in cols:
                        ins = dve.scalar_tensor_tensor(out=h[:, n], in0=z[:, n], scalar=v[:, n], in1=z[:, n],
                                                       op0=ALU.mult, op1=ALU.mult)
                    chain.link(ins, meanwhile)
                    for n in cols:
                        ins = dve.scalar_tensor_tensor(out=z[:, n], in0=h[:, n], scalar=-three, in1=z[:, n],
                                                       op0=ALU.add, op1=ALU.mult)
                    chain.link(ins, meanwhile)

            dve.memset(ones[:, :], 1.0)
            dve.memset(zeros[:, :], 0.0)
            dve.memset(zone_deg[:, :], 0.0)
            dve.memset(far_deg[:, :], 0.0)

            def take_stats(g):
                dve.wait_ge(x_landed[g], 16)
                for b in range(GROUP):
                    ins = dve.bn_stats(stats[g % 2][:, 6 * b:6 * b + 6], xn_all[:, g * GROUP + b, :])
                    if b == GROUP - 1:
                        ins.then_inc(stats_made, 1)
                    yield

            below, outside = (ring[:, :].bitcast(F32)[:, n * TILES:(n + 1) * TILES] for n in (0, 1))

            def place_edges():
                dst_i = far[:, :].bitcast(I32)
                dve.wait_ge(dst_landed, 16)
                dve.wait_ge(base_made, 1)
                dve.tensor_tensor(rel[:, :], dst_i, rel[:, :].bitcast(I32), ALU.subtract).then_inc(far_chain, 1)
                yield
                dve.wait_ge(far_chain, 1)
                dve.tensor_scalar(below, rel[:, :], 0.0, None, ALU.is_lt).then_inc(far_chain, 1)
                yield
                dve.wait_ge(far_chain, 2)
                dve.scalar_tensor_tensor(out=outside, in0=rel[:, :], scalar=float(P - 1), in1=below,
                                         op0=ALU.is_gt, op1=ALU.add).then_inc(far_chain, 1)
                yield
                dve.wait_ge(far_chain, 3)
                dve.scalar_tensor_tensor(out=far[:, :], in0=dst_i, scalar=1.0, in1=outside,
                                         op0=ALU.add, op1=ALU.mult).then_inc(far_chain, 1)
                yield
                dve.wait_ge(far_chain, 4)
                dve.tensor_reduce(far_max, far[:, :], AX.X, ALU.max).then_inc(far_reduced, 1)
                yield

            chain = Chain(stat_chain, 0)
            for _ in take_stats(0):
                pass
            for g in range(GROUPS):
                meanwhile = take_stats(g + 1) if 1 <= g < GROUPS - 1 else iter(())
                dve.wait_ge(stats_made, g + 1)
                if g >= 1:
                    dve.wait_ge(rstd_made, g)
                if g >= 3:
                    dve.wait_ge(xn_made, g - 2)
                for b in range(GROUP):
                    ins = dve.bn_aggr(mean_var[:, b, :], stats[g % 2][:, 6 * b:6 * b + 6])
                chain.link(ins, meanwhile)
                chain.link(dve.tensor_scalar(var_eps, mean_var[:, :, 1], LN_EPS, None, ALU.add), meanwhile)
                rsqrt(chain, var_eps, rstd7[g % 3], half_v, tile_i, meanwhile)
                dve.scalar_tensor_tensor(out=shift7[g % 3], in0=mean_var[:, :, 0], scalar=-1.0, in1=rstd7[g % 3],
                                         op0=ALU.mult, op1=ALU.mult).then_inc(rstd_made, 1)
                for _ in take_stats(1) if g == 0 else meanwhile:
                    pass
            edges = place_edges()
            for g in range(HI_ON_VECTOR, GROUPS):
                dve.wait_ge(xn_made, g + 1)
                dve.wait_ge(rows_stored[g % ROW_BUFS], 16 * (g // ROW_BUFS))
                dve.tensor_copy(rows16_of(g)[:, :, 0:D],
                                xn_all[:, g * GROUP:(g + 1) * GROUP, :]).then_inc(hi_made, 1)
                next(edges)
            for _ in edges:
                pass
            dve.wait_ge(const_landed, 16)
            dve.tensor_copy(shifted16[:, :], cst[:, 0:3 * P])
            dve.tensor_copy(iota16[:, :], cst[:, C_IOTA:C_IOTA + P]).then_inc(far_chain, 1)
            dve.wait_ge(far_reduced, 1)
            dve.memset(ring3[:, :, 2 * D:2 * D + 1], 1.0).then_inc(cleared, 1)
            dve.wait_ge(turn_filled, USE_FLAG + 1)
            dve.tensor_copy(small[0:1, 244:245], turned[0:1, 0:1]).then_inc(turn_read, 1)
            dve.wait_ge(turn_read, USE_FLAG + 1)
            dve.tensor_copy(flag[0:1, 0:1], small[0:1, 244:245]).then_inc(flag_made, 1)
            dve.wait_ge(flag_made, 1)
            dve.wait_ge(sums_cleared, 1)
            dve.wait_ge(far_chain, 5)

            def make_onehot(place, rel_col):
                return dve.tensor_scalar(onehot3[:, place, :], iota16[:, :], rel_col, None, ALU.is_equal)

            some_far = dve.value_load(flag[0:1, 0:1], min_val=0, max_val=P * NODES_PAD)
            with dve.If(some_far > 0):
                with dve.Fori(0, ZONES) as z:
                    dve.tensor_scalar(far_now[:, :], far[:, bass.ds(z * ZONE_TILES, ZONE_TILES)], -1.0, None,
                                      ALU.add).then_inc(pre_chain, 1)
                    with dve.Fori(0, BLOCKS) as w:
                        n = z * BLOCKS + w
                        dve.wait_ge(pre_chain, n + z + 1)
                        dve.wait_ge(pre_summed, n + 1)
                        for j in range(ZONE_TILES):
                            ins = make_onehot(j, far_now[:, j:j + 1])
                        ins.then_inc(pre_onehots, 1)
                        dve.wait_ge(pre_onehots, n + 1)
                        dve.tensor_scalar(far_now[:, :], far_now[:, :], -float(P), None,
                                          ALU.add).then_inc(pre_chain, 1)
                        dve.wait_ge(pre_turned, n + 1)
                        window = sums3[:, :, bass.ds(w * P + ZONE_BACK, P)]
                        dve.tensor_tensor(window, turned3, window, ALU.add)
                        dve.tensor_tensor(far_deg[:, bass.ds(w, 1)], zone_sb[0][:, D:D + 1],
                                          far_deg[:, bass.ds(w, 1)], ALU.add).then_inc(pre_added, 1)
                        dve.wait_ge(pre_added, n + 2)
                    dve.wait_ge(pre_chain, z * (BLOCKS + 1) + BLOCKS + 1)

            def tile_onehot(tile, rel_col, place):
                dve.wait_ge(tiles_used, tile + RING - OH_RING + 1)
                make_onehot(place, rel_col).then_inc(onehot_made, 1)

            def add_zone(uses, zone0, z, zone_expr):
                dve.wait_ge(turn_filled, uses["zone", z] + 1)
                dve.wait_ge(zone_added, zone0 + z + 2)
                window = sums3[:, :, bass.ds(zone_expr * ZONE_NODES, P)]
                dve.tensor_tensor(window, turned3, window, ALU.add).then_inc(turn_read, 1)
                dve.tensor_copy(zone_deg[:, bass.ds(zone_expr + 1, 1)],
                                zone_sb[z % 2][:, D:D + 1]).then_inc(zone_added, 1)

            def copy_rel(tile0, first, tiles, copies):
                dve.wait_ge(onehot_made, tile0 + first + LEAD)
                dve.tensor_copy(rel_now[:, first:first + tiles],
                                rel[:, bass.ds(tile0 + first + LEAD, tiles)]).then_inc(rel_copied, 1)
                dve.wait_ge(rel_copied, copies)

            for t in range(LEAD):
                tile_onehot(t, rel[:, t:t + 1], t)
            for n in range(ROW_BUFS):
                dve.wait_ge(rows_stored[n], 16 * ((GROUPS + ROW_BUFS - 1 - n) // ROW_BUFS))
            dve.memset(k_max, -3.0e38).then_inc(k_maxed, 1)
            def max_keys(b, k):
                dve.wait_ge(kv_copied, b + 3)
                dve.wait_ge(k_maxed, b + 1)
                dve.tensor_tensor(k_max, k_max, kv_b[k % 2][:, 0:D], ALU.max).then_inc(k_maxed, 1)

            with dve.Fori(0, B1_TURNS) as i:
                uses = Uses(i * USES_B1 + BASE_B1, b1_order())
                copy_rel(i * B1_TILES, 0, B1_TILES, i + 1)
                for k in range(B1_BLOCKS):
                    for j in b1_tiles(k):
                        tile_onehot(i * B1_TILES + j + LEAD, rel_now[:, j:j + 1], (j + LEAD) % OH_RING)
                    max_keys(i * B1_BLOCKS + k, k)
                    for z in zones_ended(b1_tiles(k)):
                        add_zone(uses, i * 2, z, i * 2 + z)
            copy_rel(KMAX_TILE, 0, ZONE_TILES, B1_TURNS + 1)

            def make_part(tile0, tiles):
                for j in tiles:
                    tile_onehot(tile0 + j + LEAD, rel_now[:, j:j + 1], (j + LEAD) % OH_RING)

            make_part(KMAX_TILE, KMAX_PARTS[0])
            max_keys(BLOCKS - 1, 0)
            make_part(KMAX_TILE, KMAX_PARTS[1])

            chain = Chain(k_chain, 0)
            dve.wait_ge(xn_copied, BLOCKS)
            for n in range(KV_BUFS):
                ins = dve.memset(v_b[n][:, :, P:P + 1], 1.0)
            chain.link(ins)
            dve.wait_ge(turn_filled, USE_KMAX_COL + 1)
            dve.tensor_reduce(k_col, turned3, AX.X, ALU.max).then_inc(turn_read, 1)
            dve.wait_ge(turn_read, USE_KMAX_COL + 1)
            for c in range(KC):
                chain.link(dve.tensor_scalar(halves(k_max_wide)[:, c, :], ones[:, :], k_col[:, c:c + 1], None,
                                             ALU.mult))
            dve.wait_ge(turn_filled, USE_KMAX_ROW + 1)
            dve.tensor_copy(k_max_row, turned[:, 0:D]).then_inc(turn_read, 1)
            dve.wait_ge(turn_read, USE_KMAX_ROW + 1)
            add_zone({("zone", 0): USE_KMAX_ZONE}, KMAX_TILE // ZONE_TILES, 0, KMAX_TILE // ZONE_TILES)

            def shift_keys(b, uses_before, n, rows=P):
                dve.wait_ge(k_landed[n], uses_before * 32 + 32)
                dve.tensor_tensor(k_b[n][0:rows], k_b[n][0:rows], k_max_row[0:rows],
                                  ALU.subtract).then_inc(k_shifted, 1)

            with dve.Fori(0, B2_TURNS) as i:
                uses = Uses(i * USES_B2 + BASE_B2, b2_order())
                tile0, zone0 = i * B2_TILES + B1_TURNS * B1_TILES, i * 2 + 2 * B1_TURNS
                copy_rel(tile0, B2_FIRST, B2_TILES, i + B1_TURNS + 2)
                for k in range(B2_BLOCKS):
                    shift_keys(i * B2_BLOCKS + k, i * (B2_BLOCKS // KV_BUFS) + k // KV_BUFS, k % KV_BUFS)
                    for j in b2_tiles(k):
                        tile_onehot(tile0 + j + LEAD, rel_now[:, j:j + 1], (j + LEAD) % OH_RING)
                    for z in zones_ended(b2_tiles(k)):
                        add_zone(uses, zone0, z, zone0 + z)
            shift_keys(BLOCKS - 1, (BLOCKS - 1) // KV_BUFS, 0, LAST_ROWS)
            k_links = chain

            def split_projection(b):
                chain = Chain(q_chain, b.n * Q_LINKS)
                dve.wait_ge(proj_filled, 2 * b.n + 1)
                dve.tensor_tensor(self_part, proj[:, 0:D], bias_row[:, :], ALU.add)
                chain.link(dve.tensor_reduce(q_max, by_head(proj[:, D:2 * D]), AX.X, ALU.max))
                dve.tensor_tensor(by_head(q_soft), by_head(proj[:, D:2 * D]),
                                  q_max.unsqueeze(2).to_broadcast([P, HEADS, DH]),
                                  ALU.subtract).then_inc(proj_read, 1)
                assert chain.links == SPLIT_LINKS

            def soften_q(b):
                chain = Chain(q_chain, b.n * Q_LINKS, SPLIT_LINKS)
                dve.wait_ge(q_exped, b.n + 1)
                chain.link(dve.tensor_reduce(q_sum, by_head(q_soft), AX.X, ALU.add))
                chain.link(dve.reciprocal(q_sum, q_sum))
                dve.tensor_tensor(by_head(q_soft), by_head(q_soft),
                                  q_sum.unsqueeze(2).to_broadcast([P, HEADS, DH]), ALU.mult).then_inc(q_ready, 1)

            def stage_sums(b):
                dve.wait_ge(zone_added, ZONES + 2 if isinstance(b.n, int) and b.n == BLOCKS - 1 else b.n * 2 + 5)
                if not b.first:
                    dve.wait_ge(proj_filled, b.n * 2)
                dve.tensor_copy(halves(gathered), sums3[:, :, bass.ds(b.n * P + ZONE_BACK, P)])
                dve.tensor_copy(deg4[:, :], zone_deg[:, bass.ds(b.n * 2, 4)]).then_inc(sums_staged, 1)

            def invert_degrees(b, use, meanwhile=None):
                chain = Chain(head_chain, b.n * HEAD_LINKS)
                dve.wait_ge(turn_read, use + 1)
                chain.link(dve.tensor_tensor(inv_deg, q_turned[:, D:D + 1], far_deg[:, bass.ds(b.n, 1)], ALU.add),
                           meanwhile)
                chain.link(dve.tensor_scalar(inv_deg, inv_deg, 1.0, None, ALU.max), meanwhile)
                chain.link(dve.reciprocal(inv_deg, inv_deg), meanwhile)
                return chain

            def take_parts(b, chain, meanwhile=None):
                dve.wait_ge(proj_filled, 2 * b.n + 2)
                dve.scalar_tensor_tensor(out=g_out, in0=proj[:, 0:D], scalar=inv_deg, in1=self_part,
                                         op0=ALU.mult, op1=ALU.add)
                chain.link(dve.bn_stats(st6, proj[:, D:2 * D]), meanwhile)
                stand_alone(dve, passed)
                chain.link(dve.bn_aggr(mv, st6), meanwhile)
                dve.scalar_tensor_tensor(out=mixed, in0=proj[:, D:2 * D], scalar=mv[:, 0:1], in1=gamma_row[:, :],
                                         op0=ALU.subtract, op1=ALU.mult).then_inc(proj_read, 1)

            def find_norms(b, chain, meanwhile=None):
                chain.link(dve.tensor_scalar(g_out, g_out, 0.0, None, ALU.max), meanwhile)
                chain.link(dve.tensor_tensor_reduce(g_square, g_out, g_out, 1.0, 0.0, ALU.mult, ALU.add,
                                                    sq_var[:, 0:1]), meanwhile)
                chain.link(dve.tensor_scalar(sq_var[:, 1:2], mv[:, 1:2], LN_EPS, None, ALU.add), meanwhile)

                rsqrt_scaled(chain, sq_var, inv_norms, h2, small_i[:, 24:26], meanwhile)
                dve.tensor_scalar(inv_norms[:, 1:2], inv_norms[:, 1:2], RSQRT_UNSCALE, None, ALU.mult)
                chain.link(dve.tensor_scalar(inv_norms[:, 0:1], inv_norms[:, 0:1], RSQRT_UNSCALE, 1.0 / NORM_FLOOR,
                                             ALU.mult, ALU.min), meanwhile)

            def join_parts(b, chain, meanwhile=None):
                dve.wait_ge(xin_landed[b.par], b.half * 16 + 16)
                chain.link(dve.scalar_tensor_tensor(out=partly, in0=g_out, scalar=inv_norms[:, 0:1],
                                                    in1=x_in[b.par], op0=ALU.mult, op1=ALU.add), meanwhile)
                chain.link(dve.scalar_tensor_tensor(out=x_mid, in0=mixed, scalar=inv_norms[:, 1:2], in1=partly,
                                                    op0=ALU.mult, op1=ALU.add), meanwhile)
                chain.link(dve.bn_stats(st6b, x_mid), meanwhile)
                stand_alone(dve, passed)
                chain.link(dve.bn_aggr(mvb, st6b), meanwhile)
                chain.link(dve.tensor_scalar(var_b, mvb[:, 1:2], LN_EPS, None, ALU.add), meanwhile)

            def make_tokens(b, chain, meanwhile=None):
                rsqrt_scaled(chain, var_b, inv_b, h_b, small_i[:, 26:27], meanwhile)
                chain.link(dve.tensor_scalar(inv_b, inv_b, RSQRT_UNSCALE, None, ALU.mult), meanwhile)
                dve.tensor_scalar(tokens, x_mid, mvb[:, 0:1], inv_b, ALU.subtract, ALU.mult).then_inc(tokens_ready, 1)

            def start_output(b, chain):
                dve.wait_ge(tokens_ready, b.n + 1)
                dve.wait_ge(out_stored[b.par], b.half * 16 + 16)
                chain.link(dve.tensor_tensor(out_sb[b.par], x_mid, tokens, ALU.add))
                assert chain.links == HEAD_LINKS

            def pick(b, use, meanwhile):
                chain = Chain(route_chain, b.n * ROUTE_LINKS)
                dve.wait_ge(turn_filled, use + 1)
                dve.tensor_copy(logits, turned[:, 0:EXPERTS]).then_inc(turn_read, 1)
                dve.wait_ge(turn_read, use + 1)
                stand_alone(dve, passed)
                chain.link(dve.max(top8, logits), meanwhile)
                stand_alone(dve, passed)
                chain.link(dve.max_index(top_i, top8, logits), meanwhile)
                chain.link(dve.tensor_scalar(pick1, iota_e, top_i[:, 0:1], None, ALU.is_equal), meanwhile)
                chain.link(dve.scalar_tensor_tensor(out=rest, in0=pick1, scalar=-3.0e38, in1=logits,
                                                    op0=ALU.mult, op1=ALU.add), meanwhile)
                stand_alone(dve, passed)
                chain.link(dve.max(top8b, rest), meanwhile)
                dve.tensor_tensor(gap, top8[:, 0:1], top8b[:, 0:1], ALU.subtract).then_inc(gap_made, 1)
                chain.link(dve.max_index(top_ib, top8b, rest), meanwhile)
                chain.link(dve.tensor_scalar(pick2, iota_e, top_ib[:, 0:1], None, ALU.is_equal), meanwhile)
                assert chain.links == PICK_LINKS

            def weigh(b):
                chain = Chain(route_chain, b.n * ROUTE_LINKS, PICK_LINKS)
                dve.wait_ge(tanh_made, b.n + 1)
                dve.tensor_scalar(route1, tanh_gap, 0.5, 0.5, ALU.mult, ALU.add)
                chain.link(dve.tensor_scalar(route2, tanh_gap, -0.5, 0.5, ALU.mult, ALU.add))
                chain.link(dve.tensor_scalar(comb_part, pick1, route1, None, ALU.mult))
                dve.scalar_tensor_tensor(out=combine[b.par], in0=pick2, scalar=route2, in1=comb_part,
                                         op0=ALU.mult, op1=ALU.add).then_inc(combine_made, 1)
                assert chain.links == ROUTE_LINKS
                dve.wait_ge(combine_made, b.n + 1)

            def add_expert(n, e, par):
                dve.wait_ge(expert_filled, n + len(act_h) + 1)
                dve.wait_ge(expert_added, n + 2)
                dve.scalar_tensor_tensor(out=out_sb[par], in0=expert[e % 2][:, 0:D],
                                         scalar=combine[par][:, e:e + 1], in1=out_sb[par],
                                         op0=ALU.mult, op1=ALU.add).then_inc(expert_added, 1)

            def add_bias(b, use):
                dve.wait_ge(turn_filled, use + 1)
                dve.wait_ge(expert_added, b.n * EXPERTS + 3)
                dve.tensor_tensor(out_sb[b.par], turned[:, 0:D], out_sb[b.par], ALU.add).then_inc(turn_read, 1)
                dve.wait_ge(turn_read, use + 1)

            def onehots(tiles, tile0):
                for j in tiles:
                    if not isinstance(tile0, int) or tile0 + j + LEAD < TILES:
                        tile_onehot(tile0 + j + LEAD, rel_now[:, j:j + 1], (j + LEAD) % OH_RING)
                        yield

            def step(b, nxt, after, m, e, tiles, uses, tile0, zone0, heads):
                meanwhile = onehots(tiles, tile0)
                if e == 0:
                    pick(b, uses["logits", m], meanwhile)
                if e == 1:
                    if nxt:
                        stage_sums(nxt)
                    weigh(b)
                if e == 3:
                    add_bias(b, uses["bias", m])
                if nxt:
                    if e == 0:
                        soften_q(nxt)
                    if e == 2:
                        heads[m] = invert_degrees(nxt, uses.of_or_before("q", m + 1), meanwhile)
                        take_parts(nxt, heads[m], meanwhile)
                    if e == 3:
                        find_norms(nxt, heads[m], meanwhile)
                    if e == 4:
                        join_parts(nxt, heads[m], meanwhile)
                    if e == 5:
                        make_tokens(nxt, heads[m], meanwhile)
                    if e == 6:
                        start_output(nxt, heads[m])
                for _ in meanwhile:
                    pass
                if e >= LAG or not b.first:
                    add_expert(b.n * EXPERTS + e - LAG, (e - LAG) % EXPERTS, b.par if e >= LAG else 1 - b.par)
                if e == EXPERTS - 1 and after:
                    split_projection(after)
                for z in zones_ended(tiles):
                    add_zone(uses, zone0, z, zone0 + z)

            b0, b1, b2 = NodeBlock(0, 0, 0), NodeBlock(1, 0, 1), NodeBlock(2, 1, 0)
            uses0 = Uses(BASE_HEAD0, HEAD0)
            tile0, zone0 = HEAD0_TILE, HEAD0_TILE // ZONE_TILES
            copy_rel(tile0, B2_FIRST, ZONE_TILES, B1_TURNS + B2_TURNS + 2)
            split_projection(b0)
            meanwhile = onehots(HEAD0_PARTS[0], tile0)
            for _ in meanwhile:
                pass
            soften_q(b0)
            stage_sums(b0)
            meanwhile = onehots(HEAD0_PARTS[1], tile0)
            chain = k_links
            dve.wait_ge(context_summed, BLOCKS)
            for c in range(KC):
                ins = dve.reciprocal(ctx_scale[:, c:c + 1], expert[c][:, P:P + 1])
            chain.link(ins, meanwhile)
            chain.link(dve.tensor_scalar(ctx_scale, ctx_scale, SCALE, None, ALU.mult), meanwhile)
            for c in range(KC):
                ins = dve.scalar_tensor_tensor(out=halves(ctx_sb)[:, c, :], in0=expert[c][:, 0:P],
                                               scalar=ctx_scale[:, c:c + 1], in1=head_mask,
                                               op0=ALU.mult, op1=ALU.mult)
            chain.link(ins, meanwhile)
            dve.wait_ge(turn_filled, uses0["context", 0] + 1)
            dve.tensor_copy(ctx_t, turned[:, 0:D]).then_inc(turn_read, 1)
            for _ in meanwhile:
                pass
            dve.wait_ge(mix_filled, 1)
            dve.tensor_copy(w_mix[:, :], proj[:, :]).then_inc(mix_ready, 1)
            dve.wait_ge(mix_ready, 1)
            meanwhile = onehots(HEAD0_PARTS[2], tile0)
            chain = invert_degrees(b0, uses0["q", 0], meanwhile)
            take_parts(b0, chain, meanwhile)
            find_norms(b0, chain, meanwhile)
            join_parts(b0, chain, meanwhile)
            for _ in meanwhile:
                pass
            add_zone(uses0, zone0, 1, zone0 + 1)
            make_tokens(b0, chain)
            start_output(b0, chain)
            split_projection(b1)
            heads = {}
            for e in range(LAG):
                step(b0, b1, b2, 0, e, range(0), uses0, 0, 0, heads)
            with dve.Fori(0, TURNS) as s:
                uses = Uses(s * USES_TURN + BASE_MAIN, main_order(TURN_STEPS, range(TURN_PERIODS + 1)))
                tile0 = s * TURN_TILES + MAIN_TILE
                zone0 = s * (TURN_TILES // ZONE_TILES) + MAIN_TILE // ZONE_TILES
                copy_rel(tile0, 0, TURN_TILES, s + B1_TURNS + B2_TURNS + 3)
                for m, e, tiles in TURN_STEPS:
                    b, nxt, after = (block_at(s * TURN_PERIODS, s * (TURN_PERIODS // 2), m + n) for n in (0, 1, 2))
                    step(b, nxt, after, m, e, tiles, uses, tile0, zone0, heads)
            tile0 = TILES - LAST_TILES
            copy_rel(tile0, 0, LAST_TILES - LEAD, B1_TURNS + B2_TURNS + TURNS + 3)
            for m, e, tiles in LAST_STEPS:
                b, nxt, after = last_blocks(m)
                step(b, nxt, after, m, e, tiles, Uses(BASE_LAST, LAST_ORDER), tile0,
                     tile0 // ZONE_TILES, heads)
            for e in range(EXPERTS - LAG, EXPERTS):
                add_expert((BLOCKS - 1) * EXPERTS + e, e, (BLOCKS - 1) % 2)


def constants():
    import numpy as np

    c = np.zeros((P, C_COLS), np.float32)
    c[np.arange(P), C_EYE + np.arange(P)] = 1.0
    c[:, C_IOTA:C_IOTA + P] = np.arange(P)
    c[:, C_MASK:C_MASK + P] = np.kron(np.eye(P // DH), np.ones((DH, DH)))
    return c


def kernel(x, src, dst, L0_gnn_W, L0_gnn_b, L0_mix_Wqkv, L0_mix_Wout, L0_mix_gamma, L0_ffn_router_w,
           L0_ffn_w1, L0_ffn_b1, L0_ffn_w2, L0_ffn_b2):
    import numpy as np

    import concourse.bacc as bacc
    from concourse.bass_utils import run_bass_kernel_spmd

    x = np.asarray(x)
    src, dst = np.asarray(src), np.asarray(dst)
    spare = TILES * P - EDGES

    def by_tile(edges, filler):
        filled = np.concatenate([edges, np.full(spare, filler, edges.dtype)])
        return np.ascontiguousarray(filled.reshape(TILES, P).T)

    arrays = {
        "x": np.concatenate([x, np.repeat(x[-1:], NODES_PAD - NODES, axis=0)]),
        "src": by_tile(src, 0),
        "dst": by_tile(dst, -1),
        "gnn_w": np.asarray(L0_gnn_W),
        "gnn_b": np.asarray(L0_gnn_b).reshape(1, D),
        "wqkv": np.asarray(L0_mix_Wqkv),
        "wout": np.asarray(L0_mix_Wout),
        "gamma": np.asarray(L0_mix_gamma).reshape(1, D),
        "router_wt": np.ascontiguousarray(np.asarray(L0_ffn_router_w).T),
        "w1": np.asarray(L0_ffn_w1),
        "b1t": np.ascontiguousarray(np.asarray(L0_ffn_b1).reshape(EXPERTS * KC, P).T),
        "w2": np.asarray(L0_ffn_w2),
        "b2": np.asarray(L0_ffn_b2),
        "consts": constants(),
    }
    nc = bacc.Bacc("TRN2", target_bir_lowering=False, num_devices=1)
    args = [nc.dram_tensor(name, a.shape, mybir.dt.from_np(a.dtype), kind="ExternalInput").ap()
            for name, a in arrays.items()]
    out = nc.dram_tensor("out", (NODES, D), F32, kind="ExternalOutput").ap()
    gps_kernel(nc, *args, out)
    result = run_bass_kernel_spmd(nc, [arrays], core_ids=[0])
    return result.results[0]["out"]
```
